# Optimizing a Trainium2 kernel written in Bass

```python
import numpy as np
import jax
import jax.numpy as jnp

def _softmax(x, axis=-1):
    return jax.nn.softmax(x, axis=axis)

def _gelu(x):
    return jax.nn.gelu(x, approximate=True)

def _silu(x):
    return jax.nn.silu(x)

def _sigmoid(x):
    return jax.nn.sigmoid(x)

def _layernorm(x, axis=-1, eps=1e-05):
    m = jnp.mean(x, axis=axis, keepdims=True)
    v = jnp.var(x, axis=axis, keepdims=True)
    return (x - m) / jnp.sqrt(v + eps)

def _scatter_add(tgt, idx, src, axis=0):
    return tgt.at[idx].add(src)

def _segment_sum(src, seg, n):
    return jax.ops.segment_sum(src, seg, n)
kernel_name = 'mk_gnn_preln_d4_gnn_r8_7a2d5b'

def setup_inputs(seed: int=0):
    np.random.seed(seed)
    _w = jnp.asarray

    def _rec_inputs():
        import jax
        import jax.numpy as jnp
        _gk = jax.random.key(seed)
        x = -1.686e-05 + 1 * jax.random.normal(jax.random.fold_in(_gk, 1), (6250, 160), jnp.float32)
        _s = jax.random.randint(jax.random.fold_in(_gk, 2), (100000,), 0, 6250, jnp.int32)
        _d = jax.random.randint(jax.random.fold_in(_gk, 3), (100000,), 0, 6250, jnp.int32)
        _loop = jnp.arange(6250, dtype=jnp.int32)
        src = jnp.concatenate([_s, _d, _loop])
        dst = jnp.concatenate([_d, _s, _loop])
        _o = jnp.argsort(dst, stable=True)
        src = src[_o]
        dst = dst[_o]
        edge_attr_12 = jax.random.uniform(jax.random.fold_in(_gk, 12), (206250, 12), jnp.float32, 0.0, 1)
        edge_attr_16 = jax.random.uniform(jax.random.fold_in(_gk, 13), (206250, 16), jnp.float32, 0.0, 1)
        edge_attr_4 = 0.000486536 + 0.999406 * jax.random.normal(jax.random.fold_in(_gk, 14), (206250, 4), jnp.float32)
        node_vec1 = jax.random.uniform(jax.random.fold_in(_gk, 16), (6250, 1), jnp.float32, 0.0, 0.999994)
        return (x, src, dst, edge_attr_12, edge_attr_16, edge_attr_4, node_vec1)
    x, src, dst, edge_attr_12, edge_attr_16, edge_attr_4, node_vec1 = _rec_inputs()

    def _L0_gnn_setup():
        import jax, jax.numpy as jnp
        import numpy as np
        N = 6250
        E = 50000
        MUL0 = 64
        MUL1 = 32
        NEF = 12
        RN = 100
        NUM_NEIGHBORS = 8.0
        WNUM = MUL0 + MUL0 + MUL1 + MUL1

        def _split(x):
            return (x[:, :MUL0], x[:, MUL0:].reshape(-1, MUL1, 3))

        def _fctp_scalar_attr(x0, x1, z, Ws, Wv):
            s = x0 @ Ws * z / np.sqrt(Ws.shape[0])
            v = jnp.einsum('nuc,uw->nwc', x1, Wv) * z[:, :, None] / np.sqrt(Wv.shape[0])
            return (s, v)
        key = jax.random.key(seed)
        ks = jax.random.split(key, 16)
        return {'node_input': jax.random.normal(ks[0], (N, MUL0 + 3 * MUL1), jnp.float32), 'node_attr': jax.random.uniform(ks[1], (N, 1), dtype=jnp.float32), 'edge_src': jax.random.randint(ks[2], (E,), 0, N), 'edge_dst': jax.random.randint(ks[3], (E,), 0, N), 'edge_attr': jax.random.normal(ks[4], (E, 4), jnp.float32), 'edge_features': jax.random.uniform(ks[5], (E, NEF), dtype=jnp.float32), 'W_sc0': jax.random.normal(ks[6], (MUL0, MUL0), jnp.float32), 'W_sc1': jax.random.normal(ks[7], (MUL1, MUL1), jnp.float32), 'W_l1_0': jax.random.normal(ks[8], (MUL0, MUL0), jnp.float32), 'W_l1_1': jax.random.normal(ks[9], (MUL1, MUL1), jnp.float32), 'W_fc1': jax.random.normal(ks[10], (NEF, RN), jnp.float32), 'W_fc2': jax.random.normal(ks[11], (RN, WNUM), jnp.float32), 'W_l2_0': jax.random.normal(ks[12], (MUL0 + MUL1, MUL0), jnp.float32), 'W_l2_1': jax.random.normal(ks[13], (MUL0 + MUL1, MUL1), jnp.float32)}
    _L0_gnn_all = _L0_gnn_setup()
    _L0_gnn_in = {k: v for k, v in _L0_gnn_all.items() if k in ('W_sc0', 'W_sc1', 'W_l1_0', 'W_l1_1', 'W_fc1', 'W_fc2', 'W_l2_0', 'W_l2_1')}
    del _L0_gnn_all

    def _L1_gnn_setup():
        import jax, jax.numpy as jnp
        import numpy as np
        N, E = (2500, 40000)
        CS, CV = (64, 32)
        AS_, AV, H = (16, 8, 4)
        NB = 16
        SQRT3 = 1.7320508075688772
        SQRT2 = 1.4142135623730951
        EPS = 1e-05

        def _cg_tp(s, v, y0, y1, w_ss, w_sv, w_vs, w_vv0, w_vv1):
            out_s = jnp.concatenate([w_ss * s * y0[:, None], w_vv0 * (jnp.einsum('eci,ei->ec', v, y1) / SQRT3)], axis=-1)
            out_v = jnp.concatenate([(w_sv * s)[:, :, None] * y1[:, None, :], (w_vs * jnp.ones_like(v[..., 0]))[..., None] * v * y0[:, None, None], (w_vv1 * jnp.ones_like(v[..., 0]))[..., None] * (jnp.cross(v, y1[:, None, :]) / SQRT2)], axis=1)
            return (out_s, out_v)

        def _equiv_layernorm(s, v, gamma_s, beta_s, gamma_v):
            mu = jnp.mean(s, axis=-1, keepdims=True)
            var = jnp.var(s, axis=-1, keepdims=True)
            s_n = (s - mu) * jax.lax.rsqrt(var + EPS) * gamma_s + beta_s
            rms = jnp.sqrt(jnp.mean(jnp.sum(v * v, axis=-1), axis=-1, keepdims=True) + EPS)
            v_n = v / rms[..., None] * gamma_v[None, :, None]
            return (s_n, v_n)
        key = jax.random.key(seed)
        ks = jax.random.split(key, 26)

        def rn(k, shape, fan):
            return jax.random.normal(k, shape, jnp.float32) / np.sqrt(fan)
        D1S, D1V = (CS + CV, CS + 2 * CV)
        WN = 2 * CS + 3 * CV
        inp = {'node': jax.random.normal(ks[0], (N, CS + 3 * CV), jnp.float32), 'edge_index': jax.random.randint(ks[1], (2, E), 0, N, jnp.int64 if jax.config.jax_enable_x64 else jnp.int32), 'rbf': jax.random.uniform(ks[2], (E, NB), jnp.float32), 'rsh': jax.random.normal(ks[3], (E, 4), jnp.float32), 'gamma_s': jnp.ones((CS,), jnp.float32), 'beta_s': jnp.zeros((CS,), jnp.float32), 'gamma_v': jnp.ones((CV,), jnp.float32), 'Ws_src': rn(ks[4], (CS, CS), CS), 'Wv_src': rn(ks[5], (CV, CV), CV), 'Ws_dst': rn(ks[6], (CS, CS), CS), 'Wv_dst': rn(ks[7], (CV, CV), CV), 'W_rbf': rn(ks[8], (NB, WN), NB), 'W_alpha': rn(ks[9], (D1S, H * AS_), D1S), 'alpha_dot': rn(ks[10], (1, H, AS_), AS_), 'Ws_val': rn(ks[11], (D1S, CS), D1S), 'Wv_val': rn(ks[12], (D1V, CV), D1V), 'Wg': rn(ks[13], (CS, CV), CS), 'w2_ss': rn(ks[14], (CS,), 1), 'w2_sv': rn(ks[15], (CS,), 1), 'w2_vs': rn(ks[16], (CV,), 1), 'w2_vv0': rn(ks[17], (CV,), 1), 'w2_vv1': rn(ks[18], (CV,), 1), 'Ws_vlin': rn(ks[19], (D1S, H * AS_), D1S), 'Wv_vlin': rn(ks[20], (D1V, H * AV), D1V), 'Wps': rn(ks[21], (H * AS_, CS), H * AS_), 'Wpv': rn(ks[22], (H * AV, CV), H * AV)}
        return inp
    _L1_gnn_all = _L1_gnn_setup()
    _L1_gnn_in = {k: v for k, v in _L1_gnn_all.items() if k in ('gamma_s', 'beta_s', 'gamma_v', 'Ws_src', 'Wv_src', 'Ws_dst', 'Wv_dst', 'W_rbf', 'W_alpha', 'alpha_dot', 'Ws_val', 'Wv_val', 'Wg', 'w2_ss', 'w2_sv', 'w2_vs', 'w2_vv0', 'w2_vv1', 'Ws_vlin', 'Wv_vlin', 'Wps', 'Wpv')}
    del _L1_gnn_all

    def _L2_gnn_setup():
        import jax, jax.numpy as jnp
        import numpy as np
        N, E = (6250, 100000)
        MUL0, MUL1 = (64, 32)
        D = MUL0 + 3 * MUL1
        INV3 = float(1.0 / np.sqrt(3.0))
        INV6 = float(1.0 / np.sqrt(6.0))
        C0 = float(1.0 / np.sqrt(MUL0 + MUL1))
        C1 = float(np.sqrt(3.0 / (MUL0 + 2 * MUL1)))
        LIN_S = float(1.0 / np.sqrt(MUL0))
        LIN_V = float(1.0 / np.sqrt(MUL1))
        key = jax.random.key(seed)
        ks = jax.random.split(key, 10)
        x = jax.random.normal(ks[0], (N, D), dtype=jnp.float32)
        sh = jax.random.normal(ks[1], (E, 4), dtype=jnp.float32)
        edge_index = jax.random.randint(ks[2], (2, E), 0, N, dtype=jnp.int64)
        W1 = jax.random.normal(ks[3], (MUL0, MUL0), dtype=jnp.float32)
        W2 = jax.random.normal(ks[4], (MUL1, MUL0), dtype=jnp.float32)
        W3 = jax.random.normal(ks[5], (MUL0, MUL1), dtype=jnp.float32)
        W4 = jax.random.normal(ks[6], (MUL1, MUL1), dtype=jnp.float32)
        W5 = jax.random.normal(ks[7], (MUL1, MUL1), dtype=jnp.float32)
        Ws = jax.random.normal(ks[8], (MUL0, MUL0), dtype=jnp.float32)
        Wv = jax.random.normal(ks[9], (MUL1, MUL1), dtype=jnp.float32)
        return {'x': x, 'sh': sh, 'W1': W1, 'W2': W2, 'W3': W3, 'W4': W4, 'W5': W5, 'Ws': Ws, 'Wv': Wv, 'edge_index': edge_index}
    _L2_gnn_all = _L2_gnn_setup()
    _L2_gnn_in = {k: v for k, v in _L2_gnn_all.items() if k in ('W1', 'W2', 'W3', 'W4', 'W5', 'Ws', 'Wv')}
    del _L2_gnn_all

    def _L3_gnn_setup():
        import jax, jax.numpy as jnp
        import numpy as np
        N = 2500
        E = 80000
        INV_SQRT3 = 0.5773502691896258
        INV8 = 0.125
        INV_SQRT32 = 0.17677669529663687
        INV64 = 0.015625
        INV32 = 0.03125
        INV_SQRT2048 = 0.022097086912079608
        key = jax.random.key(seed)
        ks = jax.random.split(key, 16)
        f32 = jnp.float32
        return {'node_features': jax.random.normal(ks[0], (N, 160), f32), 'edge_index': jax.random.randint(ks[1], (2, E), 0, N), 'edge_attr_tensor': jax.random.normal(ks[2], (E, 4), f32), 'node_attr_scalar_raw': jax.random.normal(ks[3], (N, 1), f32), 'Wm_ss': jax.random.normal(ks[4], (64, 64), f32), 'Wm_vv': jax.random.normal(ks[5], (32, 64), f32), 'Wm_sv': jax.random.normal(ks[6], (64, 32), f32), 'Wm_vs': jax.random.normal(ks[7], (32, 32), f32), 'Lm_s': jax.random.normal(ks[8], (64, 64), f32), 'Lm_v': jax.random.normal(ks[9], (32, 32), f32), 'Wu_ss': jax.random.normal(ks[10], (64, 64, 64), f32), 'Wu_vv': jax.random.normal(ks[11], (32, 32, 64), f32), 'Wu_sv': jax.random.normal(ks[12], (64, 32, 32), f32), 'Wu_vs': jax.random.normal(ks[13], (32, 64, 32), f32), 'Lu_s': jax.random.normal(ks[14], (64, 64), f32), 'Lu_v': jax.random.normal(ks[15], (32, 32), f32)}
    _L3_gnn_all = _L3_gnn_setup()
    _L3_gnn_in = {k: v for k, v in _L3_gnn_all.items() if k in ('Wm_ss', 'Wm_vv', 'Wm_sv', 'Wm_vs', 'Lm_s', 'Lm_v', 'Wu_ss', 'Wu_vv', 'Wu_sv', 'Wu_vs', 'Lu_s', 'Lu_v')}
    del _L3_gnn_all
    return {'x': x, 'src': src, 'dst': dst, 'edge_attr_12': edge_attr_12, 'edge_attr_16': edge_attr_16, 'edge_attr_4': edge_attr_4, 'node_vec1': node_vec1, 'L0_gnn_W_sc0': _L0_gnn_in['W_sc0'], 'L0_gnn_W_sc1': _L0_gnn_in['W_sc1'], 'L0_gnn_W_l1_0': _L0_gnn_in['W_l1_0'], 'L0_gnn_W_l1_1': _L0_gnn_in['W_l1_1'], 'L0_gnn_W_fc1': _L0_gnn_in['W_fc1'], 'L0_gnn_W_fc2': _L0_gnn_in['W_fc2'], 'L0_gnn_W_l2_0': _L0_gnn_in['W_l2_0'], 'L0_gnn_W_l2_1': _L0_gnn_in['W_l2_1'], 'L1_gnn_gamma_s': _L1_gnn_in['gamma_s'], 'L1_gnn_beta_s': _L1_gnn_in['beta_s'], 'L1_gnn_gamma_v': _L1_gnn_in['gamma_v'], 'L1_gnn_Ws_src': _L1_gnn_in['Ws_src'], 'L1_gnn_Wv_src': _L1_gnn_in['Wv_src'], 'L1_gnn_Ws_dst': _L1_gnn_in['Ws_dst'], 'L1_gnn_Wv_dst': _L1_gnn_in['Wv_dst'], 'L1_gnn_W_rbf': _L1_gnn_in['W_rbf'], 'L1_gnn_W_alpha': _L1_gnn_in['W_alpha'], 'L1_gnn_alpha_dot': _L1_gnn_in['alpha_dot'], 'L1_gnn_Ws_val': _L1_gnn_in['Ws_val'], 'L1_gnn_Wv_val': _L1_gnn_in['Wv_val'], 'L1_gnn_Wg': _L1_gnn_in['Wg'], 'L1_gnn_w2_ss': _L1_gnn_in['w2_ss'], 'L1_gnn_w2_sv': _L1_gnn_in['w2_sv'], 'L1_gnn_w2_vs': _L1_gnn_in['w2_vs'], 'L1_gnn_w2_vv0': _L1_gnn_in['w2_vv0'], 'L1_gnn_w2_vv1': _L1_gnn_in['w2_vv1'], 'L1_gnn_Ws_vlin': _L1_gnn_in['Ws_vlin'], 'L1_gnn_Wv_vlin': _L1_gnn_in['Wv_vlin'], 'L1_gnn_Wps': _L1_gnn_in['Wps'], 'L1_gnn_Wpv': _L1_gnn_in['Wpv'], 'L2_gnn_W1': _L2_gnn_in['W1'], 'L2_gnn_W2': _L2_gnn_in['W2'], 'L2_gnn_W3': _L2_gnn_in['W3'], 'L2_gnn_W4': _L2_gnn_in['W4'], 'L2_gnn_W5': _L2_gnn_in['W5'], 'L2_gnn_Ws': _L2_gnn_in['Ws'], 'L2_gnn_Wv': _L2_gnn_in['Wv'], 'L3_gnn_Wm_ss': _L3_gnn_in['Wm_ss'], 'L3_gnn_Wm_vv': _L3_gnn_in['Wm_vv'], 'L3_gnn_Wm_sv': _L3_gnn_in['Wm_sv'], 'L3_gnn_Wm_vs': _L3_gnn_in['Wm_vs'], 'L3_gnn_Lm_s': _L3_gnn_in['Lm_s'], 'L3_gnn_Lm_v': _L3_gnn_in['Lm_v'], 'L3_gnn_Wu_ss': _L3_gnn_in['Wu_ss'], 'L3_gnn_Wu_vv': _L3_gnn_in['Wu_vv'], 'L3_gnn_Wu_sv': _L3_gnn_in['Wu_sv'], 'L3_gnn_Wu_vs': _L3_gnn_in['Wu_vs'], 'L3_gnn_Lu_s': _L3_gnn_in['Lu_s'], 'L3_gnn_Lu_v': _L3_gnn_in['Lu_v']}

def reference(x, src, dst, edge_attr_12, edge_attr_16, edge_attr_4, node_vec1, L0_gnn_W_sc0, L0_gnn_W_sc1, L0_gnn_W_l1_0, L0_gnn_W_l1_1, L0_gnn_W_fc1, L0_gnn_W_fc2, L0_gnn_W_l2_0, L0_gnn_W_l2_1, L1_gnn_gamma_s, L1_gnn_beta_s, L1_gnn_gamma_v, L1_gnn_Ws_src, L1_gnn_Wv_src, L1_gnn_Ws_dst, L1_gnn_Wv_dst, L1_gnn_W_rbf, L1_gnn_W_alpha, L1_gnn_alpha_dot, L1_gnn_Ws_val, L1_gnn_Wv_val, L1_gnn_Wg, L1_gnn_w2_ss, L1_gnn_w2_sv, L1_gnn_w2_vs, L1_gnn_w2_vv0, L1_gnn_w2_vv1, L1_gnn_Ws_vlin, L1_gnn_Wv_vlin, L1_gnn_Wps, L1_gnn_Wpv, L2_gnn_W1, L2_gnn_W2, L2_gnn_W3, L2_gnn_W4, L2_gnn_W5, L2_gnn_Ws, L2_gnn_Wv, L3_gnn_Wm_ss, L3_gnn_Wm_vv, L3_gnn_Wm_sv, L3_gnn_Wm_vs, L3_gnn_Lm_s, L3_gnn_Lm_v, L3_gnn_Wu_ss, L3_gnn_Wu_vv, L3_gnn_Wu_sv, L3_gnn_Wu_vs, L3_gnn_Lu_s, L3_gnn_Lu_v):
    import jax
    import jax.numpy as jnp

    def _L0_gnn_ref(node_input, node_attr, edge_src, edge_dst, edge_attr, edge_features, W_sc0, W_sc1, W_l1_0, W_l1_1, W_fc1, W_fc2, W_l2_0, W_l2_1):
        import jax, jax.numpy as jnp
        import numpy as np
        N = 6250
        E = 50000
        MUL0 = 64
        MUL1 = 32
        NEF = 12
        RN = 100
        NUM_NEIGHBORS = 8.0
        WNUM = MUL0 + MUL0 + MUL1 + MUL1

        def _split(x):
            return (x[:, :MUL0], x[:, MUL0:].reshape(-1, MUL1, 3))

        def _fctp_scalar_attr(x0, x1, z, Ws, Wv):
            s = x0 @ Ws * z / np.sqrt(Ws.shape[0])
            v = jnp.einsum('nuc,uw->nwc', x1, Wv) * z[:, :, None] / np.sqrt(Wv.shape[0])
            return (s, v)
        x0, x1 = _split(node_input)
        z = node_attr
        s0, s1 = _fctp_scalar_attr(x0, x1, z, W_sc0, W_sc1)
        h0, h1 = _fctp_scalar_attr(x0, x1, z, W_l1_0, W_l1_1)
        h = jax.nn.silu(edge_features @ W_fc1 / np.sqrt(NEF))
        w = h @ W_fc2 / np.sqrt(RN)
        w0 = w[:, :MUL0]
        w1 = w[:, MUL0:2 * MUL0]
        w2 = w[:, 2 * MUL0:2 * MUL0 + MUL1]
        w3 = w[:, 2 * MUL0 + MUL1:]
        e0 = h0[edge_src]
        e1 = h1[edge_src]
        y0 = edge_attr[:, :1]
        y1 = edge_attr[:, 1:]
        m0a = w0 * e0 * y0
        m0b = w3 * jnp.einsum('eui,ei->eu', e1, y1) / np.sqrt(3.0)
        m1a = (w1 * e0)[:, :, None] * y1[:, None, :]
        m1b = w2[:, :, None] * (e1 * y0[:, :, None])
        mid_s = jnp.concatenate([m0a, m0b], axis=1)
        mid_v = jnp.concatenate([m1a, m1b], axis=1)
        inv = 1.0 / np.sqrt(NUM_NEIGHBORS)
        ns = jax.ops.segment_sum(mid_s, edge_dst, num_segments=N) * inv
        nv = jax.ops.segment_sum(mid_v, edge_dst, num_segments=N) * inv
        o0, o1 = _fctp_scalar_attr(ns, nv, z, W_l2_0, W_l2_1)
        c_s, c_x = (np.sin(np.pi / 8), np.cos(np.pi / 8))
        out0 = c_s * s0 + c_x * o0
        out1 = c_s * s1 + c_x * o1
        return jnp.concatenate([out0, out1.reshape(N, -1)], axis=1)

    def _L1_gnn_ref(node, rbf, rsh, gamma_s, beta_s, gamma_v, Ws_src, Wv_src, Ws_dst, Wv_dst, W_rbf, W_alpha, alpha_dot, Ws_val, Wv_val, Wg, w2_ss, w2_sv, w2_vs, w2_vv0, w2_vv1, Ws_vlin, Wv_vlin, Wps, Wpv, edge_index):
        import jax, jax.numpy as jnp
        import numpy as np
        N, E = (2500, 40000)
        CS, CV = (64, 32)
        AS_, AV, H = (16, 8, 4)
        NB = 16
        SQRT3 = 1.7320508075688772
        SQRT2 = 1.4142135623730951
        EPS = 1e-05

        def _cg_tp(s, v, y0, y1, w_ss, w_sv, w_vs, w_vv0, w_vv1):
            out_s = jnp.concatenate([w_ss * s * y0[:, None], w_vv0 * (jnp.einsum('eci,ei->ec', v, y1) / SQRT3)], axis=-1)
            out_v = jnp.concatenate([(w_sv * s)[:, :, None] * y1[:, None, :], (w_vs * jnp.ones_like(v[..., 0]))[..., None] * v * y0[:, None, None], (w_vv1 * jnp.ones_like(v[..., 0]))[..., None] * (jnp.cross(v, y1[:, None, :]) / SQRT2)], axis=1)
            return (out_s, out_v)

        def _equiv_layernorm(s, v, gamma_s, beta_s, gamma_v):
            mu = jnp.mean(s, axis=-1, keepdims=True)
            var = jnp.var(s, axis=-1, keepdims=True)
            s_n = (s - mu) * jax.lax.rsqrt(var + EPS) * gamma_s + beta_s
            rms = jnp.sqrt(jnp.mean(jnp.sum(v * v, axis=-1), axis=-1, keepdims=True) + EPS)
            v_n = v / rms[..., None] * gamma_v[None, :, None]
            return (s_n, v_n)
        n = node.shape[0]
        e = rsh.shape[0]
        s = node[:, :CS]
        v = node[:, CS:].reshape(n, CV, 3)
        s_n, v_n = _equiv_layernorm(s, v, gamma_s, beta_s, gamma_v)
        src, dst = (edge_index[0], edge_index[1])
        msg_s = (s_n @ Ws_src)[src] + (s_n @ Ws_dst)[dst]
        msg_v = jnp.einsum('ncx,cd->ndx', v_n, Wv_src)[src] + jnp.einsum('ncx,cd->ndx', v_n, Wv_dst)[dst]
        y0, y1 = (rsh[:, 0], rsh[:, 1:4])
        w1 = rbf @ W_rbf
        m1_s, m1_v = _cg_tp(msg_s, msg_v, y0, y1, w1[:, :CS], w1[:, CS:2 * CS], w1[:, 2 * CS:2 * CS + CV], w1[:, 2 * CS + CV:2 * CS + 2 * CV], w1[:, 2 * CS + 2 * CV:])
        a = (m1_s @ W_alpha).reshape(e, H, AS_)
        a = jnp.where(a > 0, a, 0.2 * a)
        a = jnp.sum(a * alpha_dot, axis=-1, keepdims=True)
        amax = jax.ops.segment_max(a, dst, num_segments=n)
        amax = jnp.where(jnp.isfinite(amax), amax, 0.0)
        ex = jnp.exp(a - amax[dst])
        den = jax.ops.segment_sum(ex, dst, num_segments=n)
        alpha = ex / (den[dst] + 1e-16)
        val_s = m1_s @ Ws_val
        val_v = jnp.einsum('ecx,cd->edx', m1_v, Wv_val)
        val_v = val_v * jax.nn.sigmoid(val_s @ Wg)[..., None]
        val_s = jax.nn.sigmoid(val_s)
        m2_s, m2_v = _cg_tp(val_s, val_v, y0, y1, w2_ss, w2_sv, w2_vs, w2_vv0, w2_vv1)
        hs = (m2_s @ Ws_vlin).reshape(e, H, AS_)
        hv = jnp.einsum('ecx,cd->edx', m2_v, Wv_vlin).reshape(e, H, AV, 3)
        h = jnp.concatenate([hs, hv.reshape(e, H, AV * 3)], axis=-1)
        agg = jax.ops.segment_sum(alpha * h, dst, num_segments=n)
        agg_s = agg[:, :, :AS_].reshape(n, H * AS_)
        agg_v = agg[:, :, AS_:].reshape(n, H * AV, 3)
        out = node + jnp.concatenate([agg_s @ Wps, jnp.einsum('ncx,cd->ndx', agg_v, Wpv).reshape(n, CV * 3)], axis=-1)
        return out

    def _L2_gnn_ref(x, sh, W1, W2, W3, W4, W5, Ws, Wv, edge_index):
        import jax, jax.numpy as jnp
        import numpy as np
        N, E = (6250, 100000)
        MUL0, MUL1 = (64, 32)
        D = MUL0 + 3 * MUL1
        INV3 = float(1.0 / np.sqrt(3.0))
        INV6 = float(1.0 / np.sqrt(6.0))
        C0 = float(1.0 / np.sqrt(MUL0 + MUL1))
        C1 = float(np.sqrt(3.0 / (MUL0 + 2 * MUL1)))
        LIN_S = float(1.0 / np.sqrt(MUL0))
        LIN_V = float(1.0 / np.sqrt(MUL1))
        n = x.shape[0]
        src, dst = (edge_index[0], edge_index[1])
        s = x[:, :MUL0]
        v = x[:, MUL0:].reshape(n, MUL1, 3)
        ss, vv = (s[src], v[src])
        e0 = sh[:, 0:1]
        e1 = sh[:, 1:4]
        dot = jnp.einsum('eui,ei->eu', vv, e1)
        out0 = C0 * (ss * e0 @ W1 + dot * INV3 @ W2)
        p3 = (ss @ W3)[:, :, None] * e1[:, None, :] * INV3
        p4 = jnp.einsum('eui,uw->ewi', vv * e0[:, :, None], W4) * INV3
        p5 = jnp.einsum('eui,uw->ewi', jnp.cross(vv, e1[:, None, :]), W5) * INV6
        out1 = C1 * (p3 + p4 + p5)
        m = jnp.concatenate([out0, out1.reshape(-1, 3 * MUL1)], axis=1)
        m_agg = jax.ops.segment_sum(m, dst, num_segments=n)
        hs = m_agg[:, :MUL0] @ Ws * LIN_S
        hv = jnp.einsum('nui,uw->nwi', m_agg[:, MUL0:].reshape(n, MUL1, 3), Wv) * LIN_V
        h = jnp.concatenate([hs, hv.reshape(n, 3 * MUL1)], axis=1)
        return x + jax.nn.relu(h)

    def _L3_gnn_ref(node_features, edge_index, edge_attr_tensor, node_attr_scalar_raw, Wm_ss, Wm_vv, Wm_sv, Wm_vs, Lm_s, Lm_v, Wu_ss, Wu_vv, Wu_sv, Wu_vs, Lu_s, Lu_v):
        import jax, jax.numpy as jnp
        import numpy as np
        N = 2500
        E = 80000
        INV_SQRT3 = 0.5773502691896258
        INV8 = 0.125
        INV_SQRT32 = 0.17677669529663687
        INV64 = 0.015625
        INV32 = 0.03125
        INV_SQRT2048 = 0.022097086912079608
        n = node_features.shape[0]
        e = edge_attr_tensor.shape[0]
        row, col = (edge_index[0], edge_index[1])
        r_vec = edge_attr_tensor[:, :3]
        dist = edge_attr_tensor[:, 3:4]
        xj = node_features[col]
        s = xj[:, :64]
        v = xj[:, 64:].reshape(e, 32, 3)
        m0 = s @ Wm_ss * dist * INV8 + jnp.einsum('eui,ei->eu', v, r_vec) @ Wm_vv * (INV_SQRT3 * INV_SQRT32)
        m1 = (s @ Wm_sv)[:, :, None] * r_vec[:, None, :] * INV8 + jnp.einsum('eui,uw->ewi', v, Wm_vs) * dist[:, :, None] * INV_SQRT32
        m0 = m0 + s @ Lm_s * INV8
        m1 = m1 + jnp.einsum('eui,uw->ewi', v, Lm_v) * INV_SQRT32
        msg = jnp.concatenate([m0, m1.reshape(e, 96)], axis=-1)
        agg = jax.ops.segment_sum(msg, row, num_segments=n)
        a0 = agg[:, :64]
        a1 = agg[:, 64:].reshape(n, 32, 3)
        xs = node_features[:, :64]
        xv = node_features[:, 64:].reshape(n, 32, 3)
        u0 = jnp.einsum('nu,nv,uvw->nw', xs, a0, Wu_ss) * INV64 + jnp.einsum('nui,nvi,uvw->nw', xv, a1, Wu_vv) * (INV_SQRT3 * INV32)
        u1 = jnp.einsum('nu,nvi,uvw->nwi', xs, a1, Wu_sv) * INV_SQRT2048 + jnp.einsum('nui,nv,uvw->nwi', xv, a0, Wu_vs) * INV_SQRT2048
        u0 = u0 + xs @ Lu_s * INV8
        u1 = u1 + jnp.einsum('nui,uw->nwi', xv, Lu_v) * INV_SQRT32
        upd = jnp.concatenate([u0, u1.reshape(n, 96)], axis=-1)
        return node_features + upd
    edge_index = jnp.stack([src, dst])
    h = jnp.maximum(_layernorm(x, axis=-1), 0.0)
    x = x + _L0_gnn_ref(h, node_vec1, src, dst, edge_attr_4, edge_attr_12, L0_gnn_W_sc0, L0_gnn_W_sc1, L0_gnn_W_l1_0, L0_gnn_W_l1_1, L0_gnn_W_fc1, L0_gnn_W_fc2, L0_gnn_W_l2_0, L0_gnn_W_l2_1)
    h = jnp.maximum(_layernorm(x, axis=-1), 0.0)
    x = x + _L1_gnn_ref(h, edge_attr_16, edge_attr_4, L1_gnn_gamma_s, L1_gnn_beta_s, L1_gnn_gamma_v, L1_gnn_Ws_src, L1_gnn_Wv_src, L1_gnn_Ws_dst, L1_gnn_Wv_dst, L1_gnn_W_rbf, L1_gnn_W_alpha, L1_gnn_alpha_dot, L1_gnn_Ws_val, L1_gnn_Wv_val, L1_gnn_Wg, L1_gnn_w2_ss, L1_gnn_w2_sv, L1_gnn_w2_vs, L1_gnn_w2_vv0, L1_gnn_w2_vv1, L1_gnn_Ws_vlin, L1_gnn_Wv_vlin, L1_gnn_Wps, L1_gnn_Wpv, edge_index)
    h = jnp.maximum(_layernorm(x, axis=-1), 0.0)
    x = x + _L2_gnn_ref(h, edge_attr_4, L2_gnn_W1, L2_gnn_W2, L2_gnn_W3, L2_gnn_W4, L2_gnn_W5, L2_gnn_Ws, L2_gnn_Wv, edge_index)
    h = jnp.maximum(_layernorm(x, axis=-1), 0.0)
    x = x + _L3_gnn_ref(h, edge_index, edge_attr_4, node_vec1, L3_gnn_Wm_ss, L3_gnn_Wm_vv, L3_gnn_Wm_sv, L3_gnn_Wm_vs, L3_gnn_Lm_s, L3_gnn_Lm_v, L3_gnn_Wu_ss, L3_gnn_Wu_vv, L3_gnn_Wu_sv, L3_gnn_Wu_vs, L3_gnn_Lu_s, L3_gnn_Lu_v)
    return x

_drawn_inputs = setup_inputs


def setup_inputs(seed=0):
    import zlib

    import numpy as np

    out = dict(_drawn_inputs(seed))
    spreads = {'L1_gnn_gamma_s': (1.0, 0.6), 'L1_gnn_beta_s': (0.0, 0.394), 'L1_gnn_gamma_v': (1.0, 0.6)}
    factors = {'L1_gnn_w2_vv1': 3.645}
    for name, (base, spread) in spreads.items():
        noise = np.random.default_rng([zlib.crc32(name.encode()), seed]).standard_normal(out[name].shape)
        drawn = base * np.exp(spread * noise) if base else spread * noise
        out[name] = jnp.asarray(drawn.astype(out[name].dtype))
    for name, factor in factors.items():
        out[name] = (out[name] * factor).astype(out[name].dtype)
    return out
```

```python
from contextlib import ExitStack

import concourse.bass as bass
from concourse import mybir
from concourse.alu_op_type import AluOpType as ALU

FP = mybir.dt.float32
BF = mybir.dt.bfloat16
I32 = mybir.dt.int32
ACT = mybir.ActivationFunctionType
AX = mybir.AxisListType.X

P = 128
G = 4
S, V = 64, 32
D = S + 3 * V
NB = 7
H, HA, HV = 4, 16, 8
HW = HA + 3 * HV
NO_SCORE = -3.0e38
C3, C6 = 3.0 ** -0.5, 6.0 ** -0.5
C32 = V ** -0.5


def vcol(c):
    return S + V * (c % 3)


def spread(ap, axis, n):
    ap = ap.unsqueeze(axis)
    shape = list(ap.shape)
    shape[axis] = n
    return ap.broadcast_to(shape)


def after(eng, sem, value):
    if isinstance(value, int) and value <= 0:
        return
    eng.wait_ge(sem, value)


def sweep(eng, macros, front, back):
    front(0, 0)
    front(1, 0)
    back(0, 0)
    with eng.Fori(0, macros // 2 - 1) as i:
        front(0, i + 1)
        back(1, i)
        front(1, i + 1)
        back(0, i + 1)
    back(1, macros // 2 - 1)


def nothing(b, i):
    pass


class Env:
    pass



def weight_phase(nc, e):
    w = e.ins
    T, NT = e.T, e.NT
    loads, scales = [], []

    def rows_of_vector(t, c):
        return (t[0][S:S + V], t[0][S + V:P], t[1][0:V])[c % 3]

    def place_s(t, col, name):
        ap = w[name]
        loads.append((t[0][0:S, col:col + ap.shape[1]], ap))

    def place_v(t, c, col, name):
        ap = w[name]
        loads.append((rows_of_vector(t, c)[:, col:col + ap.shape[1]], ap))

    def place_linear(t, col, ws, wv, cs, cv):
        place_s(t, col, ws)
        for c in range(3):
            place_v(t, c, col + vcol(c), wv)
        scale_cols(t, col, col + S, cs)
        scale_cols(t, col + S, col + D, cv)

    def scale_cols(t, a, b, by):
        if by != 1.0:
            scales.append((t[0][:, a:b], by))
            scales.append((t[1][:, a:b], by))

    import math
    sin8, cos8 = math.sin(math.pi / 8), math.cos(math.pi / 8)
    place_linear(e.w0, 0, "L0_gnn_W_l1_0", "L0_gnn_W_l1_1", S ** -0.5, C32)
    place_linear(e.w0, D, "L0_gnn_W_sc0", "L0_gnn_W_sc1", sin8 * S ** -0.5, sin8 * C32)
    place_linear(e.w1, 0, "L1_gnn_Ws_src", "L1_gnn_Wv_src", 1.0, 1.0)
    place_linear(e.w1, D, "L1_gnn_Ws_dst", "L1_gnn_Wv_dst", 1.0, 1.0)
    c0, c1 = (S + V) ** -0.5, (3.0 / (S + 2 * V)) ** 0.5
    place_linear(e.w2, 0, "L2_gnn_W1", "L2_gnn_W4", c0, c1 * C3)
    for c in range(3):
        off = D * (c + 1)
        place_v(e.w2, c, off, "L2_gnn_W2")
        scale_cols(e.w2, off, off + S, c0 * C3)
        place_s(e.w2, off + vcol(c), "L2_gnn_W3")
        scale_cols(e.w2, off + vcol(c), off + vcol(c) + V, c1 * C3)
        place_v(e.w2, (c + 2) % 3, off + vcol(c + 1), "L2_gnn_W5")
        scale_cols(e.w2, off + vcol(c + 1), off + vcol(c + 1) + V, c1 * C6)
        place_v(e.w2, (c + 1) % 3, off + vcol(c + 2), "L2_gnn_W5")
        scale_cols(e.w2, off + vcol(c + 2), off + vcol(c + 2) + V, -c1 * C6)
    place_linear(e.w3, 0, "L3_gnn_Lm_s", "L3_gnn_Lm_v", S ** -0.5, C32)
    place_linear(e.w3, D, "L3_gnn_Wm_ss", "L3_gnn_Wm_vs", S ** -0.5, C32)
    for c in range(3):
        off = 2 * D + (S + V) * c
        place_v(e.w3, c, off, "L3_gnn_Wm_vv")
        scale_cols(e.w3, off, off + S, C3 * C32)
        place_s(e.w3, off + S, "L3_gnn_Wm_sv")
        scale_cols(e.w3, off + S, off + S + V, S ** -0.5)
    place_linear(e.w2o, 0, "L2_gnn_Ws", "L2_gnn_Wv", S ** -0.5, C32)
    place_linear(e.w3l, 0, "L3_gnn_Lu_s", "L3_gnn_Lu_v", S ** -0.5, C32)
    out0 = cos8 * 8.0 ** -0.5 * (S + V) ** -0.5
    loads.append((e.w0s[:, :], w["L0_gnn_W_l2_0"]))
    loads.append((e.w0v[:, :], w["L0_gnn_W_l2_1"]))
    scales.append((e.w0s[:, :], out0))
    scales.append((e.w0v[:, :], out0))
    for h in range(H):
        t, r = e.w1o[h // 2], HW * (h % 2)
        loads.append((t[r:r + HA, 0:S], w["L1_gnn_Wps"][HA * h:HA * h + HA, :]))
        for c in range(3):
            a = r + HA + HV * c
            loads.append((t[a:a + HV, vcol(c):vcol(c) + V], w["L1_gnn_Wpv"][HV * h:HV * h + HV, :]))
    loads.append((e.wfc1[:, :], w["L0_gnn_W_fc1"]))
    loads.append((e.wfc2[:, :], w["L0_gnn_W_fc2"]))
    scales.append((e.wfc2[:, 0:2 * S + V], 100.0 ** -0.5))
    scales.append((e.wfc2[:, 2 * S + V:], 100.0 ** -0.5 * C3))
    loads.append((e.wrbf[:, :], w["L1_gnn_W_rbf"]))
    scales.append((e.wrbf[:, 2 * S + V:2 * S + 2 * V], C3))
    scales.append((e.wrbf[:, 2 * S + 2 * V:], 2.0 ** -0.5))
    loads.append((e.walval[:, 0:S], w["L1_gnn_W_alpha"]))
    loads.append((e.walval[:, S:2 * S], w["L1_gnn_Ws_val"]))
    loads.append((e.wvval[:, :], w["L1_gnn_Wv_val"]))
    for c in range(3):
        loads.append((e.wg[S:P, V * c:V * c + V], w["L1_gnn_Wg"]))
    loads.append((e.adcol[:, :], w["L1_gnn_alpha_dot"].rearrange("o h a -> (h a) o")))
    for name, t in (("L1_gnn_gamma_s", e.gamma_s), ("L1_gnn_beta_s", e.beta_s)):
        loads.append((t[:, :], spread(w[name], 0, P)))
    for c in range(3):
        loads.append((e.gamma_v[:, V * c:V * c + V], spread(w["L1_gnn_gamma_v"], 0, P)))
    loads.append((e.mvs0[S:P, :], w["L1_gnn_Ws_vlin"][0:S, :]))
    loads.append((e.mvs1[S:P, :], w["L1_gnn_Wv_vlin"][0:S, :]))
    loads.append((e.w2s[S:P, 0:1], w["L1_gnn_w2_ss"].unsqueeze(1)))
    loads.append((e.w2s[S:P, 1:2], w["L1_gnn_w2_sv"].unsqueeze(1)))
    for c in range(3):
        r = slice(V * c, V * c + V)
        loads.append((e.vl[r, 0:S], w["L1_gnn_Ws_vlin"][S:S + V, :]))
        loads.append((e.vl[r, S:S + V], w["L1_gnn_Wv_vlin"][S:S + V, :]))
        loads.append((e.vl[r, S + V:S + 2 * V], w["L1_gnn_Wv_vlin"][S + V:S + 2 * V, :]))
        for k, name in enumerate(("L1_gnn_w2_vv0", "L1_gnn_w2_vs", "L1_gnn_w2_vv1")):
            loads.append((e.w2v[r, k:k + 1], w[name].unsqueeze(1)))
    for t, name in ((e.src, "src_cols"), (e.dst, "dst_cols"), (e.y, "attr_cols"), (e.z, "z_cols")):
        loads.append((t[:], w[name]))

    with ExitStack() as ctx:
        zeros = ctx.enter_context(nc.sbuf_tensor("zeros", [P, 10 * 384], FP))
        empty = ctx.enter_context(nc.sbuf_tensor("empty_state", [P, 10, 168], FP))
        hsel = ctx.enter_context(nc.sbuf_tensor("head_of_row", [S, H], FP))
        cleared = ctx.enter_context(nc.semaphore("weights_cleared"))
        loaded = ctx.enter_context(nc.semaphore("weights_loaded"))
        tables = ctx.enter_context(nc.semaphore("accumulators_cleared"))
        masks = ctx.enter_context(nc.semaphore("masks_made"))
        scaled = ctx.enter_context(nc.semaphore("weights_scaled"))
        block = ctx.enter_context(nc.Block())
        per = e.NR // P
        clears = []
        for name, width in (("acc0", 384), ("acc2", D), ("acc3", D), ("state", 168)):
            for acc in e.acc[name]:
                flat = acc.rearrange("(p r) w -> p r w", p=P)
                for r in range(0, per, 10):
                    n = min(10, per - r)
                    from_ = empty[:, 0:n, :] if name == "state" else \
                        zeros[:, 0:n * width].rearrange("p (r w) -> p r w", r=n)
                    clears.append((flat[:, r:r + n, :], from_))

        @block.sync
        def _(sp):
            sp.wait_ge(cleared, 1)
            with nc.allow_non_contiguous_dma(reason="small weight columns"):
                for to, of in loads:
                    sp.dma_start(to, of).then_inc(loaded, 16)
            sp.wait_ge(loaded, 16 * len(loads))

        @block.scalar
        def _(act):
            act.wait_ge(cleared, 1)
            for to, of in clears:
                act.dma_start(to, of).then_inc(tables, 16)
            act.wait_ge(tables, 16 * len(clears))

        @block.gpsimd
        def _(pool):
            nc.gpsimd.memset(e.ident[:, :], 0.0)
            nc.gpsimd.memset(e.earlier[:, :], 1.0)
            nc.gpsimd.memset(hsel[:, :], 1.0).then_inc(masks, 1)
            pool.wait_ge(masks, 1)
            nc.gpsimd.affine_select(out=e.ident[:, :], in_=e.ident[:, :], compare_op=ALU.not_equal, fill=1.0,
                                    base=0, pattern=[[-1, P]], channel_multiplier=1)
            nc.gpsimd.affine_select(out=e.earlier[:, :], in_=e.earlier[:, :], compare_op=ALU.is_gt, fill=0.0,
                                    base=0, pattern=[[-1, P]], channel_multiplier=1)
            nc.gpsimd.iota(e.spare_i[:, :], pattern=[[0, 1]], base=e.NP, channel_multiplier=1)
            nc.gpsimd.affine_select(out=hsel[:, :], in_=hsel[:, :], compare_op=ALU.is_ge, fill=0.0,
                                    base=0, pattern=[[-HA, H]], channel_multiplier=1).then_inc(masks, 1)
            pool.wait_ge(masks, 2)
            nc.gpsimd.affine_select(out=hsel[:, :], in_=hsel[:, :], compare_op=ALU.is_ge, fill=0.0,
                                    base=HA - 1, pattern=[[HA, H]], channel_multiplier=-1).then_inc(masks, 1)

        @block.vector
        def _(dve):
            for t in (e.w0, e.w1, e.w2, e.w3, e.w2o, e.w3l, e.w1o):
                for part in t:
                    nc.vector.memset(part[:, :], 0.0)
            nc.vector.memset(e.mvv[:, :], 0.0)
            nc.vector.memset(zeros[:, :], 0.0)
            nc.vector.memset(empty[:, :, 0:H * (HW + 1)], 0.0)
            nc.vector.memset(empty[:, :, H * (HW + 1):], NO_SCORE).then_inc(cleared, 1)
            dve.wait_ge(loaded, 16 * len(loads))
            dve.wait_ge(masks, 3)
            for ap, by in scales:
                nc.vector.tensor_scalar(ap, ap, by, None, ALU.mult)
            nc.vector.tensor_copy(e.ident_bf[:, :], e.ident[:, :])
            nc.vector.tensor_copy(e.spare[:, :], e.spare_i[:, :])
            nc.vector.tensor_scalar(e.ad4[:, :], hsel[:, :], e.adcol[:, 0:1], None, ALU.mult)
            nc.vector.tensor_scalar(e.mvs0[S:P, :], e.mvs0[S:P, :], e.w2s[S:P, 0:1], 0.5, ALU.mult, ALU.mult)
            nc.vector.tensor_scalar(e.mvs1[S:P, :], e.mvs1[S:P, :], e.w2s[S:P, 1:2], 0.5, ALU.mult, ALU.mult)
            nc.vector.tensor_scalar(e.vl[:, 0:S], e.vl[:, 0:S], e.w2v[:, 0:1], 0.5 * C3, ALU.mult, ALU.mult)
            nc.vector.tensor_scalar(e.vl[:, S:S + V], e.vl[:, S:S + V], e.w2v[:, 1:2], 0.5, ALU.mult, ALU.mult)
            nc.vector.tensor_scalar(e.vl[:, S + V:], e.vl[:, S + V:], e.w2v[:, 2:3], 0.5 * 2.0 ** -0.5,
                                    ALU.mult, ALU.mult).then_inc(scaled, 1)
            dve.wait_ge(scaled, 1)
            nc.vector.tensor_copy(e.ad[:, :, :], spread(e.ad4[:, :], 2, P))
            for c in range(3):
                r = slice(V * c, V * c + V)

                def slot(k, i, r=r):
                    return e.mvv[r, :].rearrange("p (k h w) -> p k h w", k=4, h=H)[:, k, :,
                                                                                  HA + HV * i:HA + HV * i + HV]

                hs = e.mvv[r, :].rearrange("p (k h w) -> p k h w", k=4, h=H)[:, c + 1, :, 0:HA]
                nc.vector.tensor_copy(hs, e.vl[r, 0:S].rearrange("p (h a) -> p h a", h=H))
                same = e.vl[r, S:S + V].rearrange("p (h a) -> p h a", h=H)
                cross = e.vl[r, S + V:].rearrange("p (h a) -> p h a", h=H)
                nc.vector.tensor_copy(slot(0, c), same)
                nc.vector.tensor_copy(slot((c + 1) % 3 + 1, (c + 2) % 3), cross)
                nc.vector.tensor_scalar(slot((c + 2) % 3 + 1, (c + 1) % 3), cross, -1.0, None, ALU.mult)


def bilinear_weight_phase(nc, e):
    w = e.ins
    loads, scales = [], []
    for name, t, by in (("L3_gnn_Wu_ss", e.wuss, 1.0 / 64), ("L3_gnn_Wu_vv", e.wuvv, C3 / 32),
                        ("L3_gnn_Wu_sv", e.wusv, 2048.0 ** -0.5), ("L3_gnn_Wu_vs", e.wuvs, 2048.0 ** -0.5)):
        flat = w[name].rearrange("u v w -> (u v) w")
        for c in range(t.shape[1]):
            loads.append((t[:, c, :], flat[P * c:P * c + P, :]))
        scales.append((t[:, :, :], by))
    with ExitStack() as ctx:
        loaded = ctx.enter_context(nc.semaphore("bilinear_loaded"))
        block = ctx.enter_context(nc.Block())

        @block.sync
        def _(sp):
            for to, of in loads:
                sp.dma_start(to, of).then_inc(loaded, 16)
            sp.wait_ge(loaded, 16 * len(loads))

        @block.vector
        def _(dve):
            dve.wait_ge(loaded, 16 * len(loads))
            for ap, by in scales:
                nc.vector.tensor_scalar(ap, ap, by, None, ALU.mult)


def unique_phase(nc, e):
    M = e.T // G
    for ids, rows, out, tag in ((e.dst, e.dst_rows, e.dst_u, "dst"), (e.src, e.src_rows, e.src_u, "src")):
        with ExitStack() as ctx:
            ids_f = ctx.enter_context(nc.sbuf_tensor(f"{tag}_ids", [P, e.T], FP))
            row = ctx.enter_context(nc.sbuf_tensor(f"{tag}_row", [P, 2, G * P], I32))
            junk = ctx.enter_context(nc.sbuf_tensor(f"{tag}_same_earlier", [P, 2, G, P], FP))
            count = ctx.enter_context(nc.sbuf_tensor(f"{tag}_count", [P, e.T], FP))
            step = ctx.enter_context(nc.sbuf_tensor(f"{tag}_step", [P, e.T], FP))
            loaded = [ctx.enter_context(nc.semaphore(f"{tag}_row_loaded{b}")) for b in range(2)]
            counted = ctx.enter_context(nc.semaphore(f"{tag}_counted"))
            block = ctx.enter_context(nc.Block())

            @block.sync
            def _(sp, row=row, rows=rows, loaded=loaded, counted=counted):
                def front(b, i):
                    after(sp, counted, 2 * i + b)
                    sp.dma_start(row[:, b, :], rows[bass.ds(2 * i + b, 1), :].broadcast_to([P, G * P]))\
                        .then_inc(loaded[b], 16)

                sweep(sp, M, front, nothing)

            @block.vector
            def _(dve, row=row, junk=junk, count=count, step=step, loaded=loaded, counted=counted,
                  ids_f=ids_f, ids=ids, out=out):
                nc.vector.tensor_copy(ids_f[:, :], ids[:, :]).then_inc(counted, 1)
                dve.wait_ge(counted, 1)

                def front(b, i):
                    dve.wait_ge(loaded[b], 16 * (i + 1))
                    after(dve, counted, 2 * i + b)
                    for g in range(G):
                        at = bass.ds((2 * i + b) * G + g, 1)
                        last = nc.vector.scalar_tensor_tensor(
                            out=junk[:, b, g, :], in0=row[:, b, g * P:(g + 1) * P], scalar=ids_f[:, at],
                            in1=e.earlier[:, :], op0=ALU.is_equal, op1=ALU.mult, accum_out=count[:, at])
                    last.then_inc(counted, 1)

                sweep(dve, M, front, nothing)
                dve.wait_ge(counted, M + 1)
                nc.vector.tensor_scalar(count[:, :], count[:, :], 1.0, None, ALU.min)
                nc.vector.tensor_scalar(step[:, :], ids_f[:, :], -1.0, e.spare[:, 0:1], ALU.mult, ALU.add)\
                    .then_inc(counted, 1)
                dve.wait_ge(counted, M + 2)
                nc.vector.tensor_tensor(step[:, :], step[:, :], count[:, :], ALU.mult).then_inc(counted, 1)
                dve.wait_ge(counted, M + 3)
                nc.vector.tensor_tensor(out[:, :], step[:, :], ids_f[:, :], ALU.add)



def node_phase(nc, e, tag, kind_in, kind_out, base_in, base_out, w_in, w_out, tables_out):
    steps = e.NT // NB
    M_out = w_out[0].shape[-1] if w_out else 0
    in_w, in_n = {"x": (D, 0), "radial": (384, G), "attention": (168, 2 * G), "linear": (D, G),
                  "bilinear": (D, G)}[kind_in]
    accs = {"x": [], "radial": e.acc["acc0"], "attention": e.acc["state"], "linear": e.acc["acc2"],
            "bilinear": e.acc["acc3"]}[kind_in]

    with ExitStack() as ctx:
        def sb(name, shape, dt=FP):
            return ctx.enter_context(nc.sbuf_tensor(f"{tag}_{name}", shape, dt))

        def ps(name):
            return ctx.enter_context(nc.psum_tensor(f"{tag}_{name}", [P, 512], FP))

        def sem(name):
            return ctx.enter_context(nc.semaphore(f"{tag}_{name}"))

        x = sb("x", [P, NB, D])
        h = sb("h", [P, NB, D])
        sq = sb("sq", [P, NB, D])
        st = sb("st", [P, 8, NB])
        base = sb("base", [P, NB, D])
        acc = [sb(f"acc{k}", [P, NB, in_w]) for k in range(in_n)]
        tile_in = sb("in_T", [P, 2, 512])
        tile_out = sb("out_T", [P, 2, 256])
        tab = sb("tab", [P, NB, max(M_out, D)])
        ht = [ps(f"hT{k}") for k in range(2)]
        om = [ps(f"om{k}") for k in range(4)]
        loaded, made, stored = sem("loaded"), sem("made"), sem("stored")
        chain = sem("chain")
        if kind_in != "x":
            agg_ready, agg_E, agg_M = sem("agg_ready"), sem("agg_T_ready"), sem("agg_multiplied")
        if kind_in not in ("x", "bilinear"):
            agg_T, agg_O = sem("agg_transposed"), sem("agg_read")
        h_T, h_E, h_M = sem("h_transposed"), sem("h_T_ready"), sem("h_multiplied")
        if kind_in != "bilinear":
            h_ready, h_O, var_ready, std_ready = sem("h_ready"), sem("h_read"), sem("var_ready"), sem("std_ready")
        if kind_in == "bilinear":
            hin = sb("hin", [P, NB, D])
            outer = sb("outer", [P, 2, 4096])
            outer_t = sb("outer_T", [P, 4, 512])
            pt = [ps(f"pt{k}") for k in range(2)]
            o_made, o_E, o_done = (sem(f"outer_{s}") for s in ("made", "transposed", "added"))
            forms = [([0], [0], S, S, e.wuss, 0, S),
                     ([vcol(c) for c in range(3)], [vcol(c) for c in range(3)], V, V, e.wuvv, 0, S)]
            forms += [([0], [vcol(c)], S, V, e.wusv, vcol(c), V) for c in range(3)]
            forms += [([vcol(c)], [0], V, S, e.wuvs, vcol(c), V) for c in range(3)]
            ends = []
            for form in forms:
                ends.append((ends[-1] if ends else 0) + form[2] * form[3] // (4 * P))
            GROUPS = ends[-1]
        block = ctx.enter_context(nc.Block())

        def rows(ap, j):
            return ap.rearrange("(t p) w -> p t w", p=P)[:, bass.ds(NB * j, NB), :]

        chunks_in = {"radial": [(96 * c, 96) for c in range(4)], "attention": [(0, 80), (80, 80)],
                     "linear": [(0, P), (P, V)]}.get(kind_in, [])
        n_std = {"x": 1, "radial": 3, "attention": 2, "linear": 1, "bilinear": 0}[kind_in]
        n_loads = in_n + 1 + (kind_in == "bilinear")
        stores = (1 if base_out is not None else 0) + len(tables_out) + (kind_out == "bilinear_next")

        @block.sync
        def _(sp):
            with sp.Fori(0, steps) as j:
                sp.wait_ge(made, j)
                for k in range(in_n):
                    sp.dma_start(acc[k][:, :, :], rows(accs[k][0:e.NP, :], j)).then_inc(loaded, 16)
                if kind_in == "bilinear":
                    sp.dma_start(hin[:, :, :], rows(e.h3, j)).then_inc(loaded, 16)
                sp.dma_start((x if kind_in == "x" else base)[:, :, :], rows(base_in, j)).then_inc(loaded, 16)
                sp.wait_ge(made, j + 1)
                if base_out is not None:
                    sp.dma_start(rows(base_out, j), base[:, :, :]).then_inc(stored, 16)
                if kind_out == "bilinear_next":
                    sp.dma_start(rows(e.h3, j), h[:, :, :]).then_inc(stored, 16)
                at = 0
                for t in tables_out:
                    n = t.shape[1]
                    sp.dma_start(rows(t, j), tab[:, :, at:at + n]).then_inc(stored, 16)
                    at += n
            sp.wait_ge(stored, 16 * stores * steps)

        @block.vector
        def _(dve):
            n_chain = [0]

            def chained(j, ins):
                n_chain[0] += 1
                ins.then_inc(chain, 1)
                dve.wait_ge(chain, per_step * j + n_chain[0])

            def body(j):
                dve.wait_ge(loaded, 16 * n_loads * (j + 1))
                dve.wait_ge(stored, 16 * stores * j)
                n = n_chain
                if kind_in in ("radial", "linear", "bilinear"):
                    nc.vector.tensor_tensor(acc[0][:], acc[0][:], acc[1][:], ALU.add)
                    chained(j, nc.vector.tensor_tensor(acc[2][:], acc[2][:], acc[3][:], ALU.add))
                    nc.vector.tensor_tensor(acc[0][:], acc[0][:], acc[2][:], ALU.add).then_inc(agg_ready, 1)
                if kind_in == "attention":
                    nh = H * (HW + 1)
                    mx = st[:, 0:4, :].rearrange("p a b -> p b a")
                    fk = sq[:, :, 0:8 * H].rearrange("p b (k a) -> p b k a", k=8)
                    chained(j, nc.vector.tensor_tensor(mx, acc[0][:, :, nh:], acc[1][:, :, nh:], ALU.max))
                    for k in range(2, 8):
                        chained(j, nc.vector.tensor_tensor(mx, mx, acc[k][:, :, nh:], ALU.max))
                    for k in range(8):
                        last = nc.vector.tensor_tensor(fk[:, :, k, :], acc[k][:, :, nh:], mx, ALU.subtract)
                    last.then_inc(var_ready, 1)
                    dve.wait_ge(std_ready, 2 * j + 1)
                    for k in range(8):
                        for t in range(NB):
                            a = acc[k][:, t, 0:nh].rearrange("p (h w) -> p h w", h=H)
                            last = nc.vector.tensor_tensor(a, a, spread(fk[:, t, k, :], 2, HW + 1), ALU.mult)
                    chained(j, last)
                    for w in (4, 2, 1):
                        for k in range(w):
                            last = nc.vector.tensor_tensor(acc[k][:, :, 0:nh], acc[k][:, :, 0:nh],
                                                           acc[k + w][:, :, 0:nh], ALU.add)
                        chained(j, last)
                    a0 = acc[0][:, :, 0:nh].rearrange("p b (h w) -> p b h w", h=H)
                    den = st[:, 4:8, :].rearrange("p a b -> p b a")
                    chained(j, nc.vector.tensor_scalar(den, a0[:, :, :, HW], 1e-16, None, ALU.add))
                    chained(j, nc.vector.reciprocal(den, den))
                    for t in range(NB):
                        last = nc.vector.tensor_tensor(
                            sq[:, t, :].rearrange("p (h w) -> p h w", h=H),
                            acc[0][:, t, 0:nh].rearrange("p (h w) -> p h w", h=H)[:, :, 0:HW],
                            spread(st[:, 4:8, t], 2, HW), ALU.mult)
                    last.then_inc(agg_ready, 1)
                if kind_in in ("radial", "attention", "linear"):
                    for t in range(NB):
                        dve.wait_ge(agg_M, NB * j + t + 1)
                        o = om[t % 2][:, 0:D]
                        if kind_in == "radial":
                            ins = nc.vector.scalar_tensor_tensor(
                                out=x[:, t, :], in0=o, scalar=e.z_of(j, t), in1=base[:, t, :],
                                op0=ALU.mult, op1=ALU.add)
                        elif kind_in == "attention":
                            ins = nc.vector.tensor_tensor(x[:, t, :], o, base[:, t, :], ALU.add)
                        else:
                            ins = nc.vector.scalar_tensor_tensor(
                                out=x[:, t, :], in0=o, scalar=0.0, in1=base[:, t, :],
                                op0=ALU.max, op1=ALU.add)
                        ins.then_inc(agg_O, 1)
                    dve.wait_ge(agg_O, NB * (j + 1))
                if kind_in == "bilinear":
                    outers(j)
                    return
                norm(j, x[:, :, :], h, 0, D, True)
                if base_out is not None and kind_out != "radial":
                    nc.vector.tensor_tensor(base[:], x[:], h[:], ALU.add)
                if kind_out == "attention":
                    norm(j, h[:, :, 0:S], sq, 1, S, False)
                    nc.vector.tensor_tensor(sq[:, :, 0:S], sq[:, :, 0:S], spread(e.gamma_s[:, :], 1, NB), ALU.mult)
                    hv = h[:, :, S:D]
                    chained(j, nc.vector.tensor_tensor(sq[:, :, S:D], hv, hv, ALU.mult))
                    chained(j, nc.vector.tensor_reduce(st[:, 0, :], sq[:, :, S:D], AX, ALU.add))
                    nc.vector.tensor_scalar(st[:, 1, :], st[:, 0, :], 1.0 / V, 1e-5, ALU.mult, ALU.add)\
                        .then_inc(var_ready, 1)
                    dve.wait_ge(std_ready, n_std * (j + 1))
                    nc.vector.tensor_tensor(sq[:, :, 0:S], sq[:, :, 0:S], spread(e.beta_s[:, :], 1, NB), ALU.add)
                    chained(j, nc.vector.reciprocal(st[:, 3, :], st[:, 2, :]))
                    chained(j, nc.vector.tensor_tensor(sq[:, :, S:D], hv, spread(st[:, 3, :], 2, 3 * V), ALU.mult))
                    nc.vector.tensor_tensor(sq[:, :, S:D], sq[:, :, S:D], spread(e.gamma_v[:, :], 1, NB), ALU.mult)\
                        .then_inc(h_ready, 1)
                for t in range(NB):
                    dve.wait_ge(h_M, NB * j + t + 1)
                    b = t % 2
                    half = M_out // 2
                    for k in range(2):
                        src = om[2 * b + k][:, 0:half]
                        dst = tab[:, t, k * half:(k + 1) * half]
                        if kind_out == "radial":
                            if k == 0:
                                ins = nc.vector.tensor_scalar(dst, src, e.z_of(j, t), None, ALU.mult)
                            else:
                                ins = nc.vector.scalar_tensor_tensor(
                                    out=base[:, t, :], in0=src, scalar=e.z_of(j, t), in1=x[:, t, :],
                                    op0=ALU.mult, op1=ALU.add)
                        else:
                            ins = nc.vector.tensor_copy(dst, src)
                    ins.then_inc(h_O, 1)
                dve.wait_ge(h_O, NB * (j + 1))
                dve.sem_inc(made, 1)

            def norm(j, src, dst, which, width, main):
                cols = slice(0, width)
                chained(j, nc.vector.tensor_reduce(st[:, 0, :], src, AX, ALU.add))
                chained(j, nc.vector.tensor_scalar(st[:, 1, :], st[:, 0, :], 1.0 / width, None, ALU.mult))
                chained(j, nc.vector.tensor_tensor(dst[:, :, cols], src, spread(st[:, 1, :], 2, width), ALU.subtract))
                tmp = tab[:, :, 0:width]
                chained(j, nc.vector.tensor_tensor(tmp, dst[:, :, cols], dst[:, :, cols], ALU.mult))
                chained(j, nc.vector.tensor_reduce(st[:, 2, :], tmp, AX, ALU.add))
                nc.vector.tensor_scalar(st[:, 1, :], st[:, 2, :], 1.0 / width, 1e-5, ALU.mult, ALU.add)\
                    .then_inc(var_ready, 1)
                first_std = 1 if kind_in == "attention" else 0
                dve.wait_ge(std_ready, n_std * j + first_std + 1 + which)
                chained(j, nc.vector.reciprocal(st[:, 3, :], st[:, 2, :]))
                chained(j, nc.vector.tensor_tensor(dst[:, :, cols], dst[:, :, cols], spread(st[:, 3, :], 2, width),
                                                   ALU.mult))
                if main:
                    ins = nc.vector.tensor_scalar(dst[:, :, cols], dst[:, :, cols], 0.0, None, ALU.max)
                    if kind_out == "attention":
                        chained(j, ins)
                    else:
                        ins.then_inc(h_ready, 1)
                        dve.wait_ge(h_ready, j + 1)

            def outers(j):
                dve.wait_ge(agg_ready, j + 1)
                for t in range(NB):
                    for k, form in enumerate(forms):
                        before = GROUPS * (NB * j + t)
                        dve.wait_ge(o_E, before + ends[k - 2] if k >= 2 else before - (GROUPS - ends[k - 2]) if t else before)
                        u, v = form[0], form[1]
                        nu, nv = form[2], form[3]
                        o = outer[:, k % 2, 0:nu * nv].rearrange("p (u v) -> p u v", u=nu)
                        for c in range(len(u)):
                            a = spread(hin[:, t, u[c]:u[c] + nu], 2, nv)
                            bb = spread(acc[0][:, t, v[c]:v[c] + nv], 1, nu)
                            if c == 0:
                                ins = nc.vector.tensor_tensor(o, a, bb, ALU.mult)
                            else:
                                tmp = x[:, :, :].rearrange("p b w -> p (b w)")[:, 0:nu * nv]\
                                    .rearrange("p (u v) -> p u v", u=nu)
                                chained(j, ins)
                                chained(j, nc.vector.tensor_tensor(tmp, a, bb, ALU.mult))
                                ins = nc.vector.tensor_tensor(o, o, tmp, ALU.add)
                        ins.then_inc(o_made, 1)
                    dve.wait_ge(agg_M, GROUPS * (NB * j + t + 1))
                    nc.vector.tensor_tensor(base[:, t, :], om[t % 2][:, 0:D], base[:, t, :], ALU.add)\
                        .then_inc(o_done, 1)
                dve.wait_ge(o_done, NB * (j + 1))
                dve.sem_inc(made, 1)

            per_step = {("x", "radial"): 7, ("radial", "attention"): 20, ("attention", "linear"): 20,
                        ("linear", "bilinear_next"): 8, ("bilinear", None): 29}[(kind_in, kind_out)]
            with dve.Fori(0, steps) as j:
                body(j)
            assert n_chain[0] == per_step, (tag, n_chain[0], per_step)


        @block.scalar
        def _(act):
            def transposed(j, tiles, chunk_sizes, T, E, M, to):
                for t in tiles:
                    act.wait_ge(T, NB * j + t + 1)
                    act.wait_ge(M, NB * j + t - 1 if t else NB * j)
                    for c, (_, n) in enumerate(chunk_sizes):
                        last = nc.scalar.copy(to[0:n, t % 2, P * c:P * c + P], ht[t % 2][0:n, P * c:P * c + P])
                    last.then_inc(E, 1)

            with act.Fori(0, steps) as j:
                if kind_in == "attention":
                    act.wait_ge(var_ready, 2 * j + 1)
                    nc.scalar.activation(sq[:, :, 0:8 * H], sq[:, :, 0:8 * H], ACT.Exp).then_inc(std_ready, 1)
                if chunks_in:
                    transposed(j, range(NB), chunks_in, agg_T, agg_E, agg_M, tile_in)
                if kind_in == "bilinear":
                    x_chunks = [(0, P), (P, V)]
                    transposed(j, [0], x_chunks, h_T, h_E, h_M, tile_out)
                    for t in range(NB):
                        transposed(j, [t + 1] if t + 1 < NB else [], x_chunks, h_T, h_E, h_M, tile_out)
                        for k in range(GROUPS):
                            q = GROUPS * t + k
                            act.wait_ge(o_E, GROUPS * NB * j + q + 1)
                            act.wait_ge(agg_M, GROUPS * NB * j + q - 3 if q >= 3 else GROUPS * NB * j)
                            nc.scalar.copy(outer_t[:, q % 4, :], pt[q % 2][:, :]).then_inc(agg_E, 1)
                else:
                    for k in range(1 if kind_in == "attention" else 0, n_std):
                        act.wait_ge(var_ready, n_std * j + k + 1)
                        nc.scalar.activation(st[:, 2, :], st[:, 1, :], ACT.Sqrt).then_inc(std_ready, 1)
                    transposed(j, range(NB), [(0, P), (P, V)], h_T, h_E, h_M, tile_out)

        @block.tensor
        def _(pe):
            def transpose(j, t, src, chunk_list, ready, T, E):
                if t == 0:
                    pe.wait_ge(ready, j + 1)
                else:
                    pe.wait_ge(E, NB * j + t - 1)
                for c, (a, n) in enumerate(chunk_list):
                    last = nc.tensor.transpose(ht[t % 2][0:n, P * c:P * c + P], src[:, t, a:a + n], e.ident[:, :])
                last.then_inc(T, 1)

            def products(j, src, chunk_list, ready, T, E, M, O, mult):
                transpose(j, 0, src, chunk_list, ready, T, E)
                for t in range(NB):
                    if t + 1 < NB:
                        transpose(j, t + 1, src, chunk_list, ready, T, E)
                    pe.wait_ge(E, NB * j + t + 1)
                    pe.wait_ge(O, NB * j + t - 1 if t else NB * j)
                    mult(t).then_inc(M, 1)

            def mult_in(t):
                o = om[t % 2]
                if kind_in == "radial":
                    nc.tensor.matmul(o[:, 0:S], tile_in[0:96, t % 2, 0:P], e.w0s[:, :], start=True, stop=True)
                    for c in range(3):
                        last = nc.tensor.matmul(o[:, vcol(c):vcol(c) + V], tile_in[0:96, t % 2, P * (c + 1):P * (c + 2)],
                                                e.w0v[:, :], start=True, stop=True)
                    return last
                n = chunks_in
                nc.tensor.matmul(o[:, 0:D], tile_in[0:n[0][1], t % 2, 0:P], w_in[0][0:n[0][1], :],
                                 start=True, stop=False)
                return nc.tensor.matmul(o[:, 0:D], tile_in[0:n[1][1], t % 2, P:2 * P], w_in[1][0:n[1][1], :],
                                        start=False, stop=True)

            def mult_out(t):
                half = M_out // 2
                for k in range(2):
                    o = om[2 * (t % 2) + k][:, 0:half]
                    nc.tensor.matmul(o, tile_out[:, t % 2, 0:P], w_out[0][:, k * half:(k + 1) * half],
                                     start=True, stop=False)
                    last = nc.tensor.matmul(o, tile_out[0:V, t % 2, P:2 * P], w_out[1][0:V, k * half:(k + 1) * half],
                                            start=False, stop=True)
                return last

            def bilinear(j):
                transpose(j, 0, hin, [(0, P), (P, V)], agg_ready, h_T, h_E)
                for t in range(NB):
                    if t + 1 < NB:
                        transpose(j, t + 1, hin, [(0, P), (P, V)], agg_ready, h_T, h_E)
                    pe.wait_ge(h_E, NB * j + t + 1)
                    pe.wait_ge(o_done, NB * j + t - 1 if t else NB * j)
                    o = om[t % 2]
                    nc.tensor.matmul(o[:, 0:D], tile_out[:, t % 2, 0:P], w_in[0][:, :], start=True, stop=False)
                    nc.tensor.matmul(o[:, 0:D], tile_out[0:V, t % 2, P:2 * P], w_in[1][0:V, :],
                                     start=False, stop=False).then_inc(h_M, 1)
                    pending = []
                    group = 0

                    def multiply(pend):
                        q, first, form, n, is_last = pend
                        pe.wait_ge(agg_E, GROUPS * NB * j + q + 1)
                        wt, col, width = form[4], form[5], form[6]
                        for c in range(n):
                            done = nc.tensor.matmul(o[:, col:col + width], outer_t[:, q % 4, P * c:P * c + P],
                                                    wt[:, first + c, :], start=False,
                                                    stop=is_last and c == n - 1)
                        done.then_inc(agg_M, 1)

                    for k, form in enumerate(forms):
                        n_chunks = form[2] * form[3] // P
                        for first in range(0, n_chunks, 4):
                            q = GROUPS * t + group
                            if first == 0:
                                pe.wait_ge(o_made, len(forms) * (NB * j + t) + k + 1)
                            pe.wait_ge(agg_E, GROUPS * NB * j + q - 1 if q >= 1 else GROUPS * NB * j)
                            for c in range(4):
                                ins = nc.tensor.transpose(pt[q % 2][:, P * c:P * c + P],
                                                          outer[:, k % 2, P * (first + c):P * (first + c + 1)],
                                                          e.ident[:, :])
                            ins.then_inc(o_E, 1)
                            pending.append((q, first, form, 4, group == GROUPS - 1))
                            if len(pending) > 1:
                                multiply(pending.pop(0))
                            group += 1
                    multiply(pending.pop(0))

            with pe.Fori(0, steps) as j:
                if chunks_in and kind_in != "bilinear":
                    src = sq if kind_in == "attention" else acc[0]
                    products(j, src, chunks_in, agg_ready, agg_T, agg_E, agg_M, agg_O, mult_in)
                if kind_in == "bilinear":
                    bilinear(j)
                else:
                    src = sq if kind_out == "attention" else h
                    products(j, src, [(0, P), (P, V)], h_ready, h_T, h_E, h_M, h_O, mult_out)



def edge_phase(nc, e, tag, kind, macros, gather_ids, row_ids, own_ids, unique_ids, tables, accs):
    radial = kind == "radial"
    terms = {"radial": [0, 1, 2, 3], "linear": [0, 1, 2, 3], "messages": [None, 3, 0, 1, 2]}[kind]
    K = len(terms)
    W = tables[0].shape[1]
    AW = accs[0].shape[1]
    banks = 4 if radial else 2
    per_bank = G // banks

    with ExitStack() as ctx:
        def sb(name, shape, dt=FP):
            return ctx.enter_context(nc.sbuf_tensor(f"{tag}_{name}", shape, dt))

        def ps(name):
            return ctx.enter_context(nc.psum_tensor(f"{tag}_{name}", [P, 512], FP))

        def sem(name):
            return ctx.enter_context(nc.semaphore(f"{tag}_{name}"))

        row = sb("row", [P, 2, G * P], I32)
        idf = sb("ids", [P, 2, G])
        y = sb("y", [P, 2, G, 4])
        gidx = sb("gather_idx", [P, 2, G], I32)
        uidx = sb("scatter_idx", [P, 2, G], I32)
        eq = sb("same_node", [P, 2, G, K, P])
        rows_g = sb("gathered", [P, 2, G, W])
        sums = sb("sums", [P, 2, G, AW])
        acc = [[ps(f"acc{b}_{k}") for k in range(banks)] for b in range(1 if radial else 2)]
        row_loaded = [sem(f"row_loaded{b}") for b in range(2)]
        gathered = [sem(f"gathered{b}") for b in range(2)]
        scattered, pool_passed = sem("scattered"), sem("pool_passed")
        staged, eq_ready, eq_used, sums_ready = sem("staged"), sem("eq_ready"), sem("eq_used"), sem("sums_ready")
        if radial:
            ef = sb("features", [12, 2, G * P])
            act_h = sb("hidden", [100, 2, G * P])
            mid = sb("messages", [P, 2, G, 2 * D])
            ph = [ps(f"hidden{b}") for b in range(2)]
            pw = [ps(f"weights{k}") for k in range(2)]
            ef_loaded = [sem(f"features_loaded{b}") for b in range(2)]
            h_lin, h_act, w_ready, mid_ready = sem("hidden_linear"), sem("hidden_ready"), sem("w_ready"), sem("mid_ready")
        block = ctx.enter_context(nc.Block())

        @block.sync
        def _(sp):
            def front(b, i):
                m = 2 * i + b
                after(sp, eq_ready, m - 1)
                sp.dma_start(row[:, b, :], row_ids[bass.ds(m, 1), :].broadcast_to([P, G * P])).then_inc(row_loaded[b], 16)
                if radial:
                    after(sp, h_lin, m - 1)
                    sp.dma_start(ef[:, b, :], e.ins["features_12"][:, bass.ds(m * (G * P), G * P)])\
                        .then_inc(ef_loaded[b], 16)

            sweep(sp, macros, front, nothing)

        @block.gpsimd
        def _(pool):
            def passed():
                pool.sem_inc(pool_passed, 1)

            def front(b, i):
                m = 2 * i + b
                pool.wait_ge(staged, m + 1)
                passed()
                after(pool, mid_ready if radial else eq_used, m - 1)
                passed()
                for g in range(G):
                    pool.indirect_dma_start(
                        out=rows_g[:, b, g, :], out_offset=None, in_=tables[0][:, :],
                        in_offset=bass.IndirectOffsetOnAxis(ap=gidx[:, b, g:g + 1], axis=0))\
                        .then_inc(gathered[b], 16)

            def back(b, i):
                m = 2 * i + b
                pool.wait_ge(sums_ready, m + 1)
                passed()
                after(pool, scattered, 16 * G * m)
                passed()
                for g in range(G):
                    pool.indirect_dma_start(
                        out=accs[g][:, :], out_offset=bass.IndirectOffsetOnAxis(ap=uidx[:, b, g:g + 1], axis=0),
                        in_=sums[:, b, g, :], in_offset=None, compute_op=ALU.add).then_inc(scattered, 16)

            sweep(pool, macros, front, back)
            pool.wait_ge(scattered, 16 * G * macros)

        @block.vector
        def _(dve):
            def front(b, i):
                m = 2 * i + b
                after(dve, gathered[b], 16 * G * i)
                after(dve, scattered, 16 * G * (m - 1))
                cols = bass.ds(m * G, G)
                nc.vector.tensor_copy(gidx[:, b, :], gather_ids[:, cols])
                nc.vector.tensor_copy(uidx[:, b, :], unique_ids[:, cols])
                nc.vector.tensor_copy(idf[:, b, :], own_ids[:, cols])
                nc.vector.tensor_copy(y[:, b, :, :], e.y[:, cols, :]).then_inc(staged, 1)
                dve.wait_ge(staged, m + 1)
                dve.wait_ge(row_loaded[b], 16 * (i + 1))
                after(dve, eq_used, m - 1)
                for g in range(G):
                    same = row[:, b, g * P:(g + 1) * P]
                    for k, c in enumerate(terms):
                        if c is None:
                            last = nc.vector.tensor_scalar(eq[:, b, g, k, :], same, idf[:, b, g:g + 1], None,
                                                           ALU.is_equal)
                        else:
                            last = nc.vector.tensor_scalar(eq[:, b, g, k, :], same, idf[:, b, g:g + 1],
                                                           y[:, b, g, c:c + 1], ALU.is_equal, ALU.mult)
                last.then_inc(eq_ready, 1)
                if radial:
                    dve.wait_ge(gathered[b], 16 * G * (i + 1))
                    dve.wait_ge(w_ready, m + 1)
                    for k in range(2):
                        w = pw[k][:, 0:384].rearrange("p (g w) -> p g w", g=2)
                        two = slice(2 * k, 2 * k + 2)
                        src = rows_g[:, b, two, :]
                        to = mid[:, b, two, :]
                        vec = src[:, :, S:D].rearrange("p g (c u) -> p g c u", c=3)
                        nc.vector.tensor_tensor(to[:, :, 0:S], w[:, :, 0:S], src[:, :, 0:S], ALU.mult)
                        nc.vector.tensor_tensor(to[:, :, D:D + S], w[:, :, S:2 * S], src[:, :, 0:S], ALU.mult)
                        for r, off in ((0, S), (1, D + S)):
                            a = 2 * S + V * r
                            last = nc.vector.tensor_tensor(
                                to[:, :, off:off + 3 * V].rearrange("p g (c u) -> p g c u", c=3),
                                spread(w[:, :, a:a + V], 2, 3), vec, ALU.mult)
                    last.then_inc(mid_ready, 1)

            sweep(dve, macros, front, nothing)

        @block.scalar
        def _(act):
            def front(b, i):
                m = 2 * i + b
                if radial:
                    act.wait_ge(h_lin, m + 1)
                    after(act, w_ready, m - 1)
                    nc.scalar.activation(act_h[:, b, :], ph[b][0:100, :], ACT.Silu, scale=12.0 ** -0.5)\
                        .then_inc(h_act, 1)

            def back(b, i):
                m = 2 * i + b
                act.wait_ge(eq_used, m + 1)
                after(act, scattered, 16 * G * (m - 1))
                for k in range(banks):
                    last = nc.scalar.copy(
                        sums[:, b, k * per_bank:(k + 1) * per_bank, :].rearrange("p g w -> p (g w)"),
                        acc[b % len(acc)][k][:, 0:per_bank * AW])
                last.then_inc(sums_ready, 1)

            sweep(act, macros, front, back)

        @block.tensor
        def _(pe):
            def front(b, i):
                m = 2 * i + b
                if radial:
                    pe.wait_ge(ef_loaded[b], 16 * (i + 1))
                    after(pe, h_act, m - 1)
                    nc.tensor.matmul(ph[b][0:100, :], e.wfc1[:, :], ef[:, b, :], start=True, stop=True)\
                        .then_inc(h_lin, 1)
                    pe.wait_ge(h_act, m + 1)
                    after(pe, mid_ready, m)
                    for g in range(G):
                        last = nc.tensor.matmul(pw[g // 2][:, 192 * (g % 2):192 * (g % 2) + 192],
                                                act_h[:, b, g * P:(g + 1) * P], e.wfc2[:, :], start=True, stop=True)
                    last.then_inc(w_ready, 1)

            def back(b, i):
                m = 2 * i + b
                pe.wait_ge(eq_ready, m + 1)
                if radial:
                    pe.wait_ge(mid_ready, m + 1)
                    after(pe, sums_ready, m)
                else:
                    pe.wait_ge(gathered[b], 16 * G * (i + 1))
                    after(pe, sums_ready, m - 1)
                for g in range(G):
                    o = acc[b % len(acc)][g // per_bank][:, AW * (g % per_bank):AW * (g % per_bank + 1)]
                    a = rows_g[:, b, g, :]
                    if kind == "linear":
                        for k in range(4):
                            last = nc.tensor.matmul(o, eq[:, b, g, k, :], a[:, D * k:D * k + D],
                                                    start=k == 0, stop=k == 3)
                    elif kind == "messages":
                        for k in range(2):
                            nc.tensor.matmul(o, eq[:, b, g, k, :], a[:, D * k:D * k + D], start=k == 0, stop=False)
                        for c in range(3):
                            off = 2 * D + (S + V) * c
                            nc.tensor.matmul(o[:, 0:S], eq[:, b, g, 2 + c, :], a[:, off:off + S],
                                             start=False, stop=False)
                            last = nc.tensor.matmul(o[:, vcol(c):vcol(c) + V], eq[:, b, g, 2 + c, :],
                                                    a[:, off + S:off + S + V], start=False, stop=c == 2)
                    else:
                        q = mid[:, b, g, :]
                        nc.tensor.matmul(o[:, 0:S], eq[:, b, g, 0, :], q[:, 0:S], start=True, stop=False)
                        nc.tensor.matmul(o[:, S + V:].rearrange("p (c w) -> p c w", c=3)[:, :, S:S + V],
                                         eq[:, b, g, 0, :], q[:, S:D].rearrange("p (c w) -> p c w", c=3),
                                         start=False, stop=False)
                        for c in range(3):
                            off = (S + V) * (c + 1)
                            nc.tensor.matmul(o[:, off:off + S], eq[:, b, g, c + 1, :], q[:, D:D + S],
                                             start=False, stop=False)
                            last = nc.tensor.matmul(o[:, S:S + V], eq[:, b, g, c + 1, :],
                                                    q[:, D + vcol(c):D + vcol(c) + V],
                                                    start=False, stop=c == 2)
                last.then_inc(eq_used, 1)

            sweep(pe, macros, front, back)


def long_sweep(eng, macros, f0, f1, back, f2):
    def at(f, m, i=None):
        if i is None:
            f(m % 2, m // 2)
        else:
            f(m % 2, i + m // 2)

    def step(m, i=None):
        at(f0, m + 2, i)
        at(f1, m + 1, i)
        at(back, m, i)
        at(f2, m + 1, i)

    at(f0, 0)
    at(f0, 1)
    at(f1, 0)
    at(f2, 0)
    step(0)
    with eng.Fori(0, macros // 2 - 2) as i:
        step(1, i)
        step(2, i)
    step(macros - 3)
    at(f1, macros - 1)
    at(back, macros - 2)
    at(f2, macros - 1)
    at(back, macros - 1)


def attention_phase(nc, e, macros):
    SW = H * (HW + 1) + H
    NH = H * (HW + 1)
    E1 = 2 * S + 3 * V
    with ExitStack() as ctx:
        def sb(name, shape, dt=FP):
            return ctx.enter_context(nc.sbuf_tensor(f"att_{name}", shape, dt))

        def ps(name):
            return ctx.enter_context(nc.psum_tensor(f"att_{name}", [P, 512], FP))

        def sem(name):
            return ctx.enter_context(nc.semaphore(f"att_{name}"))

        row = sb("row", [P, 2, G * P], I32)
        rbf = sb("rbf", [16, 2, G * P])
        idf = sb("ids", [P, 2, G])
        y = sb("y", [P, 2, G, 6])
        sidx, didx, uidx = (sb(n, [P, 2, G], I32) for n in ("src_idx", "dst_idx", "scatter_idx"))
        ga, gb = sb("from_src", [P, 2, G, D]), sb("from_dst", [P, 2, G, D])
        msg = sb("msg", [P, G, D + 2 * V])
        xs = sb("weighted_s", [P, G, 2, S])
        vs, vv0, vv1 = sb("weighted_v", [P, G, 3, V]), sb("dot_v", [P, G, 3, V]), sb("cross_v", [P, G, 5, V])
        t1, t2, t3 = (sb(f"product{k}", [P, G, 3, V]) for k in range(3))
        dot = sb("dot", [P, G, V])
        m1s, m1v = sb("m1_s", [P, G, S + V]), sb("m1_v", [P, G, 3, P])
        m1t = sb("m1_T", [P, 4, G * P])
        relu_t, lk = sb("relu", [S, G * P]), sb("leaky", [S, 2, G * P])
        vraw, tv, vst = sb("val_s", [P, G * P]), sb("tanh_s", [P, G * P]), sb("gated_s", [P, 2, G * P])
        tg, vvt = sb("tanh_gate", [3 * V, G * P]), sb("gated_v", [3 * V, 2, G * P])
        eq = sb("same_node", [P, 2, G, 5, P])
        other = sb("other_node", [P, 2, G, P], BF)
        mt = sb("tile_max", [P, G, H])
        dd, ex = sb("differences", [P, G, 3, H]), sb("exps", [P, G, 3, H])
        pp = sb("weighted_values", [P, 2, 4 * D])
        old, new = sb("old_state", [P, 2, G, SW]), sb("new_state", [P, 2, G, SW])
        told, tnew = sb("scaled_old", [P, G, NH]), sb("scaled_new", [P, G, NH])
        F = [ps(f"front{k}") for k in range(4)]
        B = [ps(f"back{k}") for k in range(4)]
        row_loaded, rbf_loaded, ends_gathered, state_gathered, scattered = (
            [sem(f"{n}{b}") for b in range(2)] for n in
            ("row_loaded", "rbf_loaded", "ends_gathered", "state_gathered", "scattered"))
        (pool_passed, staged, msg_done, w1_ready, m1_ready, T_ready, evac, al_ready, vv_ready, vraw_ready, vact,
         gate_ready, tg_done, eq_ready, cd_done, bc_ready, a_ready, max_done, d_ready, ex_ready, pk_ready,
         pp_done, s_done, sums_ready) = (sem(n) for n in (
             "pool_passed", "staged", "msg_done", "w1_ready", "m1_ready", "m1_transposed", "m1_T_ready",
             "alpha_ready", "vv_ready", "vraw_ready", "val_activated", "gate_ready", "gate_activated", "eq_ready",
             "values_ready", "scores_spread", "scores_ready", "max_done", "differences_ready", "exps_ready",
             "products_ready", "weighted_ready", "summed", "state_ready"))
        f0_chain, f1_chain, back_chain = sem("f0_chain"), sem("f1_chain"), sem("back_chain")
        block = ctx.enter_context(nc.Block())

        @block.sync
        def _(sp):
            def f0(b, i):
                m = 2 * i + b
                after(sp, eq_ready, m - 1)
                sp.dma_start(row[:, b, :], e.dst_rows[bass.ds(m, 1), :].broadcast_to([P, G * P]))\
                    .then_inc(row_loaded[b], 16)
                after(sp, w1_ready, m - 1)
                sp.dma_start(rbf[:, b, :], e.ins["features_16"][:, bass.ds(m * (G * P), G * P)])\
                    .then_inc(rbf_loaded[b], 16)

            long_sweep(sp, macros, f0, nothing, nothing, nothing)

        @block.gpsimd
        def _(pool):
            def passed():
                pool.sem_inc(pool_passed, 1)

            def gather(to, table, idx, sem):
                pool.indirect_dma_start(out=to, out_offset=None, in_=table[:, :],
                                        in_offset=bass.IndirectOffsetOnAxis(ap=idx, axis=0)).then_inc(sem, 16)

            def f0(b, i):
                m = 2 * i + b
                pool.wait_ge(staged, m + 1)
                passed()
                after(pool, msg_done, m - 1)
                passed()
                for g in range(G):
                    gather(ga[:, b, g, :], e.tab_src, sidx[:, b, g:g + 1], ends_gathered[b])
                    gather(gb[:, b, g, :], e.tab_dst, didx[:, b, g:g + 1], ends_gathered[b])

            def f1(b, i):
                after(pool, scattered[b], 16 * G * i)
                passed()
                for g in range(G):
                    gather(old[:, b, g, :], e.acc["state"][G * b + g], didx[:, b, g:g + 1], state_gathered[b])

            def back(b, i):
                pool.wait_ge(sums_ready, 2 * i + b + 1)
                passed()
                for g in range(G):
                    pool.indirect_dma_start(
                        out=e.acc["state"][G * b + g][:, :],
                        out_offset=bass.IndirectOffsetOnAxis(ap=uidx[:, b, g:g + 1], axis=0),
                        in_=new[:, b, g, :], in_offset=None).then_inc(scattered[b], 16)

            long_sweep(pool, macros, f0, f1, back, nothing)
            for b in range(2):
                pool.wait_ge(scattered[b], 16 * G * macros // 2)

        @block.vector
        def _(dve):
            def f0(b, i):
                m = 2 * i + b
                after(dve, ends_gathered[b], 32 * G * i)
                after(dve, state_gathered[b], 16 * G * i)
                after(dve, eq_ready, m - 1)
                cols = bass.ds(m * G, G)
                nc.vector.tensor_copy(sidx[:, b, :], e.src[:, cols])
                nc.vector.tensor_copy(didx[:, b, :], e.dst[:, cols])
                nc.vector.tensor_copy(idf[:, b, :], e.dst[:, cols])
                nc.vector.tensor_copy(y[:, b, :, 0:4], e.y[:, cols, :])
                nc.vector.tensor_copy(y[:, b, :, 4:6], e.y[:, cols, 1:3]).then_inc(staged, 1)

            def f1(b, i):
                m = 2 * i + b
                dve.wait_ge(ends_gathered[b], 32 * G * (i + 1))
                nc.vector.tensor_tensor(msg[:, :, 0:D], ga[:, b], gb[:, b], ALU.add)
                nc.vector.tensor_tensor(msg[:, :, D:], ga[:, b, :, S:S + 2 * V], gb[:, b, :, S:S + 2 * V], ALU.add)\
                    .then_inc(msg_done, 1)
                dve.wait_ge(msg_done, m + 1)
                dve.wait_ge(staged, m + 1)
                dve.wait_ge(w1_ready, m + 1)
                after(dve, T_ready, 4 * m)
                for k in range(2):
                    w = F[k][:, 0:2 * E1].rearrange("p (g w) -> p g w", g=2)
                    two = slice(2 * k, 2 * k + 2)
                    nc.vector.tensor_tensor(xs[:, two], w[:, :, 0:2 * S].rearrange("p g (k s) -> p g k s", k=2),
                                            spread(msg[:, two, 0:S], 2, 2), ALU.mult)
                    for to, r, n in ((vs, 0, 3), (vv0, 1, 3), (vv1, 2, 5)):
                        a = 2 * S + V * r
                        last = nc.vector.tensor_tensor(
                            to[:, two], msg[:, two, S:S + n * V].rearrange("p g (c u) -> p g c u", c=n),
                            spread(w[:, :, a:a + V], 2, n), ALU.mult)
                last.then_inc(f1_chain, 1)
                dve.wait_ge(f1_chain, 3 * m + 1)

                def ys(a, n, width):
                    return spread(y[:, b, :, a:a + n], 3, width)

                y0 = y[:, b, :, 0]
                nc.vector.tensor_tensor(t1[:], vv0[:], ys(1, 3, V), ALU.mult)
                nc.vector.tensor_tensor(t2[:], vv1[:, :, 1:4], ys(3, 3, V), ALU.mult)
                nc.vector.tensor_tensor(t3[:], vv1[:, :, 2:5], ys(2, 3, V), ALU.mult).then_inc(f1_chain, 1)
                nc.vector.tensor_tensor(m1s[:, :, 0:S], xs[:, :, 0], spread(y0, 2, S), ALU.mult)
                nc.vector.tensor_tensor(m1v[:, :, :, 0:S], spread(xs[:, :, 1], 2, 3), ys(1, 3, S), ALU.mult)
                nc.vector.tensor_tensor(m1v[:, :, :, S:S + V], vs[:], spread(spread(y0, 2, 3), 3, V), ALU.mult)
                dve.wait_ge(f1_chain, 3 * m + 2)
                nc.vector.tensor_tensor(dot[:], t1[:, :, 0], t1[:, :, 1], ALU.add).then_inc(f1_chain, 1)
                nc.vector.tensor_tensor(m1v[:, :, :, S + V:], t2[:], t3[:], ALU.subtract)
                dve.wait_ge(f1_chain, 3 * m + 3)
                nc.vector.tensor_tensor(m1s[:, :, S:], dot[:], t1[:, :, 2], ALU.add).then_inc(m1_ready, 1)

            def back(b, i):
                m = 2 * i + b
                for h in range(H):
                    dve.wait_ge(bc_ready, 4 * m + h + 1)
                    nc.vector.tensor_reduce(mt[:, :, h], B[h % 2][:, :].rearrange("p (g q) -> p g q", g=G),
                                            AX, ALU.max).then_inc(max_done, 1)
                after(dve, scattered[b], 16 * G * i)
                nc.vector.tensor_copy(uidx[:, b, :], e.dst_u[:, bass.ds(m * G, G)])
                dve.wait_ge(max_done, 4 * m + 4)
                dve.wait_ge(state_gathered[b], 16 * G * (i + 1))
                nc.vector.tensor_tensor(new[:, b, :, NH:], old[:, b, :, NH:], mt[:], ALU.max)\
                    .then_inc(back_chain, 1)
                dve.wait_ge(a_ready, m + 1)
                nc.vector.tensor_tensor(dd[:, :, 0], B[2][:, 0:G * H].rearrange("p (g h) -> p g h", g=G), mt[:],
                                        ALU.subtract)
                dve.wait_ge(back_chain, 2 * m + 1)
                nc.vector.tensor_tensor(dd[:, :, 1], old[:, b, :, NH:], new[:, b, :, NH:], ALU.subtract)
                nc.vector.tensor_tensor(dd[:, :, 2], mt[:], new[:, b, :, NH:], ALU.subtract).then_inc(d_ready, 1)
                dve.wait_ge(ex_ready, m + 1)

                def heads(ap, w):
                    return ap.rearrange("p g (h w) -> p g h w", h=H)

                nc.vector.tensor_tensor(heads(told[:], 0), heads(old[:, b, :, 0:NH], 0),
                                        spread(ex[:, :, 1], 3, HW + 1), ALU.mult)
                for t in range(G):
                    after(dve, s_done, 4 * m + t - 1)
                    for k in range(2):
                        dve.wait_ge(pk_ready, 8 * m + 2 * t + k + 1)
                        nc.vector.tensor_tensor(
                            pp[:, t % 2, 2 * D * k:2 * D * k + 2 * D].rearrange("p (k h w) -> p k h w", k=2, h=H),
                            B[k][:, 0:2 * D].rearrange("p (k h w) -> p k h w", k=2, h=H),
                            spread(spread(ex[:, t, 0], 1, 2), 3, HW), ALU.mult).then_inc(pp_done, 1)
                for k in range(2):
                    two = slice(2 * k, 2 * k + 2)
                    dve.wait_ge(s_done, 4 * m + 2 * k + 2)
                    ins = nc.vector.tensor_tensor(
                        heads(tnew[:, two], 0), heads(B[2 + k][:, 0:2 * NH].rearrange("p (g w) -> p g w", g=2), 0),
                        spread(ex[:, two, 2], 3, HW + 1), ALU.mult)
                ins.then_inc(back_chain, 1)
                dve.wait_ge(back_chain, 2 * m + 2)
                nc.vector.tensor_tensor(new[:, b, :, 0:NH], told[:], tnew[:], ALU.add).then_inc(sums_ready, 1)

            def f2(b, i):
                m = 2 * i + b
                dve.wait_ge(row_loaded[b], 16 * (i + 1))
                after(dve, s_done, 4 * (m - 1))
                same = row[:, b, :].rearrange("p (g q) -> p g q", g=G)
                for g in range(G):
                    mine = idf[:, b, g:g + 1]
                    nc.vector.tensor_scalar(other[:, b, g, :], same[:, g], mine, NO_SCORE, ALU.not_equal, ALU.mult)
                    nc.vector.tensor_scalar(eq[:, b, g, 4, :], same[:, g], mine, None, ALU.is_equal)
                    for k in range(4):
                        last = nc.vector.tensor_scalar(eq[:, b, g, k, :], same[:, g], mine, y[:, b, g, k:k + 1],
                                                       ALU.is_equal, ALU.mult)
                last.then_inc(eq_ready, 1)
                dve.wait_ge(vact, m + 1)
                nc.vector.scalar_tensor_tensor(out=lk[:, b, :], in0=F[0][0:S, :], scalar=0.2, in1=relu_t[:, :],
                                               op0=ALU.mult, op1=ALU.add)
                nc.vector.tensor_scalar(vst[S:P, b, :], tv[S:P, :], 1.0, None, ALU.add)
                dve.wait_ge(vv_ready, m + 1)
                dve.wait_ge(tg_done, m + 1)
                nc.vector.scalar_tensor_tensor(out=vvt[:, b, :], in0=tg[:, :], scalar=1.0, in1=F[1][0:3 * V, :],
                                               op0=ALU.add, op1=ALU.mult).then_inc(cd_done, 1)

            long_sweep(dve, macros, f0, f1, back, f2)

        @block.scalar
        def _(act):
            def back(b, i):
                m = 2 * i + b
                act.wait_ge(d_ready, m + 1)
                after(act, s_done, 4 * m)
                nc.scalar.activation(ex[:], dd[:], ACT.Exp).then_inc(ex_ready, 1)

            def f2(b, i):
                m = 2 * i + b
                for q in range(4):
                    act.wait_ge(T_ready, 4 * m + q + 1)
                    after(act, vv_ready if q else al_ready, m)
                    n = P if q else S + V
                    nc.scalar.copy(m1t[0:n, q, :], F[2 + q % 2][0:n, :]).then_inc(evac, 1)
                act.wait_ge(al_ready, m + 1)
                after(act, gate_ready, m)
                nc.scalar.copy(vraw[S:P, :], F[0][S:P, :]).then_inc(vraw_ready, 1)
                after(act, cd_done, m)
                nc.scalar.activation(relu_t[:, :], F[0][0:S, :], ACT.Relu, scale=0.8)
                nc.scalar.activation(tv[S:P, :], F[0][S:P, :], ACT.Tanh, scale=0.5).then_inc(vact, 1)
                act.wait_ge(gate_ready, m + 1)
                nc.scalar.activation(tg[:, :], F[2][0:3 * V, :], ACT.Tanh, scale=0.5).then_inc(tg_done, 1)

            long_sweep(act, macros, nothing, nothing, back, f2)

        @block.tensor
        def _(pe):
            def f1(b, i):
                m = 2 * i + b
                pe.wait_ge(rbf_loaded[b], 16 * (i + 1))
                after(pe, cd_done, m)
                for g in range(G):
                    last = nc.tensor.matmul(F[g // 2][:, E1 * (g % 2):E1 * (g % 2) + E1],
                                            rbf[:, b, g * P:(g + 1) * P], e.wrbf[:, :], start=True, stop=True)
                last.then_inc(w1_ready, 1)

            def f2(b, i):
                m = 2 * i + b
                pe.wait_ge(m1_ready, m + 1)
                after(pe, tg_done, m)
                for q in range(4):
                    if q >= 2:
                        pe.wait_ge(evac, 4 * m + q - 1)
                    for g in range(G):
                        src = m1v[:, g, q - 1, :] if q else m1s[:, g, :]
                        n = P if q else S + V
                        last = nc.tensor.transpose(F[2 + q % 2][0:n, g * P:(g + 1) * P], src, e.ident[:, :])
                    last.then_inc(T_ready, 1)
                pe.wait_ge(evac, 4 * m + 1)
                nc.tensor.matmul(F[0][:, :], e.walval[:, :], m1t[0:S + V, 0, :], start=True, stop=True)\
                    .then_inc(al_ready, 1)
                for c in range(3):
                    pe.wait_ge(evac, 4 * m + 2 + c)
                    last = nc.tensor.matmul(F[1][V * c:V * c + V, :], e.wvval[:, :], m1t[:, 1 + c, :],
                                            start=True, stop=True)
                last.then_inc(vv_ready, 1)
                pe.wait_ge(vraw_ready, m + 1)
                nc.tensor.matmul(F[2][0:3 * V, :], e.wg[S:P, :], vraw[S:P, :], start=True, stop=True)\
                    .then_inc(gate_ready, 1)

            def back(b, i):
                m = 2 * i + b
                pe.wait_ge(cd_done, m + 1)
                pe.wait_ge(eq_ready, m + 1)
                after(pe, sums_ready, m)
                for g in range(G):
                    last = nc.tensor.matmul(B[2][:, H * g:H * g + H], lk[:, b, g * P:(g + 1) * P], e.ad4[:, :],
                                            start=True, stop=True)
                last.then_inc(a_ready, 1)
                for h in range(H):
                    if h < 2:
                        after(pe, pp_done, 8 * m)
                    else:
                        pe.wait_ge(max_done, 4 * m + h - 1)
                    nc.tensor.matmul(B[h % 2][:, :], e.ad[:, h, :], lk[:, b, :], start=True, stop=False)
                    nc.tensor.matmul(B[h % 2][:, :], e.ident_bf[:, :], other[:, b].rearrange("p g q -> p (g q)"),
                                     start=False, stop=True).then_inc(bc_ready, 1)

                def products(t):
                    tile = slice(t * P, (t + 1) * P)
                    for k in range(2):
                        if t:
                            pe.wait_ge(pp_done, 8 * m + 2 * (t - 1) + k + 1)
                        else:
                            pe.wait_ge(max_done, 4 * m + 3 + k)
                        nc.tensor.matmul(B[k][:, 0:2 * D], vvt[:, b, tile], e.mvv[:, 2 * D * k:2 * D * k + 2 * D],
                                         start=True, stop=False)
                        for j in (2 * k, 2 * k + 1):
                            o = B[k][:, D * (j % 2):D * (j % 2) + D].rearrange("p (h w) -> p h w", h=H)
                            if j == 0:
                                o, w = o[:, :, 0:HA], e.mvs0
                            else:
                                o, w = o[:, :, HA + HV * (j - 1):HA + HV * j], e.mvs1
                            last = nc.tensor.matmul(o, vst[S:P, b, tile],
                                                    w[S:P, :].rearrange("p (h w) -> p h w", h=H),
                                                    start=False, stop=j % 2 == 1)
                        last.then_inc(pk_ready, 1)

                def sums(t):
                    pe.wait_ge(pp_done, 8 * m + 2 * t + 2)
                    o = B[2 + t // 2][:, NH * (t % 2):NH * (t % 2) + NH].rearrange("p (h w) -> p h w", h=H)
                    for k in range(4):
                        nc.tensor.matmul(o[:, :, 0:HW], eq[:, b, t, k, :],
                                         pp[:, t % 2, D * k:D * k + D].rearrange("p (h w) -> p h w", h=H),
                                         start=k == 0, stop=False)
                    nc.tensor.matmul(o[:, :, HW], eq[:, b, t, 4, :], ex[:, t, 0, :], start=False, stop=True)\
                        .then_inc(s_done, 1)

                products(0)
                for t in range(G):
                    if t + 1 < G:
                        products(t + 1)
                    sums(t)

            long_sweep(pe, macros, nothing, f1, back, f2)



def gnn_program(nc, ins, out):
    e = Env()
    e.ins = ins
    e.NT = ins["z_cols"].shape[1]
    e.T = ins["src_cols"].shape[1]
    e.NP = e.NT * P
    e.NR = e.NP + P
    e.src_rows, e.dst_rows = ins["src_rows"], ins["dst_rows"]
    macros = e.T // G

    def dram(name, shape):
        return nc.dram_tensor(name, shape, FP, kind="Internal").ap()

    base = [dram(f"stream{k}", [e.NP, D]) for k in range(4)]
    e.h3 = dram("h3", [e.NP, D])
    tab0, e.tab_src, e.tab_dst = (dram(n, [e.NP, D]) for n in ("table0", "table1_src", "table1_dst"))
    tab2, tab3 = dram("table2", [e.NP, 4 * D]), dram("table3", [e.NP, 2 * D + 3 * (S + V)])
    e.acc = {name: [dram(f"{name}_{k}", [e.NR, w]) for k in range(n)]
             for name, w, n in (("acc0", 384, G), ("state", 168, 2 * G), ("acc2", D, G), ("acc3", D, G))}

    with ExitStack() as ctx:
        def sb(name, shape, dt=FP):
            return ctx.enter_context(nc.sbuf_tensor(name, shape, dt))

        def pair(name, cols):
            return sb(name + "_a", [P, cols]), sb(name + "_b", [V, cols])

        e.src, e.dst, e.src_u, e.dst_u = (sb(n, [P, e.T], I32) for n in ("src", "dst", "src_unique", "dst_unique"))
        e.y, e.z = sb("attr", [P, e.T, 4]), sb("z", [P, e.NT])
        e.z_of = lambda j, t: e.z[:, bass.ds(NB * j + t, 1)]
        e.ident, e.ident_bf, e.earlier = sb("identity", [P, P]), sb("identity_bf", [P, P], BF), sb("earlier", [P, P])
        e.spare, e.spare_i = sb("spare_row", [P, 1]), sb("spare_row_i", [P, 1], I32)
        e.w0, e.w1, e.w2, e.w3 = pair("w0", 2 * D), pair("w1", 2 * D), pair("w2", 4 * D), pair("w3", 2 * D + 3 * (S + V))
        e.w2o, e.w3l = pair("w2_out", D), pair("w3_lin", D)
        e.w1o = (sb("w1_out_a", [80, D]), sb("w1_out_b", [80, D]))
        e.w0s, e.w0v = sb("w0_out_s", [S + V, S]), sb("w0_out_v", [S + V, V])
        e.wfc1, e.wfc2, e.wrbf = sb("w_fc1", [12, 100]), sb("w_fc2", [100, 192]), sb("w_rbf", [16, 224])
        e.walval, e.wvval, e.wg = sb("w_alpha_val", [S + V, 2 * S]), sb("w_val_v", [P, V]), sb("w_gate", [P, 3 * V])
        e.adcol, e.ad4, e.ad = sb("alpha_dot", [S, 1]), sb("alpha_dot_heads", [S, H]), sb("alpha_dot_spread", [S, H, P])
        e.gamma_s, e.beta_s, e.gamma_v = sb("gamma_s", [P, S]), sb("beta_s", [P, S]), sb("gamma_v", [P, 3 * V])
        e.mvs0, e.mvs1, e.mvv = sb("value_s_s", [P, S]), sb("value_s_v", [P, V]), sb("value_v", [3 * V, 4 * D])
        e.w2s, e.vl, e.w2v = sb("w2_s", [P, 2]), sb("vlin_v", [3 * V, 2 * S]), sb("w2_v", [3 * V, 3])

        weight_phase(nc, e)
        unique_phase(nc, e)
        node_phase(nc, e, "n0", "x", "radial", ins["x_rows"], base[0], None, e.w0, [tab0])
        edge_phase(nc, e, "e0", "radial", macros, e.src, e.dst_rows, e.dst, e.dst_u, [tab0], e.acc["acc0"])
        node_phase(nc, e, "n1", "radial", "attention", base[0], base[1], None, e.w1, [e.tab_src, e.tab_dst])
        attention_phase(nc, e, macros)
        node_phase(nc, e, "n2", "attention", "linear", base[1], base[2], e.w1o, e.w2, [tab2])
        edge_phase(nc, e, "e2", "linear", macros, e.src, e.dst_rows, e.dst, e.dst_u, [tab2], e.acc["acc2"])
        node_phase(nc, e, "n3", "linear", "bilinear_next", base[2], base[3], e.w2o, e.w3, [tab3])
        edge_phase(nc, e, "e3", "messages", macros, e.dst, e.src_rows, e.src, e.src_u, [tab3], e.acc["acc3"])
        e.wuss, e.wuvv = sb("wu_ss", [P, 32, S]), sb("wu_vv", [P, 8, S])
        e.wusv, e.wuvs = sb("wu_sv", [P, 16, V]), sb("wu_vs", [P, 16, V])
        bilinear_weight_phase(nc, e)
        node_phase(nc, e, "n4", "bilinear", None, base[3], out, e.w3l, None, [])


_WEIGHTS = [
    "L0_gnn_W_sc0", "L0_gnn_W_sc1", "L0_gnn_W_l1_0", "L0_gnn_W_l1_1", "L0_gnn_W_fc1", "L0_gnn_W_fc2",
    "L0_gnn_W_l2_0", "L0_gnn_W_l2_1", "L1_gnn_gamma_s", "L1_gnn_beta_s", "L1_gnn_gamma_v", "L1_gnn_Ws_src",
    "L1_gnn_Wv_src", "L1_gnn_Ws_dst", "L1_gnn_Wv_dst", "L1_gnn_W_rbf", "L1_gnn_W_alpha", "L1_gnn_alpha_dot",
    "L1_gnn_Ws_val", "L1_gnn_Wv_val", "L1_gnn_Wg", "L1_gnn_w2_ss", "L1_gnn_w2_sv", "L1_gnn_w2_vs",
    "L1_gnn_w2_vv0", "L1_gnn_w2_vv1", "L1_gnn_Ws_vlin", "L1_gnn_Wv_vlin", "L1_gnn_Wps", "L1_gnn_Wpv",
    "L2_gnn_W1", "L2_gnn_W2", "L2_gnn_W3", "L2_gnn_W4", "L2_gnn_W5", "L2_gnn_Ws", "L2_gnn_Wv", "L3_gnn_Wm_ss",
    "L3_gnn_Wm_vv", "L3_gnn_Wm_sv", "L3_gnn_Wm_vs", "L3_gnn_Lm_s", "L3_gnn_Lm_v", "L3_gnn_Wu_ss",
    "L3_gnn_Wu_vv", "L3_gnn_Wu_sv", "L3_gnn_Wu_vs", "L3_gnn_Lu_s", "L3_gnn_Lu_v"]


def _layout(inputs):
    import numpy as np

    a = {k: np.asarray(v) for k, v in inputs.items()}
    n, n_edges = a["x"].shape[0], a["src"].shape[0]
    nodes = -(-(n + 1) // (NB * P)) * NB * P
    edges = -(-n_edges // (2 * G * P)) * 2 * G * P
    tiles = edges // P
    arrays = {k: np.ascontiguousarray(a[k]) for k in _WEIGHTS}
    x = np.concatenate([a["x"][:, :S], a["x"][:, S:].reshape(n, V, 3).transpose(0, 2, 1).reshape(n, 3 * V)], axis=1)
    arrays["x_rows"] = np.pad(x, ((0, nodes - n), (0, 0)))
    z = np.pad(a["node_vec1"][:, 0], (0, nodes - n))
    arrays["z_cols"] = np.ascontiguousarray(z.reshape(nodes // P, P).T)
    for name in ("src", "dst"):
        ids = np.pad(a[name], (0, edges - n_edges), constant_values=n)
        arrays[name + "_cols"] = np.ascontiguousarray(ids.reshape(tiles, P).T)
        arrays[name + "_rows"] = ids.reshape(tiles // G, G * P)
    attr = np.pad(a["edge_attr_4"], ((0, edges - n_edges), (0, 0)))
    arrays["attr_cols"] = np.ascontiguousarray(attr.reshape(tiles, P, 4).transpose(1, 0, 2))
    for k in (12, 16):
        f = np.pad(a[f"edge_attr_{k}"], ((0, edges - n_edges), (0, 0)))
        arrays[f"features_{k}"] = np.ascontiguousarray(f.T)
    return n, nodes, arrays


def kernel(**inputs):
    import numpy as np
    import concourse.bacc as bacc
    from concourse.bass_utils import run_bass_kernel_spmd

    n, nodes, arrays = _layout(inputs)
    nc = bacc.Bacc("TRN2", target_bir_lowering=False, num_devices=1)
    aps = {name: nc.dram_tensor(name, list(a.shape), mybir.dt.from_np(a.dtype), kind="ExternalInput").ap()
           for name, a in arrays.items()}
    out = nc.dram_tensor("out_rows", [nodes, D], FP, kind="ExternalOutput").ap()
    gnn_program(nc, aps, out)
    r = run_bass_kernel_spmd(nc, [arrays], core_ids=[0]).results[0]["out_rows"]
    r = np.asarray(r)[:n]
    return np.concatenate([r[:, :S], r[:, S:].reshape(n, 3, V).transpose(0, 2, 1).reshape(n, 3 * V)], axis=1)
```

```python
from contextlib import ExitStack

import concourse.bass as bass
from concourse import mybir
from concourse.alu_op_type import AluOpType as ALU

FP = mybir.dt.float32
BF = mybir.dt.bfloat16
I32 = mybir.dt.int32
ACT = mybir.ActivationFunctionType
AX = mybir.AxisListType.X

P = 128
G = 4
S, V = 64, 32
D = S + 3 * V
NB = 7
H, HA, HV = 4, 16, 8
HW = HA + 3 * HV
DIRECTION = ((2 * D, 0, V, 0), (2 * D + S + V, V, 0, S), (2 * D + 2 * (S + V), V, 0, S + V))
W3 = 2 * D + 3 * (S + V) + V
NO_SCORE = -3.0e38
C3, C6 = 3.0 ** -0.5, 6.0 ** -0.5
C32 = V ** -0.5


def vcol(c):
    return S + V * (c % 3)


def spread(ap, axis, n):
    ap = ap.unsqueeze(axis)
    shape = list(ap.shape)
    shape[axis] = n
    return ap.broadcast_to(shape)


def after(eng, sem, value):
    if isinstance(value, int) and value <= 0:
        return
    eng.wait_ge(sem, value)


class Env:
    pass



def table_clears(e, names):
    per = e.NR // P
    clears = []
    for name in names:
        for acc in e.acc[name]:
            flat, width = acc.rearrange("(p r) w -> p r w", p=P), acc.shape[1]
            for r in range(0, per, 10):
                n = min(10, per - r)
                clears.append((flat[:, r:r + n, :], e.empty[:, 0:n, :] if name == "state" else
                               e.zeros[:, 0:n * width].rearrange("p (r w) -> p r w", r=n)))
    return clears


def weight_phase(nc, e):
    w = e.ins
    T, NT = e.T, e.NT
    loads, scales = [], []

    def rows_of_vector(t, c):
        return (t[0][S:S + V], t[0][S + V:P], t[1][0:V])[c % 3]

    def place_s(t, col, name):
        ap = w[name]
        loads.append((t[0][0:S, col:col + ap.shape[1]], ap))

    def place_v(t, c, col, name):
        ap = w[name]
        loads.append((rows_of_vector(t, c)[:, col:col + ap.shape[1]], ap))

    def place_linear(t, col, ws, wv, cs, cv):
        place_s(t, col, ws)
        for c in range(3):
            place_v(t, c, col + vcol(c), wv)
        scale_cols(t, col, col + S, cs)
        scale_cols(t, col + S, col + D, cv)

    def scale_cols(t, a, b, by):
        if by != 1.0:
            scales.append((t[0][:, a:b], by))
            scales.append((t[1][:, a:b], by))

    import math
    sin8, cos8 = math.sin(math.pi / 8), math.cos(math.pi / 8)
    place_linear(e.w0, 0, "L0_gnn_W_l1_0", "L0_gnn_W_l1_1", S ** -0.5, C32)
    place_linear(e.w0, D, "L0_gnn_W_sc0", "L0_gnn_W_sc1", sin8 * S ** -0.5, sin8 * C32)
    place_linear(e.w1, 0, "L1_gnn_Ws_src", "L1_gnn_Wv_src", 1.0, 1.0)
    place_linear(e.w1, D, "L1_gnn_Ws_dst", "L1_gnn_Wv_dst", 1.0, 1.0)
    c0, c1 = (S + V) ** -0.5, (3.0 / (S + 2 * V)) ** 0.5
    place_linear(e.w2, 0, "L2_gnn_W1", "L2_gnn_W4", c0, c1 * C3)
    for c in range(3):
        off = D * (c + 1)
        place_v(e.w2, c, off, "L2_gnn_W2")
        scale_cols(e.w2, off, off + S, c0 * C3)
        place_s(e.w2, off + vcol(c), "L2_gnn_W3")
        scale_cols(e.w2, off + vcol(c), off + vcol(c) + V, c1 * C3)
        place_v(e.w2, (c + 2) % 3, off + vcol(c + 1), "L2_gnn_W5")
        scale_cols(e.w2, off + vcol(c + 1), off + vcol(c + 1) + V, c1 * C6)
        place_v(e.w2, (c + 1) % 3, off + vcol(c + 2), "L2_gnn_W5")
        scale_cols(e.w2, off + vcol(c + 2), off + vcol(c + 2) + V, -c1 * C6)
    for off, ws, wv in ((0, "L3_gnn_Lm_s", "L3_gnn_Lm_v"), (D, "L3_gnn_Wm_ss", "L3_gnn_Wm_vs")):
        place_s(e.w3, off + V, ws)
        scale_cols(e.w3, off + V, off + V + S, S ** -0.5)
        for c, col in enumerate((0, S + V, S + 2 * V)):
            place_v(e.w3, c, off + col, wv)
            scale_cols(e.w3, off + col, off + col + V, C32)
    for c, (a, _, scalars, vectors) in enumerate(DIRECTION):
        place_v(e.w3, c, a + scalars, "L3_gnn_Wm_vv")
        scale_cols(e.w3, a + scalars, a + scalars + S, C3 * C32)
        place_s(e.w3, a + vectors, "L3_gnn_Wm_sv")
        scale_cols(e.w3, a + vectors, a + vectors + V, S ** -0.5)
    place_linear(e.w2o, 0, "L2_gnn_Ws", "L2_gnn_Wv", S ** -0.5, C32)
    place_linear(e.w3l, 0, "L3_gnn_Lu_s", "L3_gnn_Lu_v", S ** -0.5, C32)
    out0 = cos8 * 8.0 ** -0.5 * (S + V) ** -0.5
    loads.append((e.w0s[:, :], w["L0_gnn_W_l2_0"]))
    loads.append((e.w0v[:, :], w["L0_gnn_W_l2_1"]))
    scales.append((e.w0s[:, :], out0))
    scales.append((e.w0v[:, :], out0))
    for h in range(H):
        t, r = e.w1o[h // 2], HW * (h % 2)
        loads.append((t[r:r + HA, 0:S], w["L1_gnn_Wps"][HA * h:HA * h + HA, :]))
        for c in range(3):
            a = r + HA + HV * c
            loads.append((t[a:a + HV, vcol(c):vcol(c) + V], w["L1_gnn_Wpv"][HV * h:HV * h + HV, :]))
    loads.append((e.wfc1[:, :], w["L0_gnn_W_fc1"]))
    loads.append((e.wfc2[:, :], w["L0_gnn_W_fc2"]))
    scales.append((e.wfc2[:, 0:2 * S + V], 100.0 ** -0.5))
    scales.append((e.wfc2[:, 2 * S + V:], 100.0 ** -0.5 * C3))
    loads.append((e.wrbf[:, :], w["L1_gnn_W_rbf"]))
    scales.append((e.wrbf[:, 2 * S + V:2 * S + 2 * V], C3))
    scales.append((e.wrbf[:, 2 * S + 2 * V:], 2.0 ** -0.5))
    loads.append((e.walval[:, 0:S], w["L1_gnn_W_alpha"]))
    loads.append((e.walval[:, S:2 * S], w["L1_gnn_Ws_val"]))
    loads.append((e.wvval[:, :], w["L1_gnn_Wv_val"]))
    for c in range(3):
        loads.append((e.wg[S:P, V * c:V * c + V], w["L1_gnn_Wg"]))
    loads.append((e.adcol[:, :], w["L1_gnn_alpha_dot"].rearrange("o h a -> (h a) o")))
    for name, t in (("L1_gnn_gamma_s", e.gamma_s), ("L1_gnn_beta_s", e.beta_s)):
        loads.append((t[:, :], spread(w[name], 0, P)))
    for c in range(3):
        loads.append((e.gamma_v[:, V * c:V * c + V], spread(w["L1_gnn_gamma_v"], 0, P)))
    loads.append((e.mvs[S:P, 0:V], w["L1_gnn_Wv_vlin"][0:S, :]))
    loads.append((e.mvs[S:P, V:], w["L1_gnn_Ws_vlin"][0:S, :]))
    loads.append((e.w2s[S:P, 0:1], w["L1_gnn_w2_ss"].unsqueeze(1)))
    loads.append((e.w2s[S:P, 1:2], w["L1_gnn_w2_sv"].unsqueeze(1)))
    for c in range(3):
        r = slice(V * c, V * c + V)
        loads.append((e.vl[r, 0:S], w["L1_gnn_Ws_vlin"][S:S + V, :]))
        loads.append((e.vl[r, S:S + V], w["L1_gnn_Wv_vlin"][S:S + V, :]))
        loads.append((e.vl[r, S + V:S + 2 * V], w["L1_gnn_Wv_vlin"][S + V:S + 2 * V, :]))
        for k, name in enumerate(("L1_gnn_w2_vv0", "L1_gnn_w2_vs", "L1_gnn_w2_vv1")):
            loads.append((e.w2v[r, k:k + 1], w[name].unsqueeze(1)))
    for t, name in ((e.src, "src_cols"), (e.dst, "dst_cols"), (e.y, "attr_cols"), (e.z, "z_cols")):
        loads.append((t[:], w[name]))

    with ExitStack() as ctx:
        zeros, empty = e.zeros, e.empty
        hsel = ctx.enter_context(nc.sbuf_tensor("head_of_row", [S, H], FP))
        cleared = ctx.enter_context(nc.semaphore("weights_cleared"))
        loaded = ctx.enter_context(nc.semaphore("weights_loaded"))
        tables = ctx.enter_context(nc.semaphore("accumulators_cleared"))
        masks = ctx.enter_context(nc.semaphore("masks_made"))
        scaled = ctx.enter_context(nc.semaphore("weights_scaled"))
        block = ctx.enter_context(nc.Block())
        clears = table_clears(e, ("acc0",))

        @block.sync
        def _(sp):
            sp.wait_ge(cleared, 1)
            with nc.allow_non_contiguous_dma(reason="small weight columns"):
                for to, of in loads:
                    sp.dma_start(to, of).then_inc(loaded, 16)
            sp.wait_ge(loaded, 16 * len(loads))

        @block.scalar
        def _(act):
            act.wait_ge(cleared, 1)
            for to, of in clears:
                act.dma_start(to, of).then_inc(tables, 16)
            act.wait_ge(tables, 16 * len(clears))

        @block.gpsimd
        def _(pool):
            nc.gpsimd.memset(e.ident[:, :], 0.0)
            nc.gpsimd.memset(e.earlier[:, :], 1.0)
            nc.gpsimd.memset(hsel[:, :], 1.0).then_inc(masks, 1)
            pool.wait_ge(masks, 1)
            nc.gpsimd.affine_select(out=e.ident[:, :], in_=e.ident[:, :], compare_op=ALU.not_equal, fill=1.0,
                                    base=0, pattern=[[-1, P]], channel_multiplier=1)
            nc.gpsimd.affine_select(out=e.earlier[:, :], in_=e.earlier[:, :], compare_op=ALU.is_gt, fill=0.0,
                                    base=0, pattern=[[-1, P]], channel_multiplier=1)
            nc.gpsimd.iota(e.spare_i[:, :], pattern=[[0, 1]], base=e.NP, channel_multiplier=1)
            nc.gpsimd.affine_select(out=hsel[:, :], in_=hsel[:, :], compare_op=ALU.is_ge, fill=0.0,
                                    base=0, pattern=[[-HA, H]], channel_multiplier=1).then_inc(masks, 1)
            pool.wait_ge(masks, 2)
            nc.gpsimd.affine_select(out=hsel[:, :], in_=hsel[:, :], compare_op=ALU.is_ge, fill=0.0,
                                    base=HA - 1, pattern=[[HA, H]], channel_multiplier=-1).then_inc(masks, 1)

        @block.vector
        def _(dve):
            for t in (e.w0, e.w1, e.w2, e.w3, e.w2o, e.w3l, e.w1o):
                for part in t:
                    nc.vector.memset(part[:, :], 0.0)
            nc.vector.memset(e.mvv[:, :], 0.0)
            nc.vector.memset(zeros[:, :], 0.0)
            nc.vector.memset(empty[:, :, 0:H * (HW + 1)], 0.0)
            nc.vector.memset(empty[:, :, H * (HW + 1):], NO_SCORE).then_inc(cleared, 1)
            dve.wait_ge(loaded, 16 * len(loads))
            dve.wait_ge(masks, 3)
            for ap, by in scales:
                nc.vector.tensor_scalar(ap, ap, by, None, ALU.mult)
            nc.vector.tensor_copy(e.ident_bf[:, :], e.ident[:, :])
            nc.vector.tensor_copy(e.spare[:, :], e.spare_i[:, :])
            nc.vector.tensor_scalar(e.ad4[:, :], hsel[:, :], e.adcol[:, 0:1], None, ALU.mult)
            nc.vector.tensor_scalar(e.mvs[S:P, V:], e.mvs[S:P, V:], e.w2s[S:P, 0:1], 0.5, ALU.mult, ALU.mult)
            nc.vector.tensor_scalar(e.mvs[S:P, 0:V], e.mvs[S:P, 0:V], e.w2s[S:P, 1:2], 0.5, ALU.mult, ALU.mult)
            nc.vector.tensor_scalar(e.vl[:, 0:S], e.vl[:, 0:S], e.w2v[:, 0:1], 0.5 * C3, ALU.mult, ALU.mult)
            nc.vector.tensor_scalar(e.vl[:, S:S + V], e.vl[:, S:S + V], e.w2v[:, 1:2], 0.5, ALU.mult, ALU.mult)
            nc.vector.tensor_scalar(e.vl[:, S + V:], e.vl[:, S + V:], e.w2v[:, 2:3], 0.5 * 2.0 ** -0.5,
                                    ALU.mult, ALU.mult).then_inc(scaled, 1)
            dve.wait_ge(scaled, 1)
            nc.vector.tensor_copy(e.ad[:, :, :], spread(e.ad4[:, :], 2, P))
            for c in range(3):
                r = slice(V * c, V * c + V)
                nc.vector.tensor_copy(e.mvv[r, V * c:V * c + V], e.vl[r, S:S + V])
                nc.vector.tensor_copy(e.mvv[r, 3 * V + S * c:3 * V + S * c + S], e.vl[r, 0:S])
                nc.vector.tensor_copy(e.mvv[r, 9 * V + V * c:9 * V + V * c + V], e.vl[r, S + V:])


def bilinear_weight_phase(nc, e):
    w = e.ins
    loads, scales = [], []
    for name, t, by in (("L3_gnn_Wu_ss", e.wuss, 1.0 / 64), ("L3_gnn_Wu_vv", e.wuvv, C3 / 32)):
        flat = w[name].rearrange("u v w -> (u v) w")
        for c in range(t.shape[1]):
            loads.append((t[:, c, :], flat[P * c:P * c + P, :]))
        scales.append((t[:, :, :], by))
    loads.append((e.wusv[:, :], w["L3_gnn_Wu_sv"].rearrange("u v w -> u (v w)")))
    loads.append((e.wuvs[:, :].rearrange("v (u w) -> v u w", u=V), w["L3_gnn_Wu_vs"].rearrange("u v w -> v u w")))
    scales += [(e.wusv[:, :], 2048.0 ** -0.5), (e.wuvs[:, :], 2048.0 ** -0.5)]
    with ExitStack() as ctx:
        loaded = ctx.enter_context(nc.semaphore("bilinear_loaded"))
        block = ctx.enter_context(nc.Block())

        @block.sync
        def _(sp):
            for to, of in loads:
                sp.dma_start(to, of).then_inc(loaded, 16)
            sp.wait_ge(loaded, 16 * len(loads))

        @block.vector
        def _(dve):
            dve.wait_ge(loaded, 16 * len(loads))
            for ap, by in scales:
                nc.vector.tensor_scalar(ap, ap, by, None, ALU.mult)



def node_phase(nc, e, tag, kind_in, kind_out, base_in, base_out, w_in, w_out, tables_out):
    steps = e.NT // NB
    M_out = w_out[0].shape[-1] if w_out else 0
    in_w, in_n = {"x": (D, 0), "radial": (384, G), "attention": (168, 2 * G), "linear": (D, G),
                  "bilinear": (D, G)}[kind_in]
    accs = {"x": [], "radial": e.acc["acc0"], "attention": e.acc["state"], "linear": e.acc["acc2"],
            "bilinear": e.acc["acc3"]}[kind_in]

    with ExitStack() as ctx:
        def sb(name, shape, dt=FP):
            return ctx.enter_context(nc.sbuf_tensor(f"{tag}_{name}", shape, dt))

        def ps(name):
            return ctx.enter_context(nc.psum_tensor(f"{tag}_{name}", [P, 512], FP))

        def sem(name):
            return ctx.enter_context(nc.semaphore(f"{tag}_{name}"))

        x = sb("x", [P, NB, D])
        h = sb("h", [P, NB, D])
        sq = sb("sq", [P, NB, D])
        st = sb("st", [P, 8, NB])
        base = sb("base", [P, NB, D])
        acc = [sb(f"acc{k}", [P, NB, in_w]) for k in range(in_n)]
        tile_in = sb("in_T", [P, 2, 512])
        tile_out = sb("out_T", [P, 2, 384])
        tab = sb("tab", [P, NB, max(M_out, D)])
        ht = [ps(f"hT{k}") for k in range(2)]
        om = [ps(f"om{k}") for k in range(4)]
        loaded, made, stored = sem("loaded"), sem("made"), sem("stored")
        chain, base_loaded = sem("chain"), sem("base_loaded")
        if kind_in == "x":
            tables_cleared = sem("later_tables_cleared")
        if kind_in != "x":
            agg_ready, agg_E, agg_M = sem("agg_ready"), sem("agg_T_ready"), sem("agg_multiplied")
        if kind_in not in ("x", "bilinear"):
            agg_T, agg_O = sem("agg_transposed"), sem("agg_read")
        h_T, h_E, h_M = sem("h_transposed"), sem("h_T_ready"), sem("h_multiplied")
        if kind_in != "bilinear":
            h_ready, h_O, var_ready, std_ready = sem("h_ready"), sem("h_read"), sem("var_ready"), sem("std_ready")
        if kind_in == "bilinear":
            hin = sb("hin", [P, NB, D])
            outer = sb("outer", [P, 2, 4096])
            outer_t = sb("outer_T", [P, 4, 512])
            pt = [ps(f"pt{k}") for k in range(2)]
            o_made, o_E, o_done = (sem(f"outer_{s}") for s in ("made", "transposed", "added"))
            forms = [([0], [0], S, S, e.wuss, 0, S),
                     ([vcol(c) for c in range(3)], [vcol(c) for c in range(3)], V, V, e.wuvv, 0, S)]
            halves = V // 2
            terms = sb("vector_terms", [P, 3, 2 * V, V])
            vec_sum = sb("vector_sums", [P, 3, V])
            T_made, T_read = sem("T_made"), sem("T_read")
            ends = []
            for form in forms:
                ends.append((ends[-1] if ends else 0) + form[2] * form[3] // (4 * P))
            GROUPS = ends[-1]
        block = ctx.enter_context(nc.Block())

        def each_step(eng, body):
            body(0)
            if steps > 1:
                with eng.Fori(1, steps) as j:
                    body(j)

        def rows(ap, j):
            return ap.rearrange("(t p) w -> p t w", p=P)[:, bass.ds(NB * j, NB), :]

        chunks_in = {"radial": [(96 * c, 96) for c in range(4)], "attention": [(0, 80), (80, 80)],
                     "linear": [(0, P), (P, V)]}.get(kind_in, [])
        n_std = {"x": 1, "radial": 3, "attention": 2, "linear": 1, "bilinear": 0}[kind_in]
        n_loads = in_n + (kind_in == "bilinear")
        stores = (1 if base_out is not None else 0) + len(tables_out) + (kind_out == "bilinear_next")

        @block.sync
        def _(sp):
            def load_sums(j):
                for k in range(in_n):
                    sp.dma_start(acc[k][:, :, :], rows(accs[k][0:e.NP, :], j)).then_inc(loaded, 16)
                if kind_in == "bilinear":
                    sp.dma_start(hin[:, :, :], rows(e.h3, j)).then_inc(loaded, 16)

            def body(j, last):
                after(sp, made, j)
                sp.dma_start((x if kind_in == "x" else base)[:, :, :], rows(base_in, j)).then_inc(base_loaded, 16)
                if not last and chunks_in:
                    after(sp, agg_T, NB * (j + 1))
                    load_sums(j + 1)
                after(sp, made, j + 1)
                if base_out is not None:
                    sp.dma_start(rows(base_out, j), base[:, :, :]).then_inc(stored, 16)
                if kind_out == "bilinear_next":
                    sp.dma_start(rows(e.h3, j), h[:, :, :]).then_inc(stored, 16)
                at = 0
                for t in tables_out:
                    n = t.shape[1]
                    sp.dma_start(rows(t, j), tab[:, :, at:at + n]).then_inc(stored, 16)
                    at += n
                if not last and not chunks_in:
                    load_sums(j + 1)

            load_sums(0)
            if steps > 1:
                body(0, False)
            if steps > 2:
                with sp.Fori(1, steps - 1) as j:
                    body(j, False)
            body(steps - 1, True)
            after(sp, stored, 16 * stores * steps)

        @block.vector
        def _(dve):
            n_chain = [0]

            def chained(j, ins):
                n_chain[0] += 1
                ins.then_inc(chain, 1)
                after(dve, chain, per_step * j + n_chain[0])

            def body(j):
                if n_loads:
                    after(dve, loaded, 16 * n_loads * (j + 1))
                n_chain[0] = 0
                if kind_in in ("radial", "linear", "bilinear"):
                    nc.vector.tensor_tensor(acc[0][:], acc[0][:], acc[1][:], ALU.add)
                    chained(j, nc.vector.tensor_tensor(acc[2][:], acc[2][:], acc[3][:], ALU.add))
                    nc.vector.tensor_tensor(acc[0][:], acc[0][:], acc[2][:], ALU.add).then_inc(agg_ready, 1)
                if kind_in == "attention":
                    nh = H * (HW + 1)
                    mx = st[:, 0:4, :].rearrange("p a b -> p b a")
                    fk = sq[:, :, 0:8 * H].rearrange("p b (k a) -> p b k a", k=8)
                    chained(j, nc.vector.tensor_tensor(mx, acc[0][:, :, nh:], acc[1][:, :, nh:], ALU.max))
                    for k in range(2, 8):
                        chained(j, nc.vector.tensor_tensor(mx, mx, acc[k][:, :, nh:], ALU.max))
                    for k in range(8):
                        last = nc.vector.tensor_tensor(fk[:, :, k, :], acc[k][:, :, nh:], mx, ALU.subtract)
                    last.then_inc(var_ready, 1)
                    after(dve, std_ready, 2 * j + 1)
                    for k in range(8):
                        for t in range(NB):
                            a = acc[k][:, t, 0:nh].rearrange("p (h w) -> p h w", h=H)
                            last = nc.vector.tensor_tensor(a, a, spread(fk[:, t, k, :], 2, HW + 1), ALU.mult)
                    chained(j, last)
                    for w in (4, 2, 1):
                        for k in range(w):
                            last = nc.vector.tensor_tensor(acc[k][:, :, 0:nh], acc[k][:, :, 0:nh],
                                                           acc[k + w][:, :, 0:nh], ALU.add)
                        chained(j, last)
                    a0 = acc[0][:, :, 0:nh].rearrange("p b (h w) -> p b h w", h=H)
                    den = st[:, 4:8, :].rearrange("p a b -> p b a")
                    chained(j, nc.vector.tensor_scalar(den, a0[:, :, :, HW], 1e-16, None, ALU.add))
                    chained(j, nc.vector.reciprocal(den, den))
                    for t in range(NB):
                        last = nc.vector.tensor_tensor(
                            sq[:, t, :].rearrange("p (h w) -> p h w", h=H),
                            acc[0][:, t, 0:nh].rearrange("p (h w) -> p h w", h=H)[:, :, 0:HW],
                            spread(st[:, 4:8, t], 2, HW), ALU.mult)
                    last.then_inc(agg_ready, 1)
                after(dve, base_loaded, 16 * (j + 1))
                after(dve, stored, 16 * stores * j)
                if kind_in in ("radial", "attention", "linear"):
                    for t in range(NB):
                        after(dve, agg_M, NB * j + t + 1)
                        o = om[t % 2][:, 0:D]
                        if kind_in == "radial":
                            ins = nc.vector.scalar_tensor_tensor(
                                out=x[:, t, :], in0=o, scalar=e.z_of(j, t), in1=base[:, t, :],
                                op0=ALU.mult, op1=ALU.add)
                        elif kind_in == "attention":
                            ins = nc.vector.tensor_tensor(x[:, t, :], o, base[:, t, :], ALU.add)
                        else:
                            ins = nc.vector.scalar_tensor_tensor(
                                out=x[:, t, :], in0=o, scalar=0.0, in1=base[:, t, :],
                                op0=ALU.max, op1=ALU.add)
                        ins.then_inc(agg_O, 1)
                    after(dve, agg_O, NB * (j + 1))
                if kind_in == "bilinear":
                    outers(j)
                    return
                norm(j, x[:, :, :], h, 0, D, True)
                if base_out is not None and kind_out != "radial":
                    nc.vector.tensor_tensor(base[:], x[:], h[:], ALU.add)
                if kind_out == "attention":
                    norm(j, h[:, :, 0:S], sq, 1, S, False)
                    nc.vector.tensor_tensor(sq[:, :, 0:S], sq[:, :, 0:S], spread(e.gamma_s[:, :], 1, NB), ALU.mult)
                    hv = h[:, :, S:D]
                    chained(j, nc.vector.tensor_tensor(sq[:, :, S:D], hv, hv, ALU.mult))
                    chained(j, nc.vector.tensor_reduce(st[:, 0, :], sq[:, :, S:D], AX, ALU.add))
                    nc.vector.tensor_scalar(st[:, 1, :], st[:, 0, :], 1.0 / V, 1e-5, ALU.mult, ALU.add)\
                        .then_inc(var_ready, 1)
                    after(dve, std_ready, n_std * (j + 1))
                    nc.vector.tensor_tensor(sq[:, :, 0:S], sq[:, :, 0:S], spread(e.beta_s[:, :], 1, NB), ALU.add)
                    chained(j, nc.vector.reciprocal(st[:, 3, :], st[:, 2, :]))
                    chained(j, nc.vector.tensor_tensor(sq[:, :, S:D], hv, spread(st[:, 3, :], 2, 3 * V), ALU.mult))
                    nc.vector.tensor_tensor(sq[:, :, S:D], sq[:, :, S:D], spread(e.gamma_v[:, :], 1, NB), ALU.mult)\
                        .then_inc(h_ready, 1)
                for t in range(NB):
                    after(dve, h_M, NB * j + t + 1)
                    b = t % 2
                    half = M_out // 2
                    for k in range(2):
                        src = om[2 * b + k][:, 0:half]
                        dst = tab[:, t, k * half:(k + 1) * half]
                        if kind_out == "radial":
                            if k == 0:
                                ins = nc.vector.tensor_scalar(dst, src, e.z_of(j, t), None, ALU.mult)
                            else:
                                ins = nc.vector.scalar_tensor_tensor(
                                    out=base[:, t, :], in0=src, scalar=e.z_of(j, t), in1=x[:, t, :],
                                    op0=ALU.mult, op1=ALU.add)
                        else:
                            ins = nc.vector.tensor_copy(dst, src)
                    ins.then_inc(h_O, 1)
                after(dve, h_O, NB * (j + 1))
                dve.sem_inc(made, 1)

            def norm(j, src, dst, which, width, main):
                cols = slice(0, width)
                chained(j, nc.vector.tensor_reduce(st[:, 0, :], src, AX, ALU.add))
                chained(j, nc.vector.tensor_scalar(st[:, 1, :], st[:, 0, :], 1.0 / width, None, ALU.mult))
                chained(j, nc.vector.tensor_tensor(dst[:, :, cols], src, spread(st[:, 1, :], 2, width), ALU.subtract))
                tmp = tab[:, :, 0:width]
                chained(j, nc.vector.tensor_tensor(tmp, dst[:, :, cols], dst[:, :, cols], ALU.mult))
                chained(j, nc.vector.tensor_reduce(st[:, 2, :], tmp, AX, ALU.add))
                nc.vector.tensor_scalar(st[:, 1, :], st[:, 2, :], 1.0 / width, 1e-5, ALU.mult, ALU.add)\
                    .then_inc(var_ready, 1)
                first_std = 1 if kind_in == "attention" else 0
                after(dve, std_ready, n_std * j + first_std + 1 + which)
                chained(j, nc.vector.reciprocal(st[:, 3, :], st[:, 2, :]))
                chained(j, nc.vector.tensor_tensor(dst[:, :, cols], dst[:, :, cols], spread(st[:, 3, :], 2, width),
                                                   ALU.mult))
                if main:
                    ins = nc.vector.tensor_scalar(dst[:, :, cols], dst[:, :, cols], 0.0, None, ALU.max)
                    if kind_out == "attention":
                        chained(j, ins)
                    else:
                        ins.then_inc(h_ready, 1)
                        after(dve, h_ready, j + 1)

            def outers(j):
                after(dve, agg_ready, j + 1)

                def outer_product(t, k):
                    after(dve, o_E, GROUPS * (NB * j + t - 1) + ends[k] if t else GROUPS * NB * j)
                    u, v, nu, nv = forms[k][0:4]
                    o = outer[:, k, 0:nu * nv].rearrange("p (u v) -> p u v", u=nu)
                    for c in range(len(u)):
                        a = spread(hin[:, t, u[c]:u[c] + nu], 2, nv)
                        bb = spread(acc[0][:, t, v[c]:v[c] + nv], 1, nu)
                        if c == 0:
                            ins = nc.vector.tensor_tensor(o, a, bb, ALU.mult)
                        else:
                            tmp = x[:, :, :].rearrange("p b w -> p (b w)")[:, 0:nu * nv]\
                                .rearrange("p (u v) -> p u v", u=nu)
                            chained(j, ins)
                            chained(j, nc.vector.tensor_tensor(tmp, a, bb, ALU.mult))
                            ins = nc.vector.tensor_tensor(o, o, tmp, ALU.add)
                    ins.then_inc(o_made, 1)

                def contract(t, which):
                    vectors = (acc[0] if which == 0 else hin)[:, t, S:D].rearrange("p (c v) -> p c v", c=3)
                    for k in range(2):
                        after(dve, T_made, 4 * (NB * j + t) + 2 * which + k + 1)
                        T = om[2 + k][:, :].rearrange("p (v w) -> p v w", v=halves)
                        at = halves * (2 * which + k)
                        nc.vector.tensor_tensor(terms[:, :, at:at + halves, :], spread(T, 1, 3),
                                                spread(vectors[:, :, halves * k:halves * k + halves], 3, V),
                                                ALU.mult).then_inc(T_read, 1)

                def add_up(t):
                    after(dve, agg_M, GROUPS * (NB * j + t + 1))
                    nc.vector.tensor_tensor(base[:, t, :], om[t % 2][:, 0:D], base[:, t, :], ALU.add)\
                        .then_inc(o_done, 1)
                    after(dve, o_done, NB * j + t + 1)
                    chained(j, nc.vector.tensor_tensor(
                        base[:, t, S:D], base[:, t, S:D], vec_sum[:, :, :].rearrange("p c w -> p (c w)"), ALU.add))

                for t in range(NB):
                    outer_product(t, 0)
                    if t:
                        add_up(t - 1)
                    contract(t, 0)
                    outer_product(t, 1)
                    contract(t, 1)
                    after(dve, T_read, 4 * (NB * j + t + 1))
                    chained(j, nc.vector.tensor_reduce(
                        vec_sum[:, :, :], terms[:, :, :, :].rearrange("p c k w -> p c w k"), AX, ALU.add))
                add_up(NB - 1)
                after(dve, o_done, NB * (j + 1))
                dve.sem_inc(made, 1)

            per_step = {("x", "radial"): 7, ("radial", "attention"): 20, ("attention", "linear"): 20,
                        ("linear", "bilinear_next"): 8, ("bilinear", None): 1 + 6 * NB}[(kind_in, kind_out)]
            each_step(dve, body)
            assert n_chain[0] == per_step, (tag, n_chain[0], per_step)


        @block.scalar
        def _(act):
            def transposed(j, tiles, chunk_sizes, T, E, M, to):
                for t in tiles:
                    after(act, T, NB * j + t + 1)
                    after(act, M, NB * j + t - 1 if t else NB * j)
                    for c, (_, n) in enumerate(chunk_sizes):
                        last = nc.scalar.copy(to[0:n, t % 2, P * c:P * c + P], ht[t % 2][0:n, P * c:P * c + P])
                    last.then_inc(E, 1)

            def body(j):
                if kind_in == "attention":
                    after(act, var_ready, 2 * j + 1)
                    nc.scalar.activation(sq[:, :, 0:8 * H], sq[:, :, 0:8 * H], ACT.Exp).then_inc(std_ready, 1)
                if chunks_in:
                    transposed(j, range(NB), chunks_in, agg_T, agg_E, agg_M, tile_in)
                if kind_in == "bilinear":
                    x_chunks = [(0, P), (P, V), (0, S)]
                    transposed(j, [0], x_chunks, h_T, h_E, h_M, tile_out)
                    for t in range(NB):
                        transposed(j, [t + 1] if t + 1 < NB else [], x_chunks, h_T, h_E, h_M, tile_out)
                        for k in range(GROUPS):
                            q = GROUPS * t + k
                            after(act, o_E, GROUPS * NB * j + q + 1)
                            after(act, agg_M, GROUPS * NB * j + q - 3 if q >= 3 else GROUPS * NB * j)
                            nc.scalar.copy(outer_t[:, q % 4, :], pt[q % 2][:, :]).then_inc(agg_E, 1)
                else:
                    for k in range(1 if kind_in == "attention" else 0, n_std):
                        after(act, var_ready, n_std * j + k + 1)
                        nc.scalar.activation(st[:, 2, :], st[:, 1, :], ACT.Sqrt).then_inc(std_ready, 1)
                    transposed(j, range(NB), [(0, P), (P, V)], h_T, h_E, h_M, tile_out)

            if kind_in == "x":
                clears = table_clears(e, ("state", "acc2", "acc3"))
                for to, of in clears:
                    act.dma_start(to, of).then_inc(tables_cleared, 16)
            each_step(act, body)
            if kind_in == "x":
                act.wait_ge(tables_cleared, 16 * len(clears))

        @block.tensor
        def _(pe):
            def transpose(j, t, src, chunk_list, ready, T, E):
                if t == 0:
                    after(pe, ready, j + 1)
                else:
                    after(pe, E, NB * j + t - 1)
                for c, (a, n) in enumerate(chunk_list):
                    last = nc.tensor.transpose(ht[t % 2][0:n, P * c:P * c + P], src[:, t, a:a + n], e.ident[:, :])
                last.then_inc(T, 1)

            def products(j, src, chunk_list, ready, T, E, M, O, mult):
                transpose(j, 0, src, chunk_list, ready, T, E)
                for t in range(NB):
                    if t + 1 < NB:
                        transpose(j, t + 1, src, chunk_list, ready, T, E)
                    after(pe, E, NB * j + t + 1)
                    after(pe, O, NB * j + t - 1 if t else NB * j)
                    mult(t).then_inc(M, 1)

            def mult_in(t):
                o = om[t % 2]
                if kind_in == "radial":
                    nc.tensor.matmul(o[:, 0:S], tile_in[0:96, t % 2, 0:P], e.w0s[:, :], start=True, stop=True)
                    for c in range(3):
                        last = nc.tensor.matmul(o[:, vcol(c):vcol(c) + V], tile_in[0:96, t % 2, P * (c + 1):P * (c + 2)],
                                                e.w0v[:, :], start=True, stop=True)
                    return last
                n = chunks_in
                nc.tensor.matmul(o[:, 0:D], tile_in[0:n[0][1], t % 2, 0:P], w_in[0][0:n[0][1], :],
                                 start=True, stop=False)
                return nc.tensor.matmul(o[:, 0:D], tile_in[0:n[1][1], t % 2, P:2 * P], w_in[1][0:n[1][1], :],
                                        start=False, stop=True)

            def mult_out(t):
                half = M_out // 2
                for k in range(2):
                    o = om[2 * (t % 2) + k][:, 0:half]
                    nc.tensor.matmul(o, tile_out[:, t % 2, 0:P], w_out[0][:, k * half:(k + 1) * half],
                                     start=True, stop=False)
                    last = nc.tensor.matmul(o, tile_out[0:V, t % 2, P:2 * P], w_out[1][0:V, k * half:(k + 1) * half],
                                            start=False, stop=True)
                return last

            def bilinear(j):
                def transpose_both(t):
                    after(pe, agg_ready, j + 1)
                    if t:
                        after(pe, h_E, NB * j + t - 1)
                    for c, (of, a, n) in enumerate(((hin, 0, P), (hin, P, V), (acc[0], 0, S))):
                        last = nc.tensor.transpose(ht[t % 2][0:n, P * c:P * c + P], of[:, t, a:a + n], e.ident[:, :])
                    last.then_inc(h_T, 1)

                def contract(t, which):
                    scalars = tile_out[0:S, t % 2, 2 * P * which:2 * P * which + P]
                    weights = e.wuvs if which else e.wusv
                    for k in range(2):
                        after(pe, T_read, 4 * (NB * j + t) + 2 * which + k - 1 if t or which else 4 * NB * j)
                        nc.tensor.matmul(om[2 + k][:, :], scalars, weights[:, 512 * k:512 * k + 512],
                                         start=True, stop=True).then_inc(T_made, 1)

                transpose_both(0)
                for t in range(NB):
                    if t + 1 < NB:
                        transpose_both(t + 1)
                    after(pe, h_E, NB * j + t + 1)
                    after(pe, o_done, NB * j + t - 1 if t else NB * j)
                    o = om[t % 2]
                    nc.tensor.matmul(o[:, 0:D], tile_out[:, t % 2, 0:P], w_in[0][:, :], start=True, stop=False)
                    nc.tensor.matmul(o[:, 0:D], tile_out[0:V, t % 2, P:2 * P], w_in[1][0:V, :],
                                     start=False, stop=False).then_inc(h_M, 1)
                    pending = []
                    group = 0

                    def multiply(pend):
                        q, first, form, n, is_last = pend
                        after(pe, agg_E, GROUPS * NB * j + q + 1)
                        wt, col, width = form[4], form[5], form[6]
                        for c in range(n):
                            done = nc.tensor.matmul(o[:, col:col + width], outer_t[:, q % 4, P * c:P * c + P],
                                                    wt[:, first + c, :], start=False,
                                                    stop=is_last and c == n - 1)
                        done.then_inc(agg_M, 1)

                    for k, form in enumerate(forms):
                        contract(t, k)
                        n_chunks = form[2] * form[3] // P
                        for first in range(0, n_chunks, 4):
                            q = GROUPS * t + group
                            if first == 0:
                                after(pe, o_made, len(forms) * (NB * j + t) + k + 1)
                            after(pe, agg_E, GROUPS * NB * j + q - 1 if q >= 1 else GROUPS * NB * j)
                            for c in range(4):
                                ins = nc.tensor.transpose(pt[q % 2][:, P * c:P * c + P],
                                                          outer[:, k % 2, P * (first + c):P * (first + c + 1)],
                                                          e.ident[:, :])
                            ins.then_inc(o_E, 1)
                            pending.append((q, first, form, 4, group == GROUPS - 1))
                            if len(pending) > 1:
                                multiply(pending.pop(0))
                            group += 1
                    multiply(pending.pop(0))

            def body(j):
                if chunks_in and kind_in != "bilinear":
                    src = sq if kind_in == "attention" else acc[0]
                    products(j, src, chunks_in, agg_ready, agg_T, agg_E, agg_M, agg_O, mult_in)
                if kind_in == "bilinear":
                    bilinear(j)
                else:
                    src = sq if kind_out == "attention" else h
                    products(j, src, [(0, P), (P, V)], h_ready, h_T, h_E, h_M, h_O, mult_out)

            each_step(pe, body)



U = 4


def pipeline(eng, macros, *stages, depth=U):
    def slot(m, i=None):
        for ahead, f in stages:
            if i is not None:
                f((m + ahead) % depth, i + (m + ahead) // depth)
            elif 0 <= m + ahead < macros:
                f((m + ahead) % depth, (m + ahead) // depth)

    aheads = [ahead for ahead, _ in stages]
    for m in range(-max(aheads), depth):
        slot(m)
    with eng.Fori(1, macros // depth - 1) as i:
        for m in range(depth):
            slot(m, i)
    for m in range(macros - depth, macros - min(0, min(aheads))):
        slot(m)


def edge_semaphores(nc, ctx):
    def sem(name):
        return ctx.enter_context(nc.semaphore(f"edges_{name}"))

    s = Env()
    s.row_loaded = [sem(f"row_loaded{b}") for b in range(2)]
    s.ef_loaded = [sem(f"features_loaded{b}") for b in range(2)]
    s.gathered = [sem(f"gathered{b}") for b in range(U)]
    s.scattered = [sem(f"scattered_{layer}") for layer in (0, 2, 3)]
    s.pool_passed, s.staged = sem("pool_passed"), sem("staged")
    s.eq_ready, s.eq_used, s.sums_ready = sem("eq_ready"), sem("eq_used"), sem("sums_ready")
    s.h_lin, s.h_act, s.w_ready = sem("hidden_linear"), sem("hidden_ready"), sem("w_ready")
    s.mid_chain, s.mid_ready, s.unique_chain = sem("message_chain"), sem("mid_ready"), sem("unique_chain")
    return s


def edge_phase(nc, e, tag, kind, nth, macros, gather_ids, row_ids, own_ids, unique_ids, table, accs):
    radial = kind == "radial"
    terms = {"radial": [None], "linear": [0, 1, 2, 3], "messages": [None, 0, 1, 2]}[kind]
    K = len(terms)
    W = table.shape[1]
    AW = accs[0].shape[1]
    banks = 4 if radial else 2
    per_bank = G // banks
    done = nth * macros
    done_mid = 0 if radial else macros
    sem = e.edge_sem
    scattered = sem.scattered[nth]

    def count(b, i):
        return U * i + (b + done)

    def count_mid(b, i):
        return U * i + (b + done_mid)

    def in_buffer(b, i):
        return i + done // U, (U // 2) * i + (b // 2 + done // 2)

    with ExitStack() as ctx:
        def sb(name, shape, dt=FP):
            return ctx.enter_context(nc.sbuf_tensor(f"{tag}_{name}", shape, dt))

        def ps(name, cols=512):
            return ctx.enter_context(nc.psum_tensor(f"{tag}_{name}", [P, cols], FP))

        row = sb("row", [P, 2, G * P], I32)
        idf = sb("ids", [P, U, G])
        y = sb("y", [P, U, G, 4])
        gidx = sb("gather_idx", [P, U, G], I32)
        uidx = sb("scatter_idx", [P, U, G], I32)
        eq = sb("same_node", [P, 2, G, K, P])
        same_earlier = sb("same_earlier", [P, G, P])
        count_earlier, to_spare = sb("count_earlier", [P, G]), sb("to_spare", [P, G])
        rows_g = sb("gathered", [P, U, G, W])
        sums = sb("sums", [P, 2, G, AW])
        acc = [[ps(f"acc{b}_{k}") for k in range(banks)] for b in range(1 if radial else 2)]
        if kind != "linear":
            mid = sb("messages", [P, 2, G, AW])
        if radial:
            ef = sb("features", [12, 2, G * P])
            act_h = sb("hidden", [100, 2, G * P])
            ws, wv2, wv3 = sb("weighted_s", [P, G, 2, S]), sb("weighted_v", [P, G, 3, V]), sb("dot_v", [P, G, 3, V])
            dots = sb("dot_terms", [P, G, 3, V])
            ph = [ps(f"hidden{b}") for b in range(2)]
            pw = ps("weights", 1024)
        block = ctx.enter_context(nc.Block())

        @block.sync
        def _(sp):
            def load(b, i):
                n = count(b, i)
                after(sp, sem.eq_ready, n - 1)
                sp.dma_start(row[:, b % 2, :], row_ids[bass.ds(U * i + b, 1), :].broadcast_to([P, G * P]))\
                    .then_inc(sem.row_loaded[b % 2], 16)
                if radial:
                    after(sp, sem.h_lin, n - 1)
                    sp.dma_start(ef[:, b % 2, :], e.ins["features_12"][:, bass.ds((U * i + b) * (G * P), G * P)])\
                        .then_inc(sem.ef_loaded[b % 2], 16)

            pipeline(sp, macros, (3, load))

        @block.gpsimd
        def _(pool):
            def passed():
                pool.sem_inc(sem.pool_passed, 1)

            def gather(b, i):
                n = count(b, i)
                pool.wait_ge(sem.staged, n + 1)
                passed()
                if radial:
                    after(pool, sem.mid_ready, n - U + 1)
                else:
                    after(pool, sem.eq_used, n - U + 1)
                passed()
                for g in range(G):
                    pool.indirect_dma_start(
                        out=rows_g[:, b, g, :], out_offset=None, in_=table[:, :],
                        in_offset=bass.IndirectOffsetOnAxis(ap=gidx[:, b, g:g + 1], axis=0))\
                        .then_inc(sem.gathered[b], 16)

            def scatter(b, i):
                n = count(b, i)
                pool.wait_ge(sem.sums_ready, n + 1)
                passed()
                after(pool, scattered, 16 * G * (U * i + b))
                passed()
                for g in range(G):
                    pool.indirect_dma_start(
                        out=accs[g][:, :], out_offset=bass.IndirectOffsetOnAxis(ap=uidx[:, b, g:g + 1], axis=0),
                        in_=sums[:, b % 2, g, :], in_offset=None, compute_op=ALU.add).then_inc(scattered, 16)

            pipeline(pool, macros, (2, gather), (0, scatter))
            pool.wait_ge(scattered, 16 * G * macros)

        @block.vector
        def _(dve):
            def stage(b, i):
                n, (q, _) = count(b, i), in_buffer(b, i)
                after(dve, sem.gathered[b], 16 * G * q)
                after(dve, sem.eq_ready, n - U + 1)
                if kind != "linear":
                    after(dve, sem.mid_ready, count_mid(b, i) - U + 1)
                cols = bass.ds((U * i + b) * G, G)
                nc.vector.tensor_copy(gidx[:, b, :], gather_ids[:, cols])
                nc.vector.tensor_copy(idf[:, b, :], own_ids[:, cols])
                nc.vector.tensor_copy(y[:, b, :, :], e.y[:, cols, :]).then_inc(sem.staged, 1)

            def compare(b, i):
                n, (_, q2) = count(b, i), in_buffer(b, i)
                after(dve, scattered, 16 * G * (U * i + (b - U + 1)))
                cols = bass.ds((U * i + b) * G, G)
                if kind == "linear":
                    nc.vector.tensor_copy(uidx[:, b, :], unique_ids[:, cols])
                dve.wait_ge(sem.staged, n + 1)
                dve.wait_ge(sem.row_loaded[b % 2], 16 * (q2 + 1))
                if kind != "linear":
                    k = count_mid(b, i)
                    after(dve, sem.eq_ready, n)
                    nc.vector.tensor_scalar(to_spare[:], idf[:, b, :], -1.0, e.spare[:, 0:1], ALU.mult, ALU.add)
                    for g in range(G):
                        last = nc.vector.scalar_tensor_tensor(
                            out=same_earlier[:, g, :], in0=row[:, b % 2, g * P:(g + 1) * P], scalar=idf[:, b, g:g + 1],
                            in1=e.earlier[:, :], op0=ALU.is_equal, op1=ALU.mult, accum_out=count_earlier[:, g:g + 1])
                    last.then_inc(sem.unique_chain, 1)
                    dve.wait_ge(sem.unique_chain, 2 * k + 1)
                    nc.vector.scalar_tensor_tensor(out=to_spare[:], in0=count_earlier[:], scalar=1.0, in1=to_spare[:],
                                                   op0=ALU.min, op1=ALU.mult).then_inc(sem.unique_chain, 1)
                    dve.wait_ge(sem.unique_chain, 2 * k + 2)
                    nc.vector.tensor_tensor(uidx[:, b, :], to_spare[:], idf[:, b, :], ALU.add)
                    if unique_ids is not None:
                        nc.vector.tensor_tensor(unique_ids[:, cols], to_spare[:], idf[:, b, :], ALU.add)
                after(dve, sem.eq_used, n - 1)
                for g in range(G):
                    same = row[:, b % 2, g * P:(g + 1) * P]
                    for k, c in enumerate(terms):
                        if c is None:
                            last = nc.vector.tensor_scalar(eq[:, b % 2, g, k, :], same, idf[:, b, g:g + 1], None,
                                                           ALU.is_equal)
                        else:
                            last = nc.vector.tensor_scalar(eq[:, b % 2, g, k, :], same, idf[:, b, g:g + 1],
                                                           y[:, b, g, c:c + 1], ALU.is_equal, ALU.mult)
                last.then_inc(sem.eq_ready, 1)

            def near(b, i):
                (q, _) = in_buffer(b, i)
                dve.wait_ge(sem.gathered[b], 16 * G * (q + 1))
                for g in range(G):
                    last = nc.vector.scalar_tensor_tensor(
                        out=mid[:, b % 2, g, :], in0=rows_g[:, b, g, D:2 * D], scalar=y[:, b, g, 3:4],
                        in1=rows_g[:, b, g, 0:D], op0=ALU.mult, op1=ALU.add)
                last.then_inc(sem.mid_ready, 1)

            def messages(b, i):
                n, (q, _) = count(b, i), in_buffer(b, i)
                dve.wait_ge(sem.gathered[b], 16 * G * (q + 1))
                dve.wait_ge(sem.w_ready, n + 1)
                after(dve, sem.mid_ready, n)
                w = pw[:, :].rearrange("p (g w) -> p g w", g=G)
                src = rows_g[:, b, :, :]
                vec = src[:, :, S:D].rearrange("p g (c u) -> p g c u", c=3)
                nc.vector.tensor_tensor(wv3[:], spread(w[:, :, 2 * S + V:2 * S + 2 * V], 2, 3), vec, ALU.mult)
                nc.vector.tensor_tensor(ws[:], w[:, :, 0:2 * S].rearrange("p g (k s) -> p g k s", k=2),
                                        spread(src[:, :, 0:S], 2, 2), ALU.mult)
                nc.vector.tensor_tensor(wv2[:], spread(w[:, :, 2 * S:2 * S + V], 2, 3), vec, ALU.mult)\
                    .then_inc(sem.mid_chain, 1)
                dve.wait_ge(sem.mid_chain, 2 * n + 1)
                y0, y1 = y[:, b, :, 0], spread(y[:, b, :, 1:4], 3, V)
                to = mid[:, b % 2, :, :]
                vecs = to[:, :, S + V:].rearrange("p g (c w) -> p g c w", c=3)
                nc.vector.tensor_tensor(dots[:], wv3[:], y1, ALU.mult).then_inc(sem.mid_chain, 1)
                nc.vector.tensor_tensor(to[:, :, 0:S], ws[:, :, 0], spread(y0, 2, S), ALU.mult)
                nc.vector.tensor_tensor(vecs[:, :, :, 0:S], spread(ws[:, :, 1], 2, 3), spread(y[:, b, :, 1:4], 3, S),
                                        ALU.mult)
                nc.vector.tensor_tensor(vecs[:, :, :, S:], wv2[:], spread(spread(y0, 2, 3), 3, V), ALU.mult)
                dve.wait_ge(sem.mid_chain, 2 * n + 2)
                nc.vector.tensor_reduce(to[:, :, S:S + V], dots[:].rearrange("p g c u -> p g u c"), AX, ALU.add)\
                    .then_inc(sem.mid_ready, 1)

            if radial:
                pipeline(dve, macros, (3, stage), (1, compare), (1, messages))
            elif kind == "messages":
                pipeline(dve, macros, (3, stage), (1, compare), (1, near))
            else:
                pipeline(dve, macros, (3, stage), (1, compare))

        @block.scalar
        def _(act):
            def hidden(b, i):
                n = count(b, i)
                act.wait_ge(sem.h_lin, n + 1)
                after(act, sem.w_ready, n - 1)
                nc.scalar.activation(act_h[:, b % 2, :], ph[b % 2][0:100, :], ACT.Silu, scale=12.0 ** -0.5)\
                    .then_inc(sem.h_act, 1)

            def bring(b, i):
                n = count(b, i)
                act.wait_ge(sem.eq_used, n + 1)
                after(act, scattered, 16 * G * (U * i + (b - 1)))
                for k in range(banks):
                    to = sums[:, b % 2, k * per_bank:(k + 1) * per_bank, :]
                    of = acc[b % len(acc)][k][:, 0:per_bank * AW].rearrange("p (g w) -> p g w", g=per_bank)
                    if kind == "messages":
                        nc.scalar.copy(to[:, :, 0:S], of[:, :, V:V + S])
                        nc.scalar.copy(to[:, :, S:S + V], of[:, :, 0:V])
                        last = nc.scalar.copy(to[:, :, S + V:], of[:, :, S + V:])
                    else:
                        last = nc.scalar.copy(to, of)
                last.then_inc(sem.sums_ready, 1)

            if radial:
                pipeline(act, macros, (2, hidden), (0, bring))
            else:
                pipeline(act, macros, (0, bring))

        @block.tensor
        def _(pe):
            def hidden(b, i):
                n, (_, q2) = count(b, i), in_buffer(b, i)
                pe.wait_ge(sem.ef_loaded[b % 2], 16 * (q2 + 1))
                after(pe, sem.h_act, n - 1)
                nc.tensor.matmul(ph[b % 2][0:100, :], e.wfc1[:, :], ef[:, b % 2, :], start=True, stop=True)\
                    .then_inc(sem.h_lin, 1)

            def weights(b, i):
                n = count(b, i)
                pe.wait_ge(sem.h_act, n + 1)
                after(pe, sem.mid_ready, n)
                for g in range(G):
                    last = nc.tensor.matmul(pw[:, 256 * g:256 * g + 192], act_h[:, b % 2, g * P:(g + 1) * P],
                                            e.wfc2[:, :], start=True, stop=True)
                last.then_inc(sem.w_ready, 1)

            def sum_nodes(b, i):
                n, (q, _) = count(b, i), in_buffer(b, i)
                pe.wait_ge(sem.eq_ready, n + 1)
                if kind == "linear":
                    pe.wait_ge(sem.gathered[b], 16 * G * (q + 1))
                else:
                    pe.wait_ge(sem.mid_ready, count_mid(b, i) + 1)
                after(pe, sem.sums_ready, n + 1 - len(acc))
                for g in range(G):
                    o = acc[b % len(acc)][g // per_bank][:, AW * (g % per_bank):AW * (g % per_bank + 1)]
                    a = rows_g[:, b, g, :]
                    m = eq[:, b % 2, g]
                    if kind == "linear":
                        for k in range(4):
                            last = nc.tensor.matmul(o, m[:, k, :], a[:, D * k:D * k + D], start=k == 0, stop=k == 3)
                    elif kind == "messages":
                        nc.tensor.matmul(o, m[:, 0, :], mid[:, b % 2, g, :], start=True, stop=False)
                        ends = [d[0] for d in DIRECTION[1:]] + [W3]
                        for c, (off, to, _, _) in enumerate(DIRECTION):
                            last = nc.tensor.matmul(o[:, to:to + ends[c] - off], m[:, 1 + c, :], a[:, off:ends[c]],
                                                    start=False, stop=c == 2)
                    else:
                        last = nc.tensor.matmul(o, m[:, 0, :], mid[:, b % 2, g, :], start=True, stop=True)
                last.then_inc(sem.eq_used, 1)

            if radial:
                pipeline(pe, macros, (2, hidden), (1, weights), (0, sum_nodes))
            else:
                pipeline(pe, macros, (0, sum_nodes))


def attention_phase(nc, e, macros):
    SW = H * (HW + 1) + H
    NH = H * (HW + 1)
    E1 = 2 * S + 3 * V
    with ExitStack() as ctx:
        def sb(name, shape, dt=FP):
            return ctx.enter_context(nc.sbuf_tensor(f"att_{name}", shape, dt))

        def ps(name):
            return ctx.enter_context(nc.psum_tensor(f"att_{name}", [P, 512], FP))

        def sem(name):
            return ctx.enter_context(nc.semaphore(f"att_{name}"))

        row = sb("row", [P, 2, G * P], I32)
        rbf = sb("rbf", [16, 2, G * P])
        idf = sb("ids", [P, 2, G])
        y = sb("y", [P, 2, G, 6])
        sidx, didx, uidx = (sb(n, [P, 2, G], I32) for n in ("src_idx", "dst_idx", "scatter_idx"))
        ga, gb = sb("from_src", [P, 2, G, D]), sb("from_dst", [P, 2, G, D])
        msg = sb("msg", [P, G, D + 2 * V])
        xs = sb("weighted_s", [P, G, 2, S])
        vs, vv0, vv1 = sb("weighted_v", [P, G, 3, V]), sb("dot_v", [P, G, 3, V]), sb("cross_v", [P, G, 5, V])
        t1, t2, t3 = (sb(f"product{k}", [P, G, 3, V]) for k in range(3))
        dot = sb("dot", [P, G, V])
        m1s, m1v = sb("m1_s", [P, G, S + V]), sb("m1_v", [P, G, 3, P])
        m1t = sb("m1_T", [P, 4, G * P])
        relu_t, lk = sb("relu", [S, G * P]), sb("leaky", [S, 2, G * P])
        vraw, tv, vst = sb("val_s", [P, G * P]), sb("tanh_s", [P, G * P]), sb("gated_s", [P, 2, G * P])
        tg, vvt = sb("tanh_gate", [3 * V, G * P]), sb("gated_v", [3 * V, 2, G * P])
        eq = sb("same_node", [P, 2, G, P])
        other = sb("other_node", [P, 2, G, P], BF)
        mt = sb("tile_max", [P, G, H])
        dd, ex = sb("differences", [P, G, 2, H]), sb("exps", [P, G, 2, H])
        prod = sb("products", [P, G, 15 * V])
        by_dir = sb("scalar_terms", [P, G, 3, S])
        along, plus, minus = (sb(f"vector_terms{k}", [P, G, 3, V]) for k in range(3))
        pp = sb("weighted_values", [P, G, NH])
        old, new = sb("old_state", [P, 2, G, SW]), sb("new_state", [P, 2, G, SW])
        told = sb("scaled_old", [P, G, NH])
        F = [ps(f"front{k}") for k in range(4)]
        B = [ps(f"back{k}") for k in range(4)]
        row_loaded, rbf_loaded, ends_gathered, state_gathered, scattered = (
            [sem(f"{n}{b}") for b in range(2)] for n in
            ("row_loaded", "rbf_loaded", "ends_gathered", "state_gathered", "scattered"))
        (pool_passed, staged, msg_done, w1_ready, m1_ready, T_ready, evac, al_ready, vv_ready, vraw_ready, vact,
         gate_ready, tg_done, eq_ready, other_ready, cd_done, bc_ready, a_ready, max_done, d_ready, ex_ready,
         pk_ready, pk_copied, pp_ready, s_done, sums_ready) = (sem(n) for n in (
             "pool_passed", "staged", "msg_done", "w1_ready", "m1_ready", "m1_transposed", "m1_T_ready",
             "alpha_ready", "vv_ready", "vraw_ready", "val_activated", "gate_ready", "gate_activated", "eq_ready",
             "other_ready", "values_ready", "scores_spread", "scores_ready", "max_done", "differences_ready",
             "exps_ready", "products_ready", "products_copied", "weighted_ready", "summed", "state_ready"))
        f1_chain, back_chain, m1_scaled = sem("f1_chain"), sem("back_chain"), sem("m1_scaled")
        block = ctx.enter_context(nc.Block())

        def heads(ap):
            return ap.rearrange("p g (h w) -> p g h w", h=H)

        @block.sync
        def _(sp):
            def load(b, i):
                m = 2 * i + b
                after(sp, eq_ready, m - 1)
                sp.dma_start(row[:, b, :], e.dst_rows[bass.ds(m, 1), :].broadcast_to([P, G * P]))\
                    .then_inc(row_loaded[b], 16)
                after(sp, w1_ready, m - 1)
                sp.dma_start(rbf[:, b, :], e.ins["features_16"][:, bass.ds(m * (G * P), G * P)])\
                    .then_inc(rbf_loaded[b], 16)

            pipeline(sp, macros, (2, load), depth=2)

        @block.gpsimd
        def _(pool):
            def passed():
                pool.sem_inc(pool_passed, 1)

            def gather(to, table, idx, sem):
                pool.indirect_dma_start(out=to, out_offset=None, in_=table[:, :],
                                        in_offset=bass.IndirectOffsetOnAxis(ap=idx, axis=0)).then_inc(sem, 16)

            def ends(b, i):
                m = 2 * i + b
                pool.wait_ge(staged, m + 1)
                passed()
                after(pool, msg_done, m - 1)
                passed()
                for g in range(G):
                    gather(ga[:, b, g, :], e.tab_src, sidx[:, b, g:g + 1], ends_gathered[b])
                    gather(gb[:, b, g, :], e.tab_dst, didx[:, b, g:g + 1], ends_gathered[b])

            def states(b, i):
                after(pool, scattered[b], 16 * G * i)
                passed()
                for g in range(G):
                    gather(old[:, b, g, :], e.acc["state"][G * b + g], didx[:, b, g:g + 1], state_gathered[b])

            def scatter(b, i):
                pool.wait_ge(sums_ready, 2 * i + b + 1)
                passed()
                for g in range(G):
                    pool.indirect_dma_start(
                        out=e.acc["state"][G * b + g][:, :],
                        out_offset=bass.IndirectOffsetOnAxis(ap=uidx[:, b, g:g + 1], axis=0),
                        in_=new[:, b, g, :], in_offset=None).then_inc(scattered[b], 16)

            def join(b, i):
                m = 2 * i + b
                pool.wait_ge(ends_gathered[b], 32 * G * (i + 1))
                after(pool, m1_ready, m)
                nc.gpsimd.tensor_tensor(msg[:, :, 0:D], ga[:, b], gb[:, b], ALU.add)
                nc.gpsimd.tensor_tensor(msg[:, :, D:], ga[:, b, :, S:S + 2 * V], gb[:, b, :, S:S + 2 * V], ALU.add)\
                    .then_inc(msg_done, 1)

            pipeline(pool, macros, (-1, scatter), (2, ends), (1, states), (2, join), depth=2)
            for b in range(2):
                pool.wait_ge(scattered[b], 16 * G * macros // 2)

        @block.vector
        def _(dve):
            def stage(b, i):
                m = 2 * i + b
                after(dve, ends_gathered[b], 32 * G * i)
                after(dve, state_gathered[b], 16 * G * i)
                after(dve, eq_ready, m - 1)
                cols = bass.ds(m * G, G)
                nc.vector.tensor_copy(sidx[:, b, :], e.src[:, cols])
                nc.vector.tensor_copy(didx[:, b, :], e.dst[:, cols])
                nc.vector.tensor_copy(idf[:, b, :], e.dst[:, cols]).then_inc(staged, 1)

            def merge(b, i):
                m = 2 * i + b
                dve.wait_ge(s_done, m + 1)
                dve.wait_ge(back_chain, 5 * m + 5)
                for k in range(2):
                    two = slice(2 * k, 2 * k + 2)
                    last = nc.vector.tensor_tensor(
                        new[:, b, two, 0:NH], told[:, two], B[2 + k][:, 0:2 * NH].rearrange("p (g w) -> p g w", g=2),
                        ALU.add)
                last.then_inc(sums_ready, 1)

            def maxima(hs):
                def f(b, i):
                    m = 2 * i + b
                    for h in hs:
                        dve.wait_ge(bc_ready, 4 * m + h + 1)
                        nc.vector.tensor_reduce(mt[:, :, h], B[h % 2][:, :].rearrange("p (g q) -> p g q", g=G),
                                                AX, ALU.max).then_inc(max_done, 1)
                return f

            def compare(b, i):
                m = 2 * i + b
                dve.wait_ge(row_loaded[b], 16 * (i + 1))
                dve.wait_ge(staged, m + 1)
                after(dve, s_done, m - 1)
                after(dve, other_ready, m - 1)
                cols = bass.ds(m * G, G)
                nc.vector.tensor_copy(y[:, b, :, 0:4], e.y[:, cols, :])
                nc.vector.tensor_copy(y[:, b, :, 4:6], e.y[:, cols, 1:3])
                for g in range(G):
                    last = nc.vector.tensor_scalar(eq[:, b, g, :], row[:, b, g * P:(g + 1) * P], idf[:, b, g:g + 1],
                                                   None, ALU.is_equal)
                last.then_inc(eq_ready, 1)

            def differences(b, i):
                m = 2 * i + b
                after(dve, scattered[b], 16 * G * i)
                nc.vector.tensor_copy(uidx[:, b, :], e.dst_u[:, bass.ds(m * G, G)])
                dve.wait_ge(max_done, 4 * m + 4)
                dve.wait_ge(state_gathered[b], 16 * G * (i + 1))
                nc.vector.tensor_tensor(new[:, b, :, NH:], old[:, b, :, NH:], mt[:], ALU.max)\
                    .then_inc(back_chain, 1)
                dve.wait_ge(a_ready, m + 1)
                dve.wait_ge(back_chain, 5 * m + 1)
                nc.vector.tensor_tensor(dd[:, :, 0], B[2][:, 0:G * H].rearrange("p (g h) -> p g h", g=G),
                                        new[:, b, :, NH:], ALU.subtract)
                nc.vector.tensor_tensor(dd[:, :, 1], old[:, b, :, NH:], new[:, b, :, NH:], ALU.subtract)\
                    .then_inc(d_ready, 1)

            def message(b, i):
                m = 2 * i + b
                dve.wait_ge(msg_done, m + 1)
                dve.wait_ge(eq_ready, m + 1)
                dve.wait_ge(w1_ready, m + 1)
                after(dve, T_ready, 4 * m)
                after(dve, m1_scaled, m)
                for k in range(2):
                    w = F[k][:, 0:2 * E1].rearrange("p (g w) -> p g w", g=2)
                    two = slice(2 * k, 2 * k + 2)
                    nc.vector.tensor_tensor(xs[:, two], w[:, :, 0:2 * S].rearrange("p g (k s) -> p g k s", k=2),
                                            spread(msg[:, two, 0:S], 2, 2), ALU.mult)
                    for to, r, n in ((vs, 0, 3), (vv0, 1, 3), (vv1, 2, 5)):
                        a = 2 * S + V * r
                        last = nc.vector.tensor_tensor(
                            to[:, two], msg[:, two, S:S + n * V].rearrange("p g (c u) -> p g c u", c=n),
                            spread(w[:, :, a:a + V], 2, n), ALU.mult)
                last.then_inc(f1_chain, 1)
                dve.wait_ge(f1_chain, 3 * m + 1)
                ys = directions(b)
                nc.vector.tensor_tensor(t1[:], vv0[:], ys(1, 3, V), ALU.mult)
                nc.vector.tensor_tensor(t2[:], vv1[:, :, 1:4], ys(3, 3, V), ALU.mult)
                nc.vector.tensor_tensor(t3[:], vv1[:, :, 2:5], ys(2, 3, V), ALU.mult).then_inc(f1_chain, 1)
                nc.vector.tensor_tensor(m1v[:, :, :, 0:S], spread(xs[:, :, 1], 2, 3), ys(1, 3, S), ALU.mult)
                dve.wait_ge(f1_chain, 3 * m + 2)
                nc.vector.tensor_tensor(dot[:], t1[:, :, 0], t1[:, :, 1], ALU.add).then_inc(f1_chain, 1)
                nc.vector.tensor_tensor(m1v[:, :, :, S + V:], t2[:], t3[:], ALU.subtract)
                dve.wait_ge(f1_chain, 3 * m + 3)
                nc.vector.tensor_tensor(m1s[:, :, S:], dot[:], t1[:, :, 2], ALU.add).then_inc(m1_ready, 1)

            def directions(b):
                def ys(a, n, width):
                    return spread(y[:, b, :, a:a + n], 3, width)
                return ys

            def combine(b, i):
                m = 2 * i + b
                ys = directions(b)
                dve.wait_ge(pk_copied, 4 * m + 4)
                after(dve, sums_ready, m)
                Dk = prod[:, :, 6 * V:12 * V].rearrange("p g (c s) -> p g c s", c=3)
                Fk = prod[:, :, 12 * V:15 * V].rearrange("p g (c u) -> p g c u", c=3)
                nc.vector.tensor_tensor(by_dir[:], Dk, ys(1, 3, S), ALU.mult)
                nc.vector.tensor_tensor(along[:], spread(prod[:, :, 0:V], 2, 3), ys(1, 3, V), ALU.mult)
                nc.vector.tensor_tensor(plus[:, :, 0:2], Fk[:, :, 1:3], ys(3, 2, V), ALU.mult)
                nc.vector.tensor_tensor(plus[:, :, 2:3], Fk[:, :, 0:1], ys(2, 1, V), ALU.mult)
                nc.vector.tensor_tensor(minus[:, :, 1:3], Fk[:, :, 0:2], ys(3, 2, V), ALU.mult)
                nc.vector.tensor_tensor(minus[:, :, 0:1], Fk[:, :, 2:3], ys(2, 1, V), ALU.mult).then_inc(back_chain, 1)
                dve.wait_ge(ex_ready, m + 1)
                nc.vector.tensor_tensor(heads(told[:]), heads(old[:, b, :, 0:NH]), spread(ex[:, :, 1], 3, HW + 1),
                                        ALU.mult)
                dve.wait_ge(back_chain, 5 * m + 2)
                A = prod[:, :, V:3 * V]
                E = prod[:, :, 3 * V:6 * V].rearrange("p g (c u) -> p g c u", c=3)
                nc.vector.tensor_tensor(by_dir[:, :, 0], by_dir[:, :, 0], by_dir[:, :, 1], ALU.add)
                nc.vector.tensor_tensor(by_dir[:, :, 2], by_dir[:, :, 2], A, ALU.add)
                nc.vector.tensor_tensor(along[:], along[:], E, ALU.add)
                nc.vector.tensor_tensor(plus[:], plus[:], minus[:], ALU.subtract).then_inc(back_chain, 1)
                dve.wait_ge(back_chain, 5 * m + 3)
                nc.vector.tensor_tensor(by_dir[:, :, 0], by_dir[:, :, 0], by_dir[:, :, 2], ALU.add)
                nc.vector.tensor_tensor(along[:], along[:], plus[:], ALU.add).then_inc(back_chain, 1)
                after(dve, s_done, m)
                pv = heads(pp[:])
                nc.vector.tensor_copy(pv[:, :, :, HW], ex[:, :, 0])
                dve.wait_ge(back_chain, 5 * m + 4)
                nc.vector.tensor_tensor(pv[:, :, :, 0:HA], by_dir[:, :, 0].rearrange("p g (h a) -> p g h a", h=H),
                                        spread(ex[:, :, 0], 3, HA), ALU.mult).then_inc(back_chain, 1)
                for c in range(3):
                    last = nc.vector.tensor_tensor(
                        pv[:, :, :, HA + HV * c:HA + HV * c + HV],
                        along[:, :, c].rearrange("p g (h a) -> p g h a", h=H), spread(ex[:, :, 0], 3, HV), ALU.mult)
                last.then_inc(pp_ready, 1)

            def activated(b, i):
                m = 2 * i + b
                dve.wait_ge(vact, 2 * m + 1)
                nc.vector.scalar_tensor_tensor(out=lk[:, b, :], in0=F[0][0:S, :], scalar=0.2, in1=relu_t[:, :],
                                               op0=ALU.mult, op1=ALU.add).then_inc(cd_done, 1)
                dve.wait_ge(vv_ready, m + 1)
                dve.wait_ge(tg_done, m + 1)
                nc.vector.scalar_tensor_tensor(out=vvt[:, b, :], in0=tg[:, :], scalar=1.0, in1=F[1][0:3 * V, :],
                                               op0=ALU.add, op1=ALU.mult).then_inc(cd_done, 1)

            pipeline(dve, macros, (-1, merge), (0, maxima((0, 1))), (2, stage), (1, compare),
                     (0, maxima((2, 3))), (0, differences), (1, message), (0, combine), (1, activated), depth=2)

        @block.scalar
        def _(act):
            def others(b, i):
                m = 2 * i + b
                act.wait_ge(eq_ready, m + 1)
                after(act, bc_ready, 4 * (m - 1))
                nc.scalar.activation(other[:, b], eq[:, b], ACT.Copy, bias=NO_SCORE, scale=-NO_SCORE)\
                    .then_inc(other_ready, 1)

            def exps(b, i):
                m = 2 * i + b
                act.wait_ge(d_ready, m + 1)
                after(act, pp_ready, m)
                nc.scalar.activation(ex[:], dd[:], ACT.Exp).then_inc(ex_ready, 1)

            def bring(tiles):
                def f(b, i):
                    m = 2 * i + b
                    for t in tiles:
                        act.wait_ge(pk_ready, 4 * m + t + 1)
                        bank = B[t % 2]
                        nc.scalar.copy(prod[:, t, 0:V], bank[:, 0:V])
                        nc.scalar.activation(prod[:, t, V:6 * V], bank[:, V:6 * V], ACT.Copy, scale=y[:, b, t, 0:1])
                        nc.scalar.copy(prod[:, t, 6 * V:], bank[:, 6 * V:15 * V]).then_inc(pk_copied, 1)
                return f

            def by_y0(b, i):
                m = 2 * i + b
                act.wait_ge(f1_chain, 3 * m + 1)
                after(act, T_ready, 4 * m)
                for t in range(G):
                    y0 = y[:, b, t, 0:1]
                    nc.scalar.activation(m1s[:, t, 0:S], xs[:, t, 0], ACT.Copy, scale=y0)
                    last = nc.scalar.activation(m1v[:, t, :, S:S + V], vs[:, t], ACT.Copy, scale=y0)
                last.then_inc(m1_scaled, 1)

            def values(b, i):
                m = 2 * i + b
                for q in range(4):
                    act.wait_ge(T_ready, 4 * m + q + 1)
                    after(act, vv_ready if q else al_ready, m)
                    n = P if q else S + V
                    nc.scalar.copy(m1t[0:n, q, :], F[2 + q % 2][0:n, :]).then_inc(evac, 1)
                act.wait_ge(al_ready, m + 1)
                after(act, gate_ready, m)
                nc.scalar.copy(vraw[S:P, :], F[0][S:P, :]).then_inc(vraw_ready, 1)
                after(act, cd_done, 2 * m)
                nc.scalar.activation(relu_t[:, :], F[0][0:S, :], ACT.Relu, scale=0.8).then_inc(vact, 1)
                nc.scalar.activation(tv[S:P, :], F[0][S:P, :], ACT.Tanh, scale=0.5).then_inc(vact, 1)
                act.wait_ge(vact, 2 * m + 2)
                nc.scalar.activation(vst[S:P, b, :], tv[S:P, :], ACT.Copy, bias=1.0)
                act.wait_ge(gate_ready, m + 1)
                nc.scalar.activation(tg[:, :], F[2][0:3 * V, :], ACT.Tanh, scale=0.5).then_inc(tg_done, 1)

            pipeline(act, macros, (1, others), (0, exps), (0, bring(range(0, 3))), (1, by_y0), (0, bring(range(3, G))),
                     (1, values), depth=2)

        @block.tensor
        def _(pe):
            def spread_scores(hs):
                def f(b, i):
                    m = 2 * i + b
                    if hs[0] == 0:
                        pe.wait_ge(cd_done, 2 * m + 1)
                        pe.wait_ge(other_ready, m + 1)
                    for h in hs:
                        if h < 2:
                            after(pe, pk_copied, 4 * m - 1 + h)
                        else:
                            pe.wait_ge(max_done, 4 * m + h - 1)
                        nc.tensor.matmul(B[h % 2][:, :], e.ad[:, h, :], lk[:, b, :], start=True, stop=False)
                        nc.tensor.matmul(B[h % 2][:, :], e.ident_bf[:, :], other[:, b].rearrange("p g q -> p (g q)"),
                                         start=False, stop=True).then_inc(bc_ready, 1)
                return f

            def radial(b, i):
                m = 2 * i + b
                pe.wait_ge(rbf_loaded[b], 16 * (i + 1))
                after(pe, cd_done, 2 * m)
                for g in range(G):
                    last = nc.tensor.matmul(F[g // 2][:, E1 * (g % 2):E1 * (g % 2) + E1],
                                            rbf[:, b, g * P:(g + 1) * P], e.wrbf[:, :], start=True, stop=True)
                last.then_inc(w1_ready, 1)

            def scores(b, i):
                m = 2 * i + b
                after(pe, sums_ready, m)
                for g in range(G):
                    last = nc.tensor.matmul(B[2][:, H * g:H * g + H], lk[:, b, g * P:(g + 1) * P], e.ad4[:, :],
                                            start=True, stop=True)
                last.then_inc(a_ready, 1)

            def products(b, i):
                m = 2 * i + b
                pe.wait_ge(cd_done, 2 * m + 2)
                for t in range(G):
                    tile = slice(t * P, (t + 1) * P)
                    if t < 2:
                        pe.wait_ge(max_done, 4 * m + 3 + t)
                    else:
                        pe.wait_ge(pk_copied, 4 * m + t - 1)
                    nc.tensor.matmul(B[t % 2][:, 0:3 * V], vst[S:P, b, tile], e.mvs[S:P, :], start=True, stop=True)
                    nc.tensor.matmul(B[t % 2][:, 3 * V:15 * V], vvt[:, b, tile], e.mvv[:, :], start=True, stop=True)\
                        .then_inc(pk_ready, 1)

            def values(b, i):
                m = 2 * i + b
                pe.wait_ge(m1_ready, m + 1)
                pe.wait_ge(m1_scaled, m + 1)
                after(pe, tg_done, m)
                for q in range(4):
                    if q >= 2:
                        pe.wait_ge(evac, 4 * m + q - 1)
                    for g in range(G):
                        src = m1v[:, g, q - 1, :] if q else m1s[:, g, :]
                        n = P if q else S + V
                        last = nc.tensor.transpose(F[2 + q % 2][0:n, g * P:(g + 1) * P], src, e.ident[:, :])
                    last.then_inc(T_ready, 1)
                pe.wait_ge(evac, 4 * m + 1)
                nc.tensor.matmul(F[0][:, :], e.walval[:, :], m1t[0:S + V, 0, :], start=True, stop=True)\
                    .then_inc(al_ready, 1)
                for c in range(3):
                    pe.wait_ge(evac, 4 * m + 2 + c)
                    last = nc.tensor.matmul(F[1][V * c:V * c + V, :], e.wvval[:, :], m1t[:, 1 + c, :],
                                            start=True, stop=True)
                last.then_inc(vv_ready, 1)

            def gates(b, i):
                m = 2 * i + b
                pe.wait_ge(vraw_ready, m + 1)
                nc.tensor.matmul(F[2][0:3 * V, :], e.wg[S:P, :], vraw[S:P, :], start=True, stop=True)\
                    .then_inc(gate_ready, 1)

            def sums(b, i):
                m = 2 * i + b
                pe.wait_ge(pp_ready, m + 1)
                for t in range(G):
                    last = nc.tensor.matmul(B[2 + t // 2][:, NH * (t % 2):NH * (t % 2) + NH], eq[:, b, t, :],
                                            pp[:, t, :], start=True, stop=True)
                last.then_inc(s_done, 1)

            pipeline(pe, macros, (0, spread_scores((0, 1))), (1, radial), (0, spread_scores((2, 3))), (0, scores),
                     (0, products), (1, values), (1, gates), (0, sums), depth=2)



def gnn_program(nc, ins, out):
    e = Env()
    e.ins = ins
    e.NT = ins["z_cols"].shape[1]
    e.T = ins["src_cols"].shape[1]
    e.NP = e.NT * P
    e.NR = e.NP + P
    e.src_rows, e.dst_rows = ins["src_rows"], ins["dst_rows"]
    macros = e.T // G

    def dram(name, shape):
        return nc.dram_tensor(name, shape, FP, kind="Internal").ap()

    base = [dram(f"stream{k}", [e.NP, D]) for k in range(4)]
    e.h3 = dram("h3", [e.NP, D])
    tab0, e.tab_src, e.tab_dst = (dram(n, [e.NP, D]) for n in ("table0", "table1_src", "table1_dst"))
    tab2, tab3 = dram("table2", [e.NP, 4 * D]), dram("table3", [e.NP, W3])
    e.acc = {name: [dram(f"{name}_{k}", [e.NR, w]) for k in range(n)]
             for name, w, n in (("acc0", 384, G), ("state", 168, 2 * G), ("acc2", D, G), ("acc3", D, G))}

    with ExitStack() as ctx:
        def sb(name, shape, dt=FP):
            return ctx.enter_context(nc.sbuf_tensor(name, shape, dt))

        def pair(name, cols):
            return sb(name + "_a", [P, cols]), sb(name + "_b", [V, cols])

        e.src, e.dst, e.dst_u = (sb(n, [P, e.T], I32) for n in ("src", "dst", "dst_unique"))
        e.y, e.z = sb("attr", [P, e.T, 4]), sb("z", [P, e.NT])
        e.z_of = lambda j, t: e.z[:, bass.ds(NB * j + t, 1)]
        e.ident, e.ident_bf, e.earlier = sb("identity", [P, P]), sb("identity_bf", [P, P], BF), sb("earlier", [P, P])
        e.spare, e.spare_i = sb("spare_row", [P, 1]), sb("spare_row_i", [P, 1], I32)
        e.w0, e.w1, e.w2, e.w3 = pair("w0", 2 * D), pair("w1", 2 * D), pair("w2", 4 * D), pair("w3", W3)
        e.w2o, e.w3l = pair("w2_out", D), pair("w3_lin", D)
        e.w1o = (sb("w1_out_a", [80, D]), sb("w1_out_b", [80, D]))
        e.w0s, e.w0v = sb("w0_out_s", [S + V, S]), sb("w0_out_v", [S + V, V])
        e.wfc1, e.wfc2, e.wrbf = sb("w_fc1", [12, 100]), sb("w_fc2", [100, 192]), sb("w_rbf", [16, 224])
        e.walval, e.wvval, e.wg = sb("w_alpha_val", [S + V, 2 * S]), sb("w_val_v", [P, V]), sb("w_gate", [P, 3 * V])
        e.adcol, e.ad4, e.ad = sb("alpha_dot", [S, 1]), sb("alpha_dot_heads", [S, H]), sb("alpha_dot_spread", [S, H, P])
        e.gamma_s, e.beta_s, e.gamma_v = sb("gamma_s", [P, S]), sb("beta_s", [P, S]), sb("gamma_v", [P, 3 * V])
        e.mvs, e.mvv = sb("value_s", [P, 3 * V]), sb("value_v", [3 * V, 12 * V])
        e.w2s, e.vl, e.w2v = sb("w2_s", [P, 2]), sb("vlin_v", [3 * V, 2 * S]), sb("w2_v", [3 * V, 3])

        e.edge_sem = edge_semaphores(nc, ctx)
        with ExitStack() as early:
            e.zeros = early.enter_context(nc.sbuf_tensor("zeros", [P, 10 * 384], FP))
            e.empty = early.enter_context(nc.sbuf_tensor("empty_state", [P, 10, H * (HW + 1) + H], FP))
            weight_phase(nc, e)
            node_phase(nc, e, "n0", "x", "radial", ins["x_rows"], base[0], None, e.w0, [tab0])
            edge_phase(nc, e, "e0", "radial", 0, macros, e.src, e.dst_rows, e.dst, e.dst_u, tab0, e.acc["acc0"])
        node_phase(nc, e, "n1", "radial", "attention", base[0], base[1], None, e.w1, [e.tab_src, e.tab_dst])
        attention_phase(nc, e, macros)
        node_phase(nc, e, "n2", "attention", "linear", base[1], base[2], e.w1o, e.w2, [tab2])
        edge_phase(nc, e, "e2", "linear", 1, macros, e.src, e.dst_rows, e.dst, e.dst_u, tab2, e.acc["acc2"])
        node_phase(nc, e, "n3", "linear", "bilinear_next", base[2], base[3], e.w2o, e.w3, [tab3])
        edge_phase(nc, e, "e3", "messages", 2, macros, e.dst, e.src_rows, e.src, None, tab3, e.acc["acc3"])
        e.wuss, e.wuvv = sb("wu_ss", [P, 32, S]), sb("wu_vv", [P, 8, S])
        e.wusv, e.wuvs = sb("wu_sv", [S, V * V]), sb("wu_vs", [S, V * V])
        bilinear_weight_phase(nc, e)
        node_phase(nc, e, "n4", "bilinear", None, base[3], out, e.w3l, None, [])


_WEIGHTS = [
    "L0_gnn_W_sc0", "L0_gnn_W_sc1", "L0_gnn_W_l1_0", "L0_gnn_W_l1_1", "L0_gnn_W_fc1", "L0_gnn_W_fc2",
    "L0_gnn_W_l2_0", "L0_gnn_W_l2_1", "L1_gnn_gamma_s", "L1_gnn_beta_s", "L1_gnn_gamma_v", "L1_gnn_Ws_src",
    "L1_gnn_Wv_src", "L1_gnn_Ws_dst", "L1_gnn_Wv_dst", "L1_gnn_W_rbf", "L1_gnn_W_alpha", "L1_gnn_alpha_dot",
    "L1_gnn_Ws_val", "L1_gnn_Wv_val", "L1_gnn_Wg", "L1_gnn_w2_ss", "L1_gnn_w2_sv", "L1_gnn_w2_vs",
    "L1_gnn_w2_vv0", "L1_gnn_w2_vv1", "L1_gnn_Ws_vlin", "L1_gnn_Wv_vlin", "L1_gnn_Wps", "L1_gnn_Wpv",
    "L2_gnn_W1", "L2_gnn_W2", "L2_gnn_W3", "L2_gnn_W4", "L2_gnn_W5", "L2_gnn_Ws", "L2_gnn_Wv", "L3_gnn_Wm_ss",
    "L3_gnn_Wm_vv", "L3_gnn_Wm_sv", "L3_gnn_Wm_vs", "L3_gnn_Lm_s", "L3_gnn_Lm_v", "L3_gnn_Wu_ss",
    "L3_gnn_Wu_vv", "L3_gnn_Wu_sv", "L3_gnn_Wu_vs", "L3_gnn_Lu_s", "L3_gnn_Lu_v"]


def _layout(inputs):
    import numpy as np

    a = {k: np.asarray(v) for k, v in inputs.items()}
    n, n_edges = a["x"].shape[0], a["src"].shape[0]
    nodes = -(-(n + 1) // (NB * P)) * NB * P
    edges = -(-n_edges // (U * G * P)) * U * G * P
    tiles = edges // P
    arrays = {k: np.ascontiguousarray(a[k]) for k in _WEIGHTS}
    x = np.concatenate([a["x"][:, :S], a["x"][:, S:].reshape(n, V, 3).transpose(0, 2, 1).reshape(n, 3 * V)], axis=1)
    arrays["x_rows"] = np.pad(x, ((0, nodes - n), (0, 0)))
    z = np.pad(a["node_vec1"][:, 0], (0, nodes - n))
    arrays["z_cols"] = np.ascontiguousarray(z.reshape(nodes // P, P).T)
    for name in ("src", "dst"):
        ids = np.pad(a[name], (0, edges - n_edges), constant_values=n)
        arrays[name + "_cols"] = np.ascontiguousarray(ids.reshape(tiles, P).T)
        arrays[name + "_rows"] = ids.reshape(tiles // G, G * P)
    attr = np.pad(a["edge_attr_4"], ((0, edges - n_edges), (0, 0)))
    arrays["attr_cols"] = np.ascontiguousarray(attr.reshape(tiles, P, 4).transpose(1, 0, 2))
    for k in (12, 16):
        f = np.pad(a[f"edge_attr_{k}"], ((0, edges - n_edges), (0, 0)))
        arrays[f"features_{k}"] = np.ascontiguousarray(f.T)
    return n, nodes, arrays


def kernel(**inputs):
    import numpy as np
    import concourse.bacc as bacc
    from concourse.bass_utils import run_bass_kernel_spmd

    n, nodes, arrays = _layout(inputs)
    nc = bacc.Bacc("TRN2", target_bir_lowering=False, num_devices=1)
    aps = {name: nc.dram_tensor(name, list(a.shape), mybir.dt.from_np(a.dtype), kind="ExternalInput").ap()
           for name, a in arrays.items()}
    out = nc.dram_tensor("out_rows", [nodes, D], FP, kind="ExternalOutput").ap()
    gnn_program(nc, aps, out)
    r = run_bass_kernel_spmd(nc, [arrays], core_ids=[0]).results[0]["out_rows"]
    r = np.asarray(r)[:n]
    return np.concatenate([r[:, :S], r[:, S:].reshape(n, 3, V).transpose(0, 2, 1).reshape(n, 3 * V)], axis=1)
```
